# Optimizing a Trainium2 kernel written in Bass

```python
import numpy as np
import jax
import jax.numpy as jnp

def _softmax(x, axis=-1):
    return jax.nn.softmax(x, axis=axis)

def _gelu(x):
    return jax.nn.gelu(x, approximate=True)

def _silu(x):
    return jax.nn.silu(x)

def _sigmoid(x):
    return jax.nn.sigmoid(x)

def _layernorm(x, axis=-1, eps=1e-05):
    m = jnp.mean(x, axis=axis, keepdims=True)
    v = jnp.var(x, axis=axis, keepdims=True)
    return (x - m) / jnp.sqrt(v + eps)

def _scatter_add(tgt, idx, src, axis=0):
    return tgt.at[idx].add(src)

def _segment_sum(src, seg, n):
    return jax.ops.segment_sum(src, seg, n)
kernel_name = 'mk_flamingo_gated_d4_seqx_r8_8470cf'

def setup_inputs(seed: int=0):
    np.random.seed(seed)
    _w = jnp.asarray

    def _rec_inputs():
        import jax
        import jax.numpy as jnp
        _rk = jax.random.key(seed)
        x = 7.22e-05 + 1 * jax.random.normal(jax.random.fold_in(_rk, 1), (8, 256, 128), jnp.float32)
        _lenS = 256 - jax.random.randint(jax.random.fold_in(_rk, 7), (8,), 0, max(1, 256 // 4) + 1, jnp.int32)
        _lenS2 = 256 - jax.random.randint(jax.random.fold_in(_rk, 8), (8,), 0, max(1, 256 // 4) + 1, jnp.int32)
        _ctx_1024P = jax.random.normal(jax.random.fold_in(_rk, 11), (8, 16, 128), jnp.float32)
        _ctx_1024c = jax.random.dirichlet(jax.random.fold_in(_rk, 511), 0.3 * jnp.ones((16,), jnp.float32), (8, 256))
        _ctx_1024t = jnp.einsum('bsk,bkd->bsd', _ctx_1024c, _ctx_1024P)
        _ctx_1024t = _ctx_1024t * jax.lax.rsqrt(jnp.mean(jnp.square(_ctx_1024t)) + 1e-12) * 0.953939
        ctx_1024 = 4.13588e-05 + 0.999923 * (_ctx_1024t + 0.3 * jax.random.normal(jax.random.fold_in(_rk, 611), (8, 256, 128), jnp.float32))
        _g = jax.random.normal(jax.random.fold_in(_rk, 9001), (2, 4), jnp.float32)
        _g = jnp.sign(_g) * jnp.maximum(jnp.abs(_g), 1.0) + (_g == 0) * 1.0
        g_xattn = _g[0]
        g_ffn = _g[1]
        return (x, ctx_1024, g_xattn, g_ffn)
    x, ctx_1024, g_xattn, g_ffn = _rec_inputs()

    def _L0_xattn_setup():
        import jax, jax.numpy as jnp
        import numpy as np
        H = 16
        D_MODEL = 128
        D_K = D_MODEL // H
        key = jax.random.key(seed)
        ks = jax.random.split(key, 12)
        B, S = (4, 256)
        scale = 1.0 / np.sqrt(D_MODEL)
        inp = {'query': jax.random.normal(ks[0], (B, S, D_MODEL), dtype=jnp.float32), 'key': jax.random.normal(ks[1], (B, S, D_MODEL), dtype=jnp.float32), 'value': jax.random.normal(ks[2], (B, S, D_MODEL), dtype=jnp.float32), 'Wq': jax.random.normal(ks[3], (D_MODEL, D_MODEL), dtype=jnp.float32) * scale, 'bq': jnp.zeros((D_MODEL,), dtype=jnp.float32), 'Wk': jax.random.normal(ks[4], (D_MODEL, D_MODEL), dtype=jnp.float32) * scale, 'bk': jnp.zeros((D_MODEL,), dtype=jnp.float32), 'Wv': jax.random.normal(ks[5], (D_MODEL, D_MODEL), dtype=jnp.float32) * scale, 'bv': jnp.zeros((D_MODEL,), dtype=jnp.float32), 'Wo': jax.random.normal(ks[6], (D_MODEL, D_MODEL), dtype=jnp.float32) * scale, 'bo': jnp.zeros((D_MODEL,), dtype=jnp.float32)}
        return inp
    _L0_xattn_all = _L0_xattn_setup()
    _L0_xattn_in = {k: v for k, v in _L0_xattn_all.items() if k in ('Wq', 'bq', 'Wk', 'bk', 'Wv', 'bv', 'Wo', 'bo')}
    del _L0_xattn_all

    def _L0_ffn_setup():
        import jax, jax.numpy as jnp
        import numpy as np
        CAPACITY_RATIO = 0.75
        key = jax.random.key(seed)
        k1, k2, k3 = jax.random.split(key, 3)
        B, L, D = (4, 1024, 128)
        x = jax.random.normal(k1, (B, L, D), dtype=jnp.float32)
        w_router = jax.random.normal(k2, (D,), dtype=jnp.float32) * 0.02
        w_block = jax.random.normal(k3, (D, D), dtype=jnp.float32) * 0.02
        return {'x': x, 'w_router': w_router, 'w_block': w_block}
    _L0_ffn_all = _L0_ffn_setup()
    _L0_ffn_in = {k: v for k, v in _L0_ffn_all.items() if k in ('w_router', 'w_block')}
    del _L0_ffn_all

    def _L1_xattn_setup():
        import jax, jax.numpy as jnp
        import numpy as np
        EMBED = 128
        HEADS = 16
        HEAD_DIM = EMBED // HEADS
        key = jax.random.key(seed)
        ks = jax.random.split(key, 8)
        B, S = (2, 256)
        value = jax.random.normal(ks[0], (B, S, EMBED), dtype=jnp.float32)
        key_t = jax.random.normal(ks[1], (B, S, EMBED), dtype=jnp.float32)
        query = jax.random.normal(ks[2], (B, S, EMBED), dtype=jnp.float32)
        scale = 1.0 / np.sqrt(EMBED)
        Wv = jax.random.normal(ks[3], (EMBED, EMBED), dtype=jnp.float32) * scale
        Wk = jax.random.normal(ks[4], (EMBED, EMBED), dtype=jnp.float32) * scale
        Wq = jax.random.normal(ks[5], (EMBED, EMBED), dtype=jnp.float32) * scale
        Wo = jax.random.normal(ks[6], (EMBED, EMBED), dtype=jnp.float32) * scale
        bo = jax.random.normal(ks[7], (EMBED,), dtype=jnp.float32) * 0.01
        return {'value': value, 'key': key_t, 'query': query, 'Wv': Wv, 'Wk': Wk, 'Wq': Wq, 'Wo': Wo, 'bo': bo}
    _L1_xattn_all = _L1_xattn_setup()
    _L1_xattn_in = {k: v for k, v in _L1_xattn_all.items() if k in ('Wv', 'Wk', 'Wq', 'Wo', 'bo')}
    del _L1_xattn_all

    def _L1_ffn_setup():
        import jax, jax.numpy as jnp
        import numpy as np
        E = 8
        TOPK = 2
        H = 128
        I = 128
        ISH = I * 2
        B, S = (2, 128)
        key = jax.random.key(seed)
        ks = jax.random.split(key, 7)
        s = 0.02
        return {'hidden_states': jax.random.normal(ks[0], (B, S, H), jnp.float32), 'w_router': jax.random.normal(ks[1], (H, E), jnp.float32) * s, 'fc1_w': jax.random.normal(ks[2], (E, H, 2 * I), jnp.float32) * s, 'fc2_w': jax.random.normal(ks[3], (E, I, H), jnp.float32) * s, 'gate_w': jax.random.normal(ks[4], (H, ISH), jnp.float32) * s, 'up_w': jax.random.normal(ks[5], (H, ISH), jnp.float32) * s, 'down_w': jax.random.normal(ks[6], (ISH, H), jnp.float32) * s}
    _L1_ffn_all = _L1_ffn_setup()
    _L1_ffn_in = {k: v for k, v in _L1_ffn_all.items() if k in ('w_router', 'fc1_w', 'fc2_w', 'gate_w', 'up_w', 'down_w')}
    del _L1_ffn_all

    def _L2_xattn_setup():
        import jax, jax.numpy as jnp
        import numpy as np
        D_MODEL = 128
        NUM_HEADS = 16
        HEAD_DIM = D_MODEL // NUM_HEADS
        key = jax.random.key(seed)
        ks = jax.random.split(key, 10)
        B, SQ, SKV = (2, 256, 256)
        s = 1.0 / np.sqrt(D_MODEL)
        inp = {'query': jax.random.normal(ks[0], (B, SQ, D_MODEL), jnp.float32), 'key_value': jax.random.normal(ks[1], (B, SKV, D_MODEL), jnp.float32), 'Wq': jax.random.normal(ks[2], (D_MODEL, D_MODEL), jnp.float32) * s, 'bq': jnp.zeros((D_MODEL,), jnp.float32), 'Wk': jax.random.normal(ks[3], (D_MODEL, D_MODEL), jnp.float32) * s, 'bk': jnp.zeros((D_MODEL,), jnp.float32), 'Wv': jax.random.normal(ks[4], (D_MODEL, D_MODEL), jnp.float32) * s, 'bv': jnp.zeros((D_MODEL,), jnp.float32), 'Wo': jax.random.normal(ks[5], (D_MODEL, D_MODEL), jnp.float32) * s, 'bo': jnp.zeros((D_MODEL,), jnp.float32)}
        return inp
    _L2_xattn_all = _L2_xattn_setup()
    _L2_xattn_in = {k: v for k, v in _L2_xattn_all.items() if k in ('Wq', 'bq', 'Wk', 'bk', 'Wv', 'bv', 'Wo', 'bo')}
    del _L2_xattn_all

    def _L2_ffn_setup():
        import jax, jax.numpy as jnp
        import numpy as np
        B, S, DIM = (4, 256, 128)
        E, K, HID = (8, 2, 512)
        key = jax.random.key(seed)
        ks = jax.random.split(key, 8)
        init = lambda k, sh: jax.random.normal(k, sh, jnp.float32) * 0.02
        return {'x': jax.random.normal(ks[0], (B, S, DIM), jnp.float32), 'gate_w': init(ks[1], (DIM, E)), 'gate_b': jnp.zeros((E,), jnp.float32), 'w1': init(ks[2], (E, DIM, HID)), 'b1': jnp.zeros((E, HID), jnp.float32), 'w2': init(ks[3], (E, HID, DIM)), 'b2': jnp.zeros((E, DIM), jnp.float32), 'ws1': init(ks[4], (DIM, HID)), 'bs1': jnp.zeros((HID,), jnp.float32), 'ws2': init(ks[5], (HID, DIM)), 'bs2': jnp.zeros((DIM,), jnp.float32)}
    _L2_ffn_all = _L2_ffn_setup()
    _L2_ffn_in = {k: v for k, v in _L2_ffn_all.items() if k in ('gate_w', 'gate_b', 'w1', 'b1', 'w2', 'b2', 'ws1', 'bs1', 'ws2', 'bs2')}
    del _L2_ffn_all

    def _L3_xattn_setup():
        import jax, jax.numpy as jnp
        import numpy as np
        import math
        D_MODEL = 128
        N_HEADS = 16
        HEAD_DIM = D_MODEL // N_HEADS
        TOP_FACTOR = 5
        B, L = (2, 256)
        key = jax.random.key(seed)
        ks = jax.random.split(key, 12)
        f = lambda k, shp: jax.random.normal(k, shp, dtype=jnp.float32)
        w = lambda k: f(k, (D_MODEL, D_MODEL)) * 0.02
        return {'queries': f(ks[0], (B, L, D_MODEL)), 'keys': f(ks[1], (B, L, D_MODEL)), 'values': f(ks[2], (B, L, D_MODEL)), 'Wq': w(ks[3]), 'bq': jnp.zeros((D_MODEL,), jnp.float32), 'Wk': w(ks[4]), 'bk': jnp.zeros((D_MODEL,), jnp.float32), 'Wv': w(ks[5]), 'bv': jnp.zeros((D_MODEL,), jnp.float32), 'Wo': w(ks[6]), 'bo': jnp.zeros((D_MODEL,), jnp.float32)}
    _L3_xattn_all = _L3_xattn_setup()
    _L3_xattn_in = {k: v for k, v in _L3_xattn_all.items() if k in ('Wq', 'bq', 'Wk', 'bk', 'Wv', 'bv', 'Wo', 'bo')}
    del _L3_xattn_all

    def _L3_ffn_setup():
        import jax, jax.numpy as jnp
        import numpy as np
        BLOCK_SIZE = 32
        FP6_E2M3_MAX = 7.5

        def _build_fp6_e2m3_grid():
            vals = set()
            for bits in range(64):
                s = bits >> 5 & 1
                e = bits >> 3 & 3
                m = bits & 7
                v = m / 8.0 if e == 0 else (1.0 + m / 8.0) * 2.0 ** (e - 1)
                vals.add(-v if s else v)
            return np.array(sorted(vals), dtype=np.float32)
        _GRID = jnp.asarray(_build_fp6_e2m3_grid())

        def _nearest_on_grid(x, grid):
            idx = jnp.clip(jnp.searchsorted(grid, x), 0, grid.shape[0] - 1)
            idx_lo = jnp.maximum(idx - 1, 0)
            v_hi = grid[idx]
            v_lo = grid[idx_lo]
            return jnp.where(jnp.abs(x - v_lo) <= jnp.abs(x - v_hi), v_lo, v_hi)

        def _mx_quantize(t, eps=1e-30):
            rows, K = t.shape
            blocks = t.reshape(rows, K // BLOCK_SIZE, BLOCK_SIZE)
            scales = jnp.maximum(jnp.max(jnp.abs(blocks), axis=-1) / FP6_E2M3_MAX, eps)
            q = _nearest_on_grid(blocks / scales[..., None], _GRID)
            return (q, scales)
        key = jax.random.key(seed)
        k1, k2, k3 = jax.random.split(key, 3)
        x = jax.random.normal(k1, (8, 1024, 128), dtype=jnp.float32)
        weight = jax.random.normal(k2, (128, 128), dtype=jnp.float32) * 0.02
        bias = jax.random.normal(k3, (128,), dtype=jnp.float32) * 0.02
        return {'x': x, 'weight': weight, 'bias': bias}
    _L3_ffn_all = _L3_ffn_setup()
    _L3_ffn_in = {k: v for k, v in _L3_ffn_all.items() if k in ('weight', 'bias')}
    del _L3_ffn_all
    return {'x': x, 'ctx_1024': ctx_1024, 'g_xattn': g_xattn, 'g_ffn': g_ffn, 'L0_xattn_Wq': _L0_xattn_in['Wq'], 'L0_xattn_bq': _L0_xattn_in['bq'], 'L0_xattn_Wk': _L0_xattn_in['Wk'], 'L0_xattn_bk': _L0_xattn_in['bk'], 'L0_xattn_Wv': _L0_xattn_in['Wv'], 'L0_xattn_bv': _L0_xattn_in['bv'], 'L0_xattn_Wo': _L0_xattn_in['Wo'], 'L0_xattn_bo': _L0_xattn_in['bo'], 'L0_ffn_w_router': _L0_ffn_in['w_router'], 'L0_ffn_w_block': _L0_ffn_in['w_block'], 'L1_xattn_Wv': _L1_xattn_in['Wv'], 'L1_xattn_Wk': _L1_xattn_in['Wk'], 'L1_xattn_Wq': _L1_xattn_in['Wq'], 'L1_xattn_Wo': _L1_xattn_in['Wo'], 'L1_xattn_bo': _L1_xattn_in['bo'], 'L1_ffn_w_router': _L1_ffn_in['w_router'], 'L1_ffn_fc1_w': _L1_ffn_in['fc1_w'], 'L1_ffn_fc2_w': _L1_ffn_in['fc2_w'], 'L1_ffn_gate_w': _L1_ffn_in['gate_w'], 'L1_ffn_up_w': _L1_ffn_in['up_w'], 'L1_ffn_down_w': _L1_ffn_in['down_w'], 'L2_xattn_Wq': _L2_xattn_in['Wq'], 'L2_xattn_bq': _L2_xattn_in['bq'], 'L2_xattn_Wk': _L2_xattn_in['Wk'], 'L2_xattn_bk': _L2_xattn_in['bk'], 'L2_xattn_Wv': _L2_xattn_in['Wv'], 'L2_xattn_bv': _L2_xattn_in['bv'], 'L2_xattn_Wo': _L2_xattn_in['Wo'], 'L2_xattn_bo': _L2_xattn_in['bo'], 'L2_ffn_gate_w': _L2_ffn_in['gate_w'], 'L2_ffn_gate_b': _L2_ffn_in['gate_b'], 'L2_ffn_w1': _L2_ffn_in['w1'], 'L2_ffn_b1': _L2_ffn_in['b1'], 'L2_ffn_w2': _L2_ffn_in['w2'], 'L2_ffn_b2': _L2_ffn_in['b2'], 'L2_ffn_ws1': _L2_ffn_in['ws1'], 'L2_ffn_bs1': _L2_ffn_in['bs1'], 'L2_ffn_ws2': _L2_ffn_in['ws2'], 'L2_ffn_bs2': _L2_ffn_in['bs2'], 'L3_xattn_Wq': _L3_xattn_in['Wq'], 'L3_xattn_bq': _L3_xattn_in['bq'], 'L3_xattn_Wk': _L3_xattn_in['Wk'], 'L3_xattn_bk': _L3_xattn_in['bk'], 'L3_xattn_Wv': _L3_xattn_in['Wv'], 'L3_xattn_bv': _L3_xattn_in['bv'], 'L3_xattn_Wo': _L3_xattn_in['Wo'], 'L3_xattn_bo': _L3_xattn_in['bo'], 'L3_ffn_weight': _L3_ffn_in['weight'], 'L3_ffn_bias': _L3_ffn_in['bias']}

def reference(x, ctx_1024, g_xattn, g_ffn, L0_xattn_Wq, L0_xattn_bq, L0_xattn_Wk, L0_xattn_bk, L0_xattn_Wv, L0_xattn_bv, L0_xattn_Wo, L0_xattn_bo, L0_ffn_w_router, L0_ffn_w_block, L1_xattn_Wv, L1_xattn_Wk, L1_xattn_Wq, L1_xattn_Wo, L1_xattn_bo, L1_ffn_w_router, L1_ffn_fc1_w, L1_ffn_fc2_w, L1_ffn_gate_w, L1_ffn_up_w, L1_ffn_down_w, L2_xattn_Wq, L2_xattn_bq, L2_xattn_Wk, L2_xattn_bk, L2_xattn_Wv, L2_xattn_bv, L2_xattn_Wo, L2_xattn_bo, L2_ffn_gate_w, L2_ffn_gate_b, L2_ffn_w1, L2_ffn_b1, L2_ffn_w2, L2_ffn_b2, L2_ffn_ws1, L2_ffn_bs1, L2_ffn_ws2, L2_ffn_bs2, L3_xattn_Wq, L3_xattn_bq, L3_xattn_Wk, L3_xattn_bk, L3_xattn_Wv, L3_xattn_bv, L3_xattn_Wo, L3_xattn_bo, L3_ffn_weight, L3_ffn_bias):
    import jax
    import jax.numpy as jnp

    def _L0_xattn_ref(query, key, value, Wq, bq, Wk, bk, Wv, bv, Wo, bo):
        import jax, jax.numpy as jnp
        import numpy as np
        H = 16
        D_MODEL = 128
        D_K = D_MODEL // H
        B, S, _ = query.shape

        def proj(x, W, b):
            y = x @ W.T + b
            return y.reshape(B, S, H, D_K).transpose(0, 2, 1, 3)
        q = proj(query, Wq, bq)
        k = proj(key, Wk, bk)
        v = proj(value, Wv, bv)
        scores = jnp.einsum('bhqd,bhkd->bhqk', q, k) / jnp.sqrt(jnp.float32(D_K))
        attn = jax.nn.softmax(scores, axis=-1)
        x = jnp.einsum('bhqk,bhkd->bhqd', attn, v)
        x = x.transpose(0, 2, 1, 3).reshape(B, S, H * D_K)
        return x @ Wo.T + bo

    def _L0_ffn_ref(x, w_router, w_block):
        import jax, jax.numpy as jnp
        import numpy as np
        CAPACITY_RATIO = 0.75
        B, L, D = x.shape
        k = max(1, int(L * CAPACITY_RATIO))
        scores = jnp.einsum('bld,d->bl', x, w_router)
        _, top_idx = jax.lax.top_k(scores, k)
        selected = jnp.take_along_axis(x, top_idx[:, :, None], axis=1)
        processed = jax.nn.gelu(jnp.einsum('bkd,de->bke', selected, w_block))
        batch_idx = jnp.arange(B)[:, None]
        out = x.at[batch_idx, top_idx].set(processed)
        return out

    def _L1_xattn_ref(value, key, query, Wv, Wk, Wq, Wo, bo):
        import jax, jax.numpy as jnp
        import numpy as np
        EMBED = 128
        HEADS = 16
        HEAD_DIM = EMBED // HEADS
        B = query.shape[0]

        def split(x, W):
            y = jnp.einsum('bse,fe->bsf', x, W)
            return y.reshape(B, -1, HEADS, HEAD_DIM).transpose(0, 2, 1, 3)
        v = split(value, Wv)
        k = split(key, Wk)
        q = split(query, Wq)
        scores = jnp.einsum('bhqd,bhkd->bhqk', q, k) / jnp.sqrt(jnp.float32(HEAD_DIM))
        attn = jax.nn.softmax(scores, axis=-1)
        out = jnp.einsum('bhqk,bhkd->bhqd', attn, v)
        out = out.transpose(0, 2, 1, 3).reshape(B, -1, EMBED)
        return jnp.einsum('bse,fe->bsf', out, Wo) + bo

    def _L1_ffn_ref(hidden_states, w_router, fc1_w, fc2_w, gate_w, up_w, down_w):
        import jax, jax.numpy as jnp
        import numpy as np
        E = 8
        TOPK = 2
        H = 128
        I = 128
        ISH = I * 2
        B, S = (2, 128)
        orig_shape = hidden_states.shape
        x = hidden_states.reshape(-1, orig_shape[-1])
        logits = x @ w_router
        top_logits, top_idx = jax.lax.top_k(logits, TOPK)
        scores = jax.nn.softmax(top_logits, axis=-1)
        flat_idx = top_idx.reshape(-1)
        sorted_idx = jnp.argsort(flat_idx)
        permuted = x[sorted_idx // TOPK]
        eid = flat_idx[sorted_idx]
        out_perm = jnp.zeros((permuted.shape[0], orig_shape[-1]), x.dtype)
        for e in range(E):
            m = (eid == e).astype(x.dtype)[:, None]
            h1 = permuted * m @ fc1_w[e]
            proj, gate = jnp.split(h1, 2, axis=-1)
            out_perm = out_perm + jax.nn.silu(proj) * gate @ fc2_w[e]
        unperm = jnp.zeros_like(out_perm).at[sorted_idx].set(out_perm)
        moe_out = (unperm.reshape(-1, TOPK, orig_shape[-1]) * scores[:, :, None]).sum(axis=1)
        moe_out = moe_out.reshape(orig_shape)
        shared = jax.nn.silu(hidden_states @ gate_w) * (hidden_states @ up_w) @ down_w
        return moe_out + shared

    def _L2_xattn_ref(query, key_value, Wq, bq, Wk, bk, Wv, bv, Wo, bo):
        import jax, jax.numpy as jnp
        import numpy as np
        D_MODEL = 128
        NUM_HEADS = 16
        HEAD_DIM = D_MODEL // NUM_HEADS
        B, SQ, _ = query.shape
        SKV = key_value.shape[1]
        Q = query @ Wq.T + bq
        K = key_value @ Wk.T + bk
        V = key_value @ Wv.T + bv
        Q = Q.reshape(B, SQ, NUM_HEADS, HEAD_DIM).transpose(0, 2, 1, 3)
        K = K.reshape(B, SKV, NUM_HEADS, HEAD_DIM).transpose(0, 2, 1, 3)
        V = V.reshape(B, SKV, NUM_HEADS, HEAD_DIM).transpose(0, 2, 1, 3)
        scores = jnp.einsum('bhqd,bhkd->bhqk', Q, K) / np.sqrt(HEAD_DIM)
        causal = jnp.tril(jnp.ones((SQ, SKV), bool))
        scores = jnp.where(causal[None, None], scores, -jnp.inf)
        attn = jax.nn.softmax(scores, axis=-1)
        out = jnp.einsum('bhqk,bhkd->bhqd', attn, V)
        out = out.transpose(0, 2, 1, 3).reshape(B, SQ, D_MODEL)
        return out @ Wo.T + bo

    def _L2_ffn_ref(x, gate_w, gate_b, w1, b1, w2, b2, ws1, bs1, ws2, bs2):
        import jax, jax.numpy as jnp
        import numpy as np
        B, S, DIM = (4, 256, 128)
        E, K, HID = (8, 2, 512)
        orig_shape = x.shape
        xf = x.reshape(-1, DIM)
        logits = xf @ gate_w + gate_b
        top_w, top_i = jax.lax.top_k(logits, K)
        gw = jax.nn.softmax(top_w, axis=-1).astype(xf.dtype)
        combine = (gw[:, :, None] * jax.nn.one_hot(top_i, E, dtype=xf.dtype)).sum(axis=1)
        out = jnp.zeros_like(xf)
        for e in range(E):
            h = jax.nn.gelu(xf @ w1[e] + b1[e], approximate=False)
            out = out + combine[:, e:e + 1] * (h @ w2[e] + b2[e])
        shared = jax.nn.gelu(xf @ ws1 + bs1, approximate=False) @ ws2 + bs2
        return (out + shared).reshape(orig_shape)

    def _L3_xattn_ref(queries, keys, values, Wq, bq, Wk, bk, Wv, bv, Wo, bo):
        import jax, jax.numpy as jnp
        import numpy as np
        import math
        D_MODEL = 128
        N_HEADS = 16
        HEAD_DIM = D_MODEL // N_HEADS
        TOP_FACTOR = 5
        B, L = (2, 256)
        Bq, L_q, _ = queries.shape
        L_k = keys.shape[1]
        H, D = (N_HEADS, HEAD_DIM)

        def proj(x, W, b, Lx):
            return (x @ W.T + b).reshape(Bq, Lx, H, D).transpose(0, 2, 1, 3)
        q = proj(queries, Wq, bq, L_q)
        k = proj(keys, Wk, bk, L_k)
        v = proj(values, Wv, bv, L_k)
        q_norm = q / jnp.linalg.norm(q, axis=-1, keepdims=True)
        k_norm = k / jnp.linalg.norm(k, axis=-1, keepdims=True)
        scores_all = jnp.einsum('bhqd,bhkd->bhqk', q_norm, k_norm)
        mean_scores = scores_all.mean(axis=-1)
        u = max(1, L_q // TOP_FACTOR)
        _, top_idx = jax.lax.top_k(mean_scores, u)
        q_sel = jnp.take_along_axis(q, top_idx[..., None], axis=2)
        scores = jnp.einsum('bhud,bhkd->bhuk', q_sel, k) / math.sqrt(D)
        attn = jax.nn.softmax(scores, axis=-1)
        ctx_sel = jnp.einsum('bhuk,bhkd->bhud', attn, v)
        bidx = jnp.arange(Bq)[:, None, None]
        hidx = jnp.arange(H)[None, :, None]
        context = jnp.zeros((Bq, H, L_q, D), dtype=queries.dtype)
        context = context.at[bidx, hidx, top_idx].set(ctx_sel)
        out = context.transpose(0, 2, 1, 3).reshape(Bq, L_q, H * D)
        return out @ Wo.T + bo

    def _L3_ffn_ref(x, weight, bias):
        import jax, jax.numpy as jnp
        import numpy as np
        BLOCK_SIZE = 32
        FP6_E2M3_MAX = 7.5

        def _build_fp6_e2m3_grid():
            vals = set()
            for bits in range(64):
                s = bits >> 5 & 1
                e = bits >> 3 & 3
                m = bits & 7
                v = m / 8.0 if e == 0 else (1.0 + m / 8.0) * 2.0 ** (e - 1)
                vals.add(-v if s else v)
            return np.array(sorted(vals), dtype=np.float32)
        _GRID = jnp.asarray(_build_fp6_e2m3_grid())

        def _nearest_on_grid(x, grid):
            idx = jnp.clip(jnp.searchsorted(grid, x), 0, grid.shape[0] - 1)
            idx_lo = jnp.maximum(idx - 1, 0)
            v_hi = grid[idx]
            v_lo = grid[idx_lo]
            return jnp.where(jnp.abs(x - v_lo) <= jnp.abs(x - v_hi), v_lo, v_hi)

        def _mx_quantize(t, eps=1e-30):
            rows, K = t.shape
            blocks = t.reshape(rows, K // BLOCK_SIZE, BLOCK_SIZE)
            scales = jnp.maximum(jnp.max(jnp.abs(blocks), axis=-1) / FP6_E2M3_MAX, eps)
            q = _nearest_on_grid(blocks / scales[..., None], _GRID)
            return (q, scales)
        batch_shape = x.shape[:-1]
        in_features = x.shape[-1]
        x2 = x.astype(jnp.float32).reshape(-1, in_features)
        w2 = weight.astype(jnp.float32)
        xq, xs = _mx_quantize(x2)
        wq, ws = _mx_quantize(w2)
        xd = (xq * xs[..., None]).reshape(x2.shape)
        wd = (wq * ws[..., None]).reshape(w2.shape)
        out = xd @ wd.T + bias
        return out.reshape(*batch_shape, -1)
    x = x + jnp.tanh(g_xattn[0]) * _L0_xattn_ref(_layernorm(x, axis=-1), ctx_1024, ctx_1024, L0_xattn_Wq, L0_xattn_bq, L0_xattn_Wk, L0_xattn_bk, L0_xattn_Wv, L0_xattn_bv, L0_xattn_Wo, L0_xattn_bo)
    x = x + jnp.tanh(g_ffn[0]) * _L0_ffn_ref(_layernorm(x, axis=-1), L0_ffn_w_router, L0_ffn_w_block)
    x = x + jnp.tanh(g_xattn[1]) * _L1_xattn_ref(ctx_1024, ctx_1024, _layernorm(x, axis=-1), L1_xattn_Wv, L1_xattn_Wk, L1_xattn_Wq, L1_xattn_Wo, L1_xattn_bo)
    x = x + jnp.tanh(g_ffn[1]) * _L1_ffn_ref(_layernorm(x, axis=-1), L1_ffn_w_router, L1_ffn_fc1_w, L1_ffn_fc2_w, L1_ffn_gate_w, L1_ffn_up_w, L1_ffn_down_w)
    x = x + jnp.tanh(g_xattn[2]) * _L2_xattn_ref(_layernorm(x, axis=-1), ctx_1024, L2_xattn_Wq, L2_xattn_bq, L2_xattn_Wk, L2_xattn_bk, L2_xattn_Wv, L2_xattn_bv, L2_xattn_Wo, L2_xattn_bo)
    x = x + jnp.tanh(g_ffn[2]) * _L2_ffn_ref(_layernorm(x, axis=-1), L2_ffn_gate_w, L2_ffn_gate_b, L2_ffn_w1, L2_ffn_b1, L2_ffn_w2, L2_ffn_b2, L2_ffn_ws1, L2_ffn_bs1, L2_ffn_ws2, L2_ffn_bs2)
    x = x + jnp.tanh(g_xattn[3]) * _L3_xattn_ref(_layernorm(x, axis=-1), ctx_1024, ctx_1024, L3_xattn_Wq, L3_xattn_bq, L3_xattn_Wk, L3_xattn_bk, L3_xattn_Wv, L3_xattn_bv, L3_xattn_Wo, L3_xattn_bo)
    x = x + jnp.tanh(g_ffn[3]) * _L3_ffn_ref(_layernorm(x, axis=-1), L3_ffn_weight, L3_ffn_bias)
    return x

_drawn_inputs = setup_inputs


def setup_inputs(seed=0):
    import zlib

    import numpy as np

    out = dict(_drawn_inputs(seed))
    spreads = {'L0_xattn_bq': (0.0, 0.1),
     'L0_xattn_bk': (0.0, 2.0),
     'L0_xattn_bv': (0.0, 0.1),
     'L0_xattn_bo': (0.0, 0.1),
     'L2_xattn_bq': (0.0, 1.652),
     'L2_xattn_bk': (0.0, 2.0),
     'L2_xattn_bv': (0.0, 0.409),
     'L2_xattn_bo': (0.0, 0.391),
     'L2_ffn_gate_b': (0.0, 0.1),
     'L2_ffn_b1': (0.0, 0.682),
     'L2_ffn_b2': (0.0, 0.385),
     'L2_ffn_bs1': (0.0, 0.573),
     'L2_ffn_bs2': (0.0, 0.314),
     'L3_xattn_bq': (0.0, 0.8),
     'L3_xattn_bk': (0.0, 0.8),
     'L3_xattn_bv': (0.0, 0.8),
     'L3_xattn_bo': (0.0, 0.552)}
    factors = {'g_ffn': 8.0,
     'L1_xattn_bo': 5.69,
     'L1_ffn_w_router': 8.0,
     'L1_ffn_fc1_w': 8.0,
     'L1_ffn_fc2_w': 8.0,
     'L1_ffn_gate_w': 7.47,
     'L1_ffn_up_w': 7.409,
     'L1_ffn_down_w': 7.4,
     'L3_xattn_Wq': 6.455,
     'L3_xattn_Wk': 7.451,
     'L3_xattn_Wv': 7.167,
     'L3_xattn_Wo': 5.876,
     'L3_ffn_bias': 15.245,
     'L2_ffn_w1': 3.623,
     'L2_ffn_ws1': 3.164}
    for name, (base, spread) in spreads.items():
        noise = np.random.default_rng([zlib.crc32(name.encode()), seed]).standard_normal(out[name].shape)
        drawn = base * np.exp(spread * noise) if base else spread * noise
        out[name] = jnp.asarray(drawn.astype(out[name].dtype))
    for name, factor in factors.items():
        out[name] = (out[name] * factor).astype(out[name].dtype)
    return out
```

```python
from contextlib import ExitStack

import concourse.bass as bass
from concourse import mybir

F32 = mybir.dt.float32
BF16 = mybir.dt.bfloat16
U32 = mybir.dt.uint32
ALU = mybir.AluOpType
ACT = mybir.ActivationFunctionType
AX = mybir.AxisListType

P = 128
BATCHES, ROWS, D = 8, 256, 128
HEADS, HD = 16, 8
LAYERS = 4
STREAMS = 2
PAIRS = BATCHES // STREAMS
RT = ROWS // P
BANK = 512
TERMS = 6
SC_ROWS = 96
MAX_ROW = 96
SCT_ROWS = 99
VW = 32
CAUSAL, SPARSE = 2, 3
KEEP0 = ROWS * 3 // 4
TOPQ = ROWS // 5
ROUNDS = -(-TOPQ // 8)
SENT = 8 * ROUNDS - TOPQ
BIG = 3.0e38
EXPERTS = 8
HID = 512
HC = HID // P
SQRT_HD = float(HD) ** -0.5
FP6_MAX = 7.5
MAGIC = 1.5 * 2.0 ** 23

R_BV, R_BO, R_BQ3, R_BK3, R_BF3, R_GB = 0, 4 * D, 8 * D, 9 * D, 10 * D, 11 * D
R_W = 11 * D + EXPERTS


def schedule():
    out = [("load", s, 0) for s in range(STREAMS)] + [("keys", s, 0) for s in range(STREAMS)]
    for l in range(LAYERS):
        for step in ("query", "maxima", "attend", "project"):
            for s in range(STREAMS):
                out.append((step, s, l))
                if step == "attend" and l + 1 < LAYERS:
                    out.append(("keys", s, l + 1))
        for s in range(STREAMS):
            out.append((f"ffn{l}", s, l))
    return out + [("store", s, 0) for s in range(STREAMS)]


SCHEDULE = schedule()

MOE1 = [("h", 0), ("h", 1)] + [x for e in range(2, EXPERTS + 2) for x in (("o", e - 2), ("h", e))] + [("o", EXPERTS)]
MOE2 = ([("h", 0), ("b", 0)] + [x for e in range(1, EXPERTS + 1) for x in (("h", e), ("o", e - 1))]
        + [("o", EXPERTS)])


def max_tiles(l):
    out = []
    for r in range(RT):
        keys = P * (r + 1) if l == CAUSAL else ROWS
        n = BANK // keys
        out += [(r, keys, h0, n) for h0 in range(0, HEADS, n)]
    return out


def signals(step, s, l):
    sparse = l == SPARSE
    norm = {"var_ready": 1, "rstd_ready": 1, f"h_ready{s}": 1, "ac_full": 1, "ac_read": 1}
    tiles = len(max_tiles(l))
    return {
        "load": {f"x_loaded{s}": 16, f"ctx_loaded{s}": 16},
        "keys": {"dv_full": 4 if sparse else 2, "dv_read": 4 if sparse else 2, "hi_ready": 1,
                 f"k_parts_done{s}": 1, f"k_moved{s}": 32, "rows_ready": 2 * sparse, "rn_ready": sparse},
        "query": {**norm, "xb_ready": 1, "dv_full": 3 if sparse else 1, "dv_read": 3 if sparse else 1,
                  "ac_full": 2 if sparse else 1, "ac_read": 2 if sparse else 1, "hi_ready": 1,
                  f"q_parts_done{s}": 1, f"q_moved{s}": 32, "rows_ready": 2 * sparse, "rn_ready": sparse,
                  "sel_ready": sparse},
        "maxima": {"a_full": tiles, "a_read": tiles, "m_parts_done": 1, "ac_full": 1, "ac_read": 1,
                   f"m_moved{s}": 32},
        "attend": {"b_full": HEADS, "b_read": HEADS, "pv_done": 4, "c_read": 2},
        "project": {"a_full": RT, "a_read": RT, "heads_ready": 1, "ac_full": 1, "ac_read": 1,
                    "dv_full": 1, "dv_read": 1},
        "ffn0": {**norm, "ac_full": 2, "ac_read": 2, "dv_full": 1, "dv_read": 1, "x_done": 1},
        "ffn1": {**norm, "dv_full": 1, "dv_read": 1, "gap_ready": 1, "gap_exp": 1, "silu_ready": EXPERTS + 2,
                 "a_full": len(MOE1), "a_read": len(MOE1)},
        "ffn2": {**norm, "ac_full": 2, "ac_read": 2, "dv_full": 1, "dv_read": 1, "gap_ready": 1, "gap_exp": 1,
                 "comb_ready": 1, "b_full": 2 * (EXPERTS + 1), "b_read": 2 * (EXPERTS + 1),
                 "a_full": EXPERTS + 2, "a_read": EXPERTS + 2},
        "ffn3": {**norm, "xb_ready": 1, "xd_ready": 1, "dv_full": 1, "dv_read": 1},
        "store": {f"stored{s}": 16},
    }[step]


LINKS = {"dve_step": 210, "pool_step": 16}
CREDIT = {"a_read": 2, "b_read": 2, "c_read": 2, "dv_read": 1, "ac_read": 1, "pv_done": 2,
          "stored0": 1, "stored1": 1}


class Ledger:

    def __init__(self):
        self.start, total = [], {}
        for step, s, l in SCHEDULE:
            self.start.append(dict(total))
            for name, n in signals(step, s, l).items():
                total[name] = total.get(name, 0) + int(n)
        self.per_turn = {**total, **LINKS}

    def index(self, i, name, k):
        return self.start[i].get(name, 0) + k

    def value(self, turn, i, name, k):
        return turn * self.per_turn[name] + (self.index(i, name, k) + CREDIT.get(name, 0))


LEDGER = Ledger()
SEMAPHORES = sorted(LEDGER.per_turn)
STEP = {item: i for i, item in enumerate(SCHEDULE)}


def flamingo(nc, x, ctxT, attn_w, bias_cols, bias_rows, g_all, router0, block0, router1, fc1, fc2,
             gate_up, down, router2, w1, ws1, b1_cols, w2, ws2, b2_all, w3, ident_in, causal_qk,
             causal_kq, before_in, iota_in, out):
    with ExitStack() as ctx:
        def sb(name, shape, dt=F32):
            return ctx.enter_context(nc.sbuf_tensor(name, shape, dt))

        def two(name, shape, dt=F32):
            return [sb(f"{name}{s}", shape, dt) for s in range(STREAMS)]

        def psum(name, shape):
            return ctx.enter_context(nc.psum_tensor(name, shape, F32))

        def sem(name):
            return ctx.enter_context(nc.semaphore(name))

        attn_sb = sb("attn_sb", [P, LAYERS, 4, D])
        bcol = sb("bcol", [P, LAYERS, 2])
        brow = sb("brow", [P, R_W])
        gates = sb("gates", [P, 2 * LAYERS])
        tg = sb("tg", [P, 2 * LAYERS])
        gbo = sb("gbo", [P, LAYERS + 1, D])
        r0_sb = sb("r0_sb", [P, 1])
        r0_bc = sb("r0_bc", [P, P])
        blk0 = sb("blk0", [P, D])
        r1_sb = sb("r1_sb", [P, EXPERTS])
        fc1_sb = sb("fc1_sb", [P, EXPERTS + 2, 2, P])
        fc2_sb = sb("fc2_sb", [P, EXPERTS + 2, D])
        r2_sb = sb("r2_sb", [P, EXPERTS])
        w1_sb = sb("w1_sb", [P, EXPERTS + 1, HC, P])
        w2_sb = sb("w2_sb", [P, EXPERTS + 1, HC, D])
        b1_sb = sb("b1_sb", [P, EXPERTS + 1, HC])
        b2_sb = sb("b2_sb", [EXPERTS + 1, D])
        w3_sb = sb("w3_sb", [P, D])
        w3T = sb("w3T", [P, D])
        ident = sb("ident", [P, P])
        identb = sb("identb", [P, P], BF16)
        cqk = sb("cqk", [P, P])
        ckq = sb("ckq", [P, P])
        cqk_b = sb("cqk_b", [P, P], BF16)
        ckq_b = sb("ckq_b", [P, P], BF16)
        before = sb("before", [P, RT, ROWS])
        iota = sb("iota", [P, EXPERTS])
        mhalf = sb("mhalf", [P, RT * HEADS])
        eps = sb("eps", [P, RT])
        idle = sb("idle", [1, 1])
        mean_k = sb("mean_k", [P, P])

        xs = two("xs", [P, RT, D])
        cT = two("cT", [P, ROWS])
        stats = two("stats", [P, RT, 6])
        mv = two("mv", [P, RT, 2])
        veps = two("veps", [P, RT])
        rstd = two("rstd", [P, RT])
        h = two("h", [P, RT, D])
        hT = two("hT", [P, ROWS])
        q_parts = two("q_parts", [P, TERMS, ROWS], BF16)
        k_parts = two("k_parts", [P, TERMS, ROWS], BF16)
        resid = two("resid", [P, ROWS])
        q_st = two("q_st", [SCT_ROWS, HEADS, ROWS], BF16)
        k_st = two("k_st", [SCT_ROWS, HEADS, ROWS], BF16)
        v_aug = two("v_aug", [P, RT, HEADS, VW])
        mx = two("mx", [P, RT, HEADS])
        mres = two("mres", [P, RT, HEADS])
        m_parts = two("m_parts", [P, RT, P], BF16)
        mT = two("mT", [3 * HEADS, ROWS], BF16)
        raw = two("raw", [P, 4, ROWS])
        rden = two("rden", [P, RT, HEADS])
        heads_out = two("heads_out", [P, RT, D])
        coT = two("coT", [P, ROWS])
        ss = two("ss", [P, RT * HEADS])
        rn = two("rn", [P, RT * HEADS])
        dot = two("dot", [P, RT * HEADS])
        kbar = two("kbar", [P, D])
        work = two("work", [HEADS, SENT + ROWS])
        top8q = two("top8q", [HEADS, 8])
        selT = two("selT", [HEADS, ROWS])
        selm = two("selm", [P, RT, HEADS])
        junk = sb("junk", [P, ROWS])
        col = two("col", [P, 8, RT])
        lg = two("lg", [P, RT, EXPERTS])
        top = two("top", [P, RT, 8])
        topi = two("topi", [P, RT, 8], U32)
        topf = two("topf", [P, RT, 2])
        comb = two("comb", [P, RT, EXPERTS + 1])
        cmb2 = two("cmb2", [P, RT, EXPERTS])
        combT = two("combT", [EXPERTS + 1, ROWS])
        work_rows = [two(f"work_rows{i}_", [P, RT, D]) for i in range(4)]
        ffo = work_rows[2]
        sc3 = two("sc3", [P, RT * 4])
        rsc3 = two("rsc3", [P, RT * 4])
        amax = two("amax", [P, RT * 4])
        NPR, NACT, NHID = 8, 4, 2
        probs = sb("probs", [P, NPR, RT * ROWS])
        sil = sb("sil", [P, NACT, ROWS])
        acts = sb("acts", [P, NACT, ROWS])
        hid = sb("hid", [P, NHID, HC, ROWS])

        A = psum("A", [P, 2, BANK])
        B = psum("B", [P, 2, BANK])
        C = psum("C", [P, 2, 2, ROWS])
        DV = psum("DV", [P, BANK])
        AC = psum("AC", [P, BANK])

        def scratch(name, rows):
            return [nc.dram_tensor(f"{name}{s}", (rows, ROWS), BF16, kind="Internal").ap() for s in range(STREAMS)]

        q_scr, k_scr, m_scr = scratch("q_scr", TERMS * P), scratch("k_scr", TERMS * P), scratch("m_scr", 3 * HEADS)

        sems = {name: sem(name) for name in SEMAPHORES}
        attn_loaded, ffn_loaded, big_loaded = sem("attn_loaded"), sem("ffn_loaded"), sem("big_loaded")
        gates_done, w3_quantised, w3_turned = sem("gates_done"), sem("w3_quantised"), sem("w3_turned")
        w3_copied, setup_done, setup_step = sem("w3_copied"), sem("setup_done"), sem("setup_step")

        attention_loads = [
            (attn_sb[:, :, :, :], attn_w), (bcol[:, :, :], bias_cols), (ident[:, :], ident_in),
            (brow[:, :], bias_rows.broadcast_to([P, R_W])), (gates[:, :], g_all.broadcast_to([P, 2 * LAYERS])),
            (cqk[:, :], causal_qk), (ckq[:, :], causal_kq), (iota[:, :], iota_in),
            (before[:, :, :], before_in), (r0_sb[:, :], router0), (w3_sb[:, :], w3)]
        ffn_loads = [
            (blk0[:, :], block0), (r1_sb[:, :], router1),
            (fc1_sb[:, 0:EXPERTS, :, :].rearrange("d e a i -> d e (a i)"), fc1.rearrange("e d i -> d e i")),
            (fc1_sb[:, EXPERTS:EXPERTS + 2, :, :], gate_up),
            (fc2_sb[:, 0:EXPERTS, :], fc2.rearrange("e i d -> i e d")),
            (fc2_sb[:, EXPERTS:EXPERTS + 2, :], down.rearrange("(c i) d -> i c d", c=2))]
        big_loads = [
            (r2_sb[:, :], router2), (b1_sb[:, :, :], b1_cols), (b2_sb[:, :], b2_all),
            (w1_sb[:, 0:EXPERTS, :, :].rearrange("d e c i -> d e (c i)"), w1.rearrange("e d i -> d e i")),
            (w1_sb[:, EXPERTS, :, :].rearrange("d c i -> d (c i)"), ws1),
            (w2_sb[:, 0:EXPERTS, :, :].rearrange("i e c d -> i (e c) d"),
             w2.rearrange("e (c i) d -> i (e c) d", c=HC)),
            (w2_sb[:, EXPERTS, :, :], ws2.rearrange("(c i) d -> i c d", c=HC))]

        class Walk:

            def __init__(self, turn, own=None):
                self.turn, self.own, self.i, self.links = turn, own, 0, 0

            def at(self, name, k):
                return LEDGER.value(self.turn, self.i, name, k)

            def at_step(self, name, k, *item):
                return LEDGER.value(self.turn, STEP[item], name, k)

            def slot(self, name, k, slots):
                return (LEDGER.index(self.i, name, k) - 1) % slots

            def step(self):
                self.links += 1
                return self.turn * LINKS[self.own] + self.links

        block = ctx.enter_context(nc.Block())

        @block.sync
        def _(sp):
            for s in range(STREAMS):
                sp.sem_inc(sems[f"stored{s}"], CREDIT[f"stored{s}"])
            for dst, src in attention_loads:
                sp.dma_start(dst, src).then_inc(attn_loaded, 16)

            with sp.Fori(0, PAIRS) as turn:
                w = Walk(turn)
                for w.i, (step, s, l) in enumerate(SCHEDULE):
                    if step == "load":
                        sp.wait_ge(sems[f"stored{s}"], w.at(f"stored{s}", 0))
                        b = turn * STREAMS + s
                        sp.dma_start(cT[s][:, :], ctxT[b, :, :]).then_inc(sems[f"ctx_loaded{s}"], 16)
                        sp.dma_start(xs[s][:, :, :], x[b, :, :].rearrange("(t p) d -> p t d", p=P))\
                          .then_inc(sems[f"x_loaded{s}"], 16)
                    if step in ("keys", "query"):
                        n = step[0]
                        parts, scr, st = (k_parts, k_scr, k_st) if n == "k" else (q_parts, q_scr, q_st)
                        moved = sems[f"{n}_moved{s}"]
                        sp.wait_ge(sems[f"{n}_parts_done{s}"], w.at(f"{n}_parts_done{s}", 1))
                        sp.dma_start(scr[s].rearrange("(i p) r -> p i r", p=P), parts[s][:, :, :]).then_inc(moved, 16)
                        sp.wait_ge(moved, w.at(f"{n}_moved{s}", 16))
                        sp.dma_start(st[s][0:TERMS * HD, :, :].rearrange("p h r -> p (h r)"),
                                     scr[s].rearrange("(i h) r -> i (h r)", h=HEADS)).then_inc(moved, 16)
                    if step == "maxima":
                        moved = sems[f"m_moved{s}"]
                        sp.wait_ge(sems["ac_read"], w.at("ac_read", 1))
                        sp.dma_start(m_scr[s], mT[s][:, :]).then_inc(moved, 16)
                        sp.wait_ge(moved, w.at(f"m_moved{s}", 16))
                        sp.dma_start(q_st[s][MAX_ROW:MAX_ROW + 3, :, :].rearrange("p h r -> p (h r)"),
                                     m_scr[s].rearrange("(i h) r -> i (h r)", h=HEADS)).then_inc(moved, 16)
                    if step == "store":
                        sp.wait_ge(sems["dv_read"], w.at_step("dv_read", 1, "ffn3", s, LAYERS - 1))
                        sp.dma_start(out[turn * STREAMS + s, :, :].rearrange("(t p) d -> p t d", p=P),
                                     xs[s][:, :, :]).then_inc(sems[f"stored{s}"], 16)
            for s in range(STREAMS):
                sp.wait_ge(sems[f"stored{s}"], 16 * PAIRS + CREDIT[f"stored{s}"])

        @block.gpsimd
        def _(pool):
            for dst, src in ffn_loads:
                pool.dma_start(dst, src).then_inc(ffn_loaded, 16)
            for dst, src in big_loads:
                pool.dma_start(dst, src).then_inc(big_loaded, 16)
            pool.wait_ge(setup_done, 1)

            with pool.Fori(0, PAIRS) as turn:
                w = Walk(turn, "pool_step")
                for w.i, (step, s, l) in enumerate(SCHEDULE):
                    if step == "query" or step.startswith("ffn"):
                        pool.wait_ge(sems["var_ready"], w.at("var_ready", 1))
                        nc.gpsimd.tensor_tensor(veps[s][:, :], mv[s][:, :, 1], eps[:, :], ALU.add).then_inc(sems["pool_step"], 1)
                        pool.wait_ge(sems["pool_step"], w.step())
                        nc.gpsimd.tensor_tensor(rstd[s][:, :], veps[s][:, :], mhalf[:, 0:RT], ALU.pow)\
                          .then_inc(sems["rstd_ready"], 1)
                    if step == "query" or step == "ffn3":
                        pool.wait_ge(sems[f"h_ready{s}"], w.at(f"h_ready{s}", 1))
                        bias = gbo[:, l if step == "query" else LAYERS, :]
                        nc.gpsimd.tensor_tensor(xs[s][:, :, :], xs[s][:, :, :],
                                                bias.unsqueeze(1).broadcast_to([P, RT, D]), ALU.add)\
                          .then_inc(sems["xb_ready"], 1)
                    if step in ("keys", "query") and l == SPARSE:
                        pool.wait_ge(sems["rows_ready"], w.at("rows_ready", 1))
                        nc.gpsimd.tensor_tensor(rn[s][:, :], ss[s][:, :], mhalf[:, :], ALU.pow)\
                          .then_inc(sems["rn_ready"], 1)
                assert w.links == LINKS["pool_step"], w.links

        @block.scalar
        def _(act):
            for name in ("b_read", "c_read", "ac_read"):
                act.sem_inc(sems[name], CREDIT[name])
            act.wait_ge(attn_loaded, 16 * len(attention_loads))
            nc.scalar.activation(tg[:, :], gates[:, :], ACT.Tanh).then_inc(gates_done, 1)
            act.wait_ge(w3_turned, 1)
            nc.scalar.activation(w3T[:, :], AC[:, 0:D], ACT.Copy).then_inc(w3_copied, 1)
            act.wait_ge(setup_done, 1)

            with act.Fori(0, PAIRS) as turn:
                w = Walk(turn)

                def copy_ac(k, dst, src, func=ACT.Copy):
                    act.wait_ge(sems["ac_full"], w.at("ac_full", k))
                    nc.scalar.activation(dst, src, func).then_inc(sems["ac_read"], 1)

                for w.i, (step, s, l) in enumerate(SCHEDULE):
                    if step == "query" or step.startswith("ffn"):
                        copy_ac(1, hT[s][:, :], AC[:, 0:ROWS])
                    if step in ("keys", "query"):
                        parts, b = (k_parts, 1) if step == "keys" else (q_parts, 0)
                        act.wait_ge(sems["dv_full"], w.at("dv_full", 1))
                        nc.scalar.activation(parts[s][:, 0, :], DV[:, 0:ROWS], ACT.Identity,
                                             bias=bcol[:, l, b:b + 1]).then_inc(sems["hi_ready"], 1)
                    if step == "query" and l == SPARSE:
                        copy_ac(2, work[s][:, SENT:SENT + ROWS], AC[0:HEADS, 0:ROWS])
                    if step == "maxima":
                        copy_ac(1, mT[s][:, :], AC[:, :].bitcast(BF16)[0:3 * HEADS, 0:ROWS])
                    if step == "attend":
                        n = P + ROWS if l == CAUSAL else RT * ROWS
                        for k in range(1, HEADS + 1):
                            act.wait_ge(sems["b_full"], w.at("b_full", k))
                            act.wait_ge(sems["pv_done"], w.at("pv_done", (k - 1) // 4 + 1 - NPR // 4))
                            nc.scalar.activation(probs[:, (k - 1) % NPR, 0:n], B[:, w.slot("b_full", k, 2), 0:n],
                                                 ACT.Exp, scale=SQRT_HD).then_inc(sems["b_read"], 1)
                            if k in (13, HEADS):
                                half = 0 if k == 13 else 1
                                act.wait_ge(sems["pv_done"], w.at("pv_done", 2 * half + 2))
                                nc.scalar.activation(raw[s][:, 2 * half:2 * half + 2, :], C[:, half, :, :], ACT.Copy)\
                                  .then_inc(sems["c_read"], 1)
                    if step == "project":
                        copy_ac(1, coT[s][:, :], AC[:, 0:ROWS])
                    if step == "ffn0":
                        copy_ac(2, ffo[s][:, :, :].rearrange("p t d -> p (t d)"), AC[:, 0:RT * D], ACT.Gelu_apprx_tanh)
                    if step in ("ffn1", "ffn2"):
                        act.wait_ge(sems["gap_ready"], w.at("gap_ready", 1))
                        nc.scalar.activation(col[s][:, 1, :], col[s][:, 0, :], ACT.Exp).then_inc(sems["gap_exp"], 1)
                    if step == "ffn1":
                        for k, (kind, e) in enumerate(MOE1, 1):
                            if kind == "h":
                                act.wait_ge(sems["a_full"], w.at("a_full", k))
                                nc.scalar.activation(sil[:, w.slot("silu_ready", e + 1, NACT), :],
                                                     A[:, w.slot("a_full", k, 2), 0:ROWS], ACT.Silu)\
                                  .then_inc(sems["silu_ready"], 1)
                    if step == "ffn2":
                        copy_ac(2, combT[s][:, :], AC[0:EXPERTS + 1, 0:ROWS])
                        for e in range(EXPERTS + 1):
                            if e >= NHID:
                                act.wait_ge(sems["a_full"], w.at("a_full", e + 2 - NHID))
                            for half in range(2):
                                act.wait_ge(sems["b_full"], w.at("b_full", 2 * e + half + 1))
                                for j in range(2):
                                    c = 2 * half + j
                                    ins = nc.scalar.activation(
                                        hid[:, e % NHID, c, :],
                                        B[:, w.slot("b_full", 2 * e + half + 1, 2), j * ROWS:(j + 1) * ROWS],
                                        ACT.Gelu, bias=b1_sb[:, e, c:c + 1])
                                ins.then_inc(sems["b_read"], 1)

        @block.tensor
        def _(pe):
            for name in ("pv_done",):
                pe.sem_inc(sems[name], CREDIT[name])
            pe.wait_ge(w3_quantised, 1)
            nc.tensor.transpose(AC[:, 0:D], work_rows[0][0][:, 0, :], ident[:, :]).then_inc(w3_turned, 1)
            pe.wait_ge(w3_copied, 1)
            pe.wait_ge(setup_done, 1)

            with pe.Fori(0, PAIRS) as turn:
                w = Walk(turn)

                def turn_rows(k, src):
                    pe.wait_ge(sems["ac_read"], w.at("ac_read", k - 1))
                    for r in range(RT):
                        ins = nc.tensor.transpose(AC[:, r * P:(r + 1) * P], src[:, r, :], ident[:, :])
                    ins.then_inc(sems["ac_full"], 1)

                def rows_product(dst, xT, rhs):
                    n = rhs.shape[-1]
                    for r in range(RT):
                        ins = nc.tensor.matmul(dst[:, r * n:(r + 1) * n], xT[:, r * P:(r + 1) * P], rhs,
                                               start=True, stop=True)
                    return ins

                def scores(s, l, k, r, keys, h0, n):
                    pe.wait_ge(sems["a_read"], w.at("a_read", k - 2))
                    bank = A[:, w.slot("a_full", k, 2), :]
                    for i in range(n):
                        o = bank[:, i * keys:(i + 1) * keys]
                        ins = nc.tensor.matmul(o, q_st[s][0:SC_ROWS, h0 + i, r * P:(r + 1) * P],
                                               k_st[s][0:SC_ROWS, h0 + i, 0:keys], start=True, stop=l != CAUSAL)
                        if l == CAUSAL:
                            ins = nc.tensor.matmul(o[:, keys - P:keys], identb[:, :], cqk_b[:, :], start=False, stop=True)
                    ins.then_inc(sems["a_full"], 1)

                def scores_turned(s, l, hh):
                    pe.wait_ge(sems["b_read"], w.at("b_read", hh + 1 - 2))
                    bank = B[:, w.slot("b_full", hh + 1, 2), :]
                    for t in range(RT):
                        q0 = P * t if l == CAUSAL else 0
                        o = bank[:, t * ROWS:t * ROWS + ROWS - q0]
                        ins = nc.tensor.matmul(o, k_st[s][0:SCT_ROWS, hh, t * P:(t + 1) * P],
                                               q_st[s][0:SCT_ROWS, hh, q0:ROWS], start=True, stop=l != CAUSAL)
                        if l == CAUSAL:
                            ins = nc.tensor.matmul(o[:, 0:P], identb[:, :], ckq_b[:, :], start=False, stop=True)
                    ins.then_inc(sems["b_full"], 1)

                def weigh(s, l, g, t):
                    if t == 0:
                        pe.wait_ge(sems["b_read"], w.at("b_read", 4 * g + 4))
                        if g % 2 == 0:
                            pe.wait_ge(sems["c_read"], w.at("c_read", g // 2 + 1 - 2))
                    q0 = P * t if l == CAUSAL else 0
                    for j in range(4):
                        hh = 4 * g + j
                        ins = nc.tensor.matmul(C[VW * j:VW * (j + 1), g // 2, g % 2, q0:ROWS], v_aug[s][:, t, hh, :],
                                               probs[:, hh % NPR, t * ROWS:t * ROWS + ROWS - q0],
                                               start=t == 0, stop=t == RT - 1, tile_position=(0, VW * j))
                    if t == RT - 1:
                        ins.then_inc(sems["pv_done"], 1)

                def hidden1(e, k):
                    pe.wait_ge(sems["a_read"], w.at("a_read", k - 2))
                    for a in range(2):
                        ins = nc.tensor.matmul(A[:, w.slot("a_full", k, 2), a * ROWS:(a + 1) * ROWS],
                                               fc1_sb[:, e, a, :], hT[s][:, :], start=True, stop=True)
                    ins.then_inc(sems["a_full"], 1)

                def output1(e, k):
                    chunks = [e] if e < EXPERTS else [e, e + 1]
                    pe.wait_ge(sems["a_read"], w.at("a_read", MOE1.index(("h", chunks[-1])) + 1))
                    pe.wait_ge(sems["a_read"], w.at("a_read", k - 2))
                    for r in range(RT):
                        for c in chunks:
                            ins = nc.tensor.matmul(A[:, w.slot("a_full", k, 2), r * D:(r + 1) * D],
                                                   acts[:, w.slot("silu_ready", c + 1, NACT), r * P:(r + 1) * P],
                                                   fc2_sb[:, c, :], start=c == chunks[0], stop=c == chunks[-1])
                    ins.then_inc(sems["a_full"], 1)

                def hidden2(e):
                    for half in range(2):
                        pe.wait_ge(sems["b_read"], w.at("b_read", 2 * e + half + 1 - 2))
                        for j in range(2):
                            ins = nc.tensor.matmul(B[:, w.slot("b_full", 2 * e + half + 1, 2), j * ROWS:(j + 1) * ROWS],
                                                   w1_sb[:, e, 2 * half + j, :], hT[s][:, :], start=True, stop=True)
                        ins.then_inc(sems["b_full"], 1)

                def output2(e, k):
                    pe.wait_ge(sems["b_read"], w.at("b_read", 2 * e + 2))
                    pe.wait_ge(sems["a_read"], w.at("a_read", k + 1 - 2))
                    for r in range(RT):
                        for c in range(HC):
                            ins = nc.tensor.matmul(A[:, w.slot("a_full", k + 1, 2), r * D:(r + 1) * D],
                                                   hid[:, e % NHID, c, r * P:(r + 1) * P],
                                                   w2_sb[:, e, c, :], start=c == 0, stop=c == HC - 1)
                    ins.then_inc(sems["a_full"], 1)

                for w.i, (step, s, l) in enumerate(SCHEDULE):
                    if step == "keys":
                        if l == 0:
                            pe.wait_ge(sems[f"ctx_loaded{s}"], w.at_step(f"ctx_loaded{s}", 16, "load", s, 0))
                        pe.wait_ge(sems["dv_read"], w.at("dv_read", 0))
                        nc.tensor.matmul(DV[:, 0:ROWS], attn_sb[:, l, 1, :], cT[s][:, :], start=True, stop=True)\
                          .then_inc(sems["dv_full"], 1)
                        pe.wait_ge(sems["dv_read"], w.at("dv_read", 1))
                        rows_product(DV, cT[s], attn_sb[:, l, 2, :]).then_inc(sems["dv_full"], 1)
                        if l == SPARSE:
                            pe.wait_ge(sems["dv_read"], w.at("dv_read", 2))
                            rows_product(DV, cT[s], attn_sb[:, l, 1, :]).then_inc(sems["dv_full"], 1)
                            pe.wait_ge(sems["rows_ready"], w.at("rows_ready", 2))
                            pe.wait_ge(sems["dv_read"], w.at("dv_read", 3))
                            for t in range(RT):
                                ins = nc.tensor.matmul(DV[:, 0:D], mean_k[:, :], work_rows[1][s][:, t, :],
                                                       start=t == 0, stop=t == RT - 1)
                            ins.then_inc(sems["dv_full"], 1)
                    if step in ("query", "ffn0", "ffn1", "ffn2"):
                        pe.wait_ge(sems[f"h_ready{s}"], w.at(f"h_ready{s}", 1))
                        turn_rows(1, h[s])
                        pe.wait_ge(sems["ac_read"], w.at("ac_read", 1))
                    if step == "query":
                        pe.wait_ge(sems["dv_read"], w.at("dv_read", 0))
                        nc.tensor.matmul(DV[:, 0:ROWS], attn_sb[:, l, 0, :], hT[s][:, :], start=True, stop=True)\
                          .then_inc(sems["dv_full"], 1)
                        if l == SPARSE:
                            pe.wait_ge(sems["dv_read"], w.at("dv_read", 1))
                            rows_product(DV, hT[s], attn_sb[:, l, 0, :]).then_inc(sems["dv_full"], 1)
                            pe.wait_ge(sems["rows_ready"], w.at("rows_ready", 2))
                            pe.wait_ge(sems["ac_read"], w.at("ac_read", 1))
                            for r in range(RT):
                                ins = nc.tensor.transpose(AC[0:HEADS, r * P:(r + 1) * P],
                                                          rn[s][:, r * HEADS:(r + 1) * HEADS], ident[:, :])
                            ins.then_inc(sems["ac_full"], 1)
                            pe.wait_ge(sems["sel_ready"], w.at("sel_ready", 1))
                            pe.wait_ge(sems["dv_read"], w.at("dv_read", 2))
                            for r in range(RT):
                                ins = nc.tensor.matmul(DV[:, r * HEADS:(r + 1) * HEADS], selT[s][:, r * P:(r + 1) * P],
                                                       ident[0:HEADS, 0:HEADS], start=True, stop=True)
                            ins.then_inc(sems["dv_full"], 1)
                    if step == "maxima":
                        pe.wait_ge(sems[f"q_moved{s}"], w.at_step(f"q_moved{s}", 32, "query", s, l))
                        pe.wait_ge(sems[f"k_moved{s}"], w.at_step(f"k_moved{s}", 32, "keys", s, l))
                        for k, tile in enumerate(max_tiles(l), 1):
                            scores(s, l, k, *tile)
                        pe.wait_ge(sems["m_parts_done"], w.at("m_parts_done", 1))
                        pe.wait_ge(sems["ac_read"], w.at("ac_read", 0))
                        for r in range(RT):
                            ins = nc.tensor.transpose(AC[:, :].bitcast(BF16)[:, r * P:(r + 1) * P],
                                                      m_parts[s][:, r, :], identb[:, :])
                        ins.then_inc(sems["ac_full"], 1)
                    if step == "attend":
                        pe.wait_ge(sems[f"m_moved{s}"], w.at_step(f"m_moved{s}", 32, "maxima", s, l))
                        pe.wait_ge(sems["dv_read"], w.at_step("dv_read", 2, "keys", s, l))
                        for g in range(5):
                            for i in range(4):
                                if g < 4:
                                    scores_turned(s, l, 4 * g + i)
                                if g > 0 and i % 2 == 1:
                                    weigh(s, l, g - 1, i // 2)
                    if step == "project":
                        pe.wait_ge(sems["c_read"], w.at_step("c_read", 2, "attend", s, l))
                        for r in range(RT):
                            pe.wait_ge(sems["a_read"], w.at("a_read", r + 1 - 2))
                            for g in range(4):
                                ins = nc.tensor.transpose(A[:, w.slot("a_full", r + 1, 2), g * P:(g + 1) * P],
                                                          raw[s][:, g, r * P:(r + 1) * P], ident[:, :])
                            ins.then_inc(sems["a_full"], 1)
                        pe.wait_ge(sems["heads_ready"], w.at("heads_ready", 1))
                        turn_rows(1, heads_out[s])
                        pe.wait_ge(sems["ac_read"], w.at("ac_read", 1))
                        pe.wait_ge(sems["dv_read"], w.at("dv_read", 0))
                        rows_product(DV, coT[s], attn_sb[:, l, 3, :]).then_inc(sems["dv_full"], 1)
                    if step == "ffn0":
                        pe.wait_ge(ffn_loaded, 16 * len(ffn_loads))
                        pe.wait_ge(sems["dv_read"], w.at("dv_read", 0))
                        nc.tensor.matmul(DV[:, 0:ROWS], r0_bc[:, :], hT[s][:, :], start=True, stop=True)\
                          .then_inc(sems["dv_full"], 1)
                        pe.wait_ge(sems["ac_read"], w.at("ac_read", 1))
                        rows_product(AC, hT[s], blk0[:, :]).then_inc(sems["ac_full"], 1)
                    if step in ("ffn1", "ffn2"):
                        if step == "ffn2":
                            pe.wait_ge(big_loaded, 16 * len(big_loads))
                        pe.wait_ge(sems["dv_read"], w.at("dv_read", 0))
                        rows_product(DV, hT[s], (r1_sb if step == "ffn1" else r2_sb)[:, :]).then_inc(sems["dv_full"], 1)
                    if step == "ffn1":
                        for k, (kind, e) in enumerate(MOE1, 1):
                            (hidden1 if kind == "h" else output1)(e, k)
                    if step == "ffn2":
                        for kind, e in MOE2:
                            if kind == "h":
                                hidden2(e)
                            elif kind == "o":
                                output2(e, e + 1)
                            else:
                                pe.wait_ge(sems["comb_ready"], w.at("comb_ready", 1))
                                pe.wait_ge(sems["ac_read"], w.at("ac_read", 1))
                                for r in range(RT):
                                    ins = nc.tensor.transpose(AC[0:EXPERTS + 1, r * P:(r + 1) * P], comb[s][:, r, :],
                                                              ident[:, :])
                                ins.then_inc(sems["ac_full"], 1)
                                pe.wait_ge(sems["ac_read"], w.at("ac_read", 2))
                                pe.wait_ge(sems["a_read"], w.at("a_read", -1))
                                rows_product(A[:, w.slot("a_full", 1, 2), :], combT[s], b2_sb[:, :])\
                                    .then_inc(sems["a_full"], 1)
                    if step == "ffn3":
                        pe.wait_ge(sems["xd_ready"], w.at("xd_ready", 1))
                        turn_rows(1, h[s])
                        pe.wait_ge(sems["ac_read"], w.at("ac_read", 1))
                        pe.wait_ge(sems["dv_read"], w.at("dv_read", 0))
                        rows_product(DV, hT[s], w3T[:, :]).then_inc(sems["dv_full"], 1)

        @block.vector
        def _(dve):
            for name in ("a_read", "dv_read"):
                dve.sem_inc(sems[name], CREDIT[name])
            nc.vector.memset(mhalf[:, :], -0.5)
            nc.vector.memset(mean_k[:, :], 1.0 / ROWS)
            nc.vector.memset(eps[:, :], 1e-5)
            for s in range(STREAMS):
                nc.vector.memset(q_st[s][:, :, :].bitcast(F32), 0.0)
                nc.vector.memset(k_st[s][0:MAX_ROW, :, :].bitcast(F32), 0.0)
                nc.vector.memset(m_parts[s][:, :, :], 0.0)
                nc.vector.memset(k_st[s][MAX_ROW:SCT_ROWS, :, :], 1.0)
                nc.vector.memset(v_aug[s][:, :, :, HD:VW], 1.0)
                nc.vector.memset(work[s][:, 0:SENT], BIG)
            setup_count = iter(range(1, 100))

            def next_setup():
                return next(setup_count)

            def fp6(done, after, s, rows, src, dst):
                y, a, m2, inv = (wr[s][:, 0:rows, :] for wr in work_rows)
                amx, scale, rscale = (t[s][:, 0:4 * rows] for t in (amax, sc3, rsc3))

                def blocks(ap):
                    return ap.rearrange("p t (b i) -> p (t b) i", b=4)

                def per_block(ap):
                    return ap.unsqueeze(2).broadcast_to([P, 4 * rows, D // 4])

                nc.vector.tensor_reduce(amx, blocks(src), AX.X, ALU.max, apply_absolute_value=True).then_inc(done, 1)
                dve.wait_ge(done, after())
                nc.vector.tensor_scalar(scale, amx, 1.0 / FP6_MAX, 1e-30, ALU.mult, ALU.max).then_inc(done, 1)
                dve.wait_ge(done, after())
                nc.vector.reciprocal(rscale, scale).then_inc(done, 1)
                dve.wait_ge(done, after())
                nc.vector.tensor_tensor(blocks(y), blocks(src), per_block(rscale), ALU.mult).then_inc(done, 1)
                dve.wait_ge(done, after())
                nc.vector.tensor_tensor(a, y, y, ALU.mult).then_inc(done, 1)
                dve.wait_ge(done, after())
                nc.vector.tensor_scalar(m2, a, 4.0, -4.0, ALU.is_ge, ALU.mult).then_inc(done, 1)
                dve.wait_ge(done, after())
                nc.vector.tensor_scalar(inv, a, 16.0, -2.0, ALU.is_ge, ALU.mult).then_inc(done, 1)
                dve.wait_ge(done, after())
                nc.vector.scalar_tensor_tensor(inv, m2, 8.0, inv, ALU.add, ALU.add).then_inc(done, 1)
                dve.wait_ge(done, after())
                nc.vector.tensor_tensor(y, y, inv, ALU.mult).then_inc(done, 1)
                dve.wait_ge(done, after())
                nc.vector.tensor_scalar(a, y, MAGIC, MAGIC, ALU.add, ALU.subtract).then_inc(done, 1)
                dve.wait_ge(done, after())
                nc.vector.tensor_tensor(y, a, y, ALU.subtract).then_inc(done, 1)
                dve.wait_ge(done, after())
                nc.vector.scalar_tensor_tensor(a, y, 0.5, a, ALU.is_ge, ALU.subtract).then_inc(done, 1)
                dve.wait_ge(done, after())
                nc.vector.reciprocal(m2, inv).then_inc(done, 1)
                dve.wait_ge(done, after())
                nc.vector.scalar_tensor_tensor(y, a, -1.0, m2, ALU.mult, ALU.mult).then_inc(done, 1)
                dve.wait_ge(done, after())
                return nc.vector.tensor_tensor(blocks(dst), blocks(y), per_block(scale), ALU.mult)

            dve.wait_ge(attn_loaded, 16 * len(attention_loads))
            nc.vector.tensor_copy(identb[:, :], ident[:, :])
            nc.vector.tensor_copy(cqk_b[:, :], cqk[:, :])
            nc.vector.tensor_copy(ckq_b[:, :], ckq[:, :])
            nc.vector.tensor_copy(r0_bc[:, :], r0_sb[:, :].broadcast_to([P, P])).then_inc(setup_step, 1)
            dve.wait_ge(setup_step, next_setup())
            dve.wait_ge(gates_done, 1)
            for l in range(LAYERS):
                nc.vector.tensor_scalar(gbo[:, l, :], brow[:, R_BO + l * D:R_BO + (l + 1) * D], tg[:, l:l + 1], None,
                                        ALU.mult)
            for s in range(STREAMS):
                nc.vector.tensor_copy(comb[s][:, :, EXPERTS],
                                      tg[:, LAYERS + 2:LAYERS + 3].broadcast_to([P, RT]))
            nc.vector.tensor_scalar(gbo[:, LAYERS, :], brow[:, R_BF3:R_BF3 + D],
                                               tg[:, 2 * LAYERS - 1:2 * LAYERS], None, ALU.mult).then_inc(setup_step, 1)
            dve.wait_ge(setup_step, next_setup())
            fp6(setup_step, next_setup, 0, 1, w3_sb[:, :].unsqueeze(1), work_rows[0][0][:, 0:1, :]).then_inc(w3_quantised, 1)
            dve.wait_ge(w3_copied, 1)
            nc.vector.memset(junk[:, :], 0.0).then_inc(setup_done, 1)

            with dve.Fori(0, PAIRS) as turn:
                w = Walk(turn, "dve_step")

                def pause():
                    nc.vector.memset(idle[:, :], 0.0)

                def norm(s):
                    for r in range(RT):
                        ins = nc.vector.bn_stats(stats[s][:, r, :], xs[s][:, r, :])
                    ins.then_inc(sems["dve_step"], 1)
                    dve.wait_ge(sems["dve_step"], w.step())
                    pause()
                    nc.vector.bn_aggr(mv[s][:, 0, :], stats[s][:, 0, :])
                    nc.vector.bn_aggr(mv[s][:, 1, :], stats[s][:, 1, :]).then_inc(sems["var_ready"], 1)
                    dve.wait_ge(sems["rstd_ready"], w.at("rstd_ready", 1))
                    for r in range(RT):
                        ins = nc.vector.tensor_scalar(h[s][:, r, :], xs[s][:, r, :], mv[s][:, r, 0:1],
                                                      rstd[s][:, r:r + 1], ALU.subtract, ALU.mult)
                    ins.then_inc(sems[f"h_ready{s}"], 1)

                def split(s, l, parts, b, name):
                    dve.wait_ge(sems["hi_ready"], w.at("hi_ready", 1))
                    nc.vector.scalar_tensor_tensor(resid[s][:, :], DV[:, 0:ROWS], bcol[:, l, b:b + 1],
                                                   parts[s][:, 0, :], ALU.add, ALU.subtract)\
                        .then_inc(sems["dv_read"], 1)
                    dve.wait_ge(sems["dv_read"], w.at("dv_read", 1))
                    mid, low = (3, 5) if name == "q" else (1, 2)
                    nc.vector.tensor_copy(parts[s][:, mid, :], resid[s][:, :]).then_inc(sems["dve_step"], 1)
                    dve.wait_ge(sems["dve_step"], w.step())
                    nc.vector.tensor_tensor(parts[s][:, low, :], resid[s][:, :], parts[s][:, mid, :],
                                                 ALU.subtract).then_inc(sems["dve_step"], 1)
                    dve.wait_ge(sems["dve_step"], w.step())
                    if name == "q":
                        nc.vector.tensor_copy(parts[s][:, 1, :], parts[s][:, 0, :])
                        nc.vector.tensor_copy(parts[s][:, 2, :], parts[s][:, 0, :])
                        ins = nc.vector.tensor_copy(parts[s][:, 4, :], parts[s][:, 3, :])
                    else:
                        nc.vector.tensor_copy(parts[s][:, 3:5, :], parts[s][:, 0:2, :])
                        ins = nc.vector.tensor_copy(parts[s][:, 5, :], parts[s][:, 0, :])
                    ins.then_inc(sems[f"{name}_parts_done{s}"], 1)

                def rows_norms(s, k, bias):
                    dve.wait_ge(sems["dv_full"], w.at("dv_full", k))
                    nc.vector.tensor_tensor(work_rows[0][s][:, :, :],
                                            DV[:, 0:RT * D].rearrange("p (h t d) -> p t h d", t=RT, h=1).rearrange("p t h d -> p t (h d)"),
                                            bias, ALU.add).then_inc(sems["dv_read"], 1)
                    dve.wait_ge(sems["dv_read"], w.at("dv_read", k))
                    nc.vector.tensor_tensor(work_rows[1][s][:, :, :], work_rows[0][s][:, :, :],
                                                 work_rows[0][s][:, :, :], ALU.mult).then_inc(sems["dve_step"], 1)
                    dve.wait_ge(sems["dve_step"], w.step())
                    head_sums(ss[s], work_rows[1][s]).then_inc(sems["rows_ready"], 1)

                def head_sums(dst, src):
                    return nc.vector.tensor_reduce(dst[:, :].rearrange("p (t h) -> p t h", t=RT),
                                                   src[:, :, :].rearrange("p t (d h) -> p t h d", d=HD), AX.X, ALU.add)

                def by_head(ap):
                    return ap.rearrange("p (t h) -> p t h", t=RT).unsqueeze(2).broadcast_to([P, RT, HD, HEADS])

                def over_tiles(ap, n):
                    return ap.unsqueeze(1).broadcast_to([P, RT, n])

                def choose(s):
                    bias = over_tiles(brow[:, R_BQ3:R_BQ3 + D], D)
                    rows_norms(s, 2, bias)
                    dve.wait_ge(sems["rows_ready"], w.at("rows_ready", 1))
                    nc.vector.tensor_tensor(work_rows[1][s][:, :, :], work_rows[0][s][:, :, :],
                                                 over_tiles(kbar[s][:, :], D), ALU.mult).then_inc(sems["dve_step"], 1)
                    dve.wait_ge(sems["dve_step"], w.step())
                    head_sums(dot[s], work_rows[1][s]).then_inc(sems["dve_step"], 1)
                    dve.wait_ge(sems["dve_step"], w.step())
                    dve.wait_ge(sems["rn_ready"], w.at("rn_ready", 1))
                    nc.vector.tensor_tensor(rn[s][:, :], rn[s][:, :], dot[s][:, :], ALU.mult)\
                        .then_inc(sems["rows_ready"], 1)
                    dve.wait_ge(sems["ac_read"], w.at("ac_read", 2))
                    for r in range(ROUNDS):
                        pause()
                        nc.vector.max(top8q[s][:, :], work[s][:, :]).then_inc(sems["dve_step"], 1)
                        dve.wait_ge(sems["dve_step"], w.step())
                        pause()
                        nc.vector.match_replace(work[s][:, :], top8q[s][:, :], work[s][:, :], -BIG).then_inc(sems["dve_step"], 1)
                        dve.wait_ge(sems["dve_step"], w.step())
                    nc.vector.tensor_scalar(selT[s][:, :], work[s][:, SENT:SENT + ROWS], -0.5 * BIG, None, ALU.is_le)\
                        .then_inc(sems["sel_ready"], 1)
                    dve.wait_ge(sems["sel_ready"], w.at("sel_ready", 1))
                    nc.vector.memset(work[s][:, 0:SENT], BIG).then_inc(sems["dve_step"], 1)
                    dve.wait_ge(sems["dve_step"], w.step())
                    dve.wait_ge(sems["dv_full"], w.at("dv_full", 3))
                    nc.vector.tensor_copy(selm[s][:, :, :].rearrange("p t h -> p (t h)"), DV[:, 0:RT * HEADS])\
                        .then_inc(sems["dv_read"], 1)

                def combine(s, l):
                    dve.wait_ge(sems["dv_full"], w.at("dv_full", 1))
                    logits = DV[:, 0:RT * EXPERTS].rearrange("p (t e) -> p t e", t=RT)
                    if l == 2:
                        ins = nc.vector.tensor_tensor(lg[s][:, :, :], logits,
                                                      over_tiles(brow[:, R_GB:R_GB + EXPERTS], EXPERTS), ALU.add)
                    else:
                        ins = nc.vector.tensor_copy(lg[s][:, :, :], logits)
                    ins.then_inc(sems["dv_read"], 1)
                    dve.wait_ge(sems["dv_read"], w.at("dv_read", 1))
                    pause()
                    nc.vector.max(top[s][:, 0, :], lg[s][:, 0, :])
                    nc.vector.max(top[s][:, 1, :], lg[s][:, 1, :]).then_inc(sems["dve_step"], 1)
                    dve.wait_ge(sems["dve_step"], w.step())
                    pause()
                    nc.vector.max_index(topi[s][:, 0, :], top[s][:, 0, :], lg[s][:, 0, :])
                    nc.vector.max_index(topi[s][:, 1, :], top[s][:, 1, :], lg[s][:, 1, :]).then_inc(sems["dve_step"], 1)
                    dve.wait_ge(sems["dve_step"], w.step())
                    nc.vector.tensor_copy(topf[s][:, :, :], topi[s][:, :, 0:2])
                    nc.vector.tensor_tensor(col[s][:, 0, :], top[s][:, :, 1], top[s][:, :, 0], ALU.subtract)\
                        .then_inc(sems["gap_ready"], 1)
                    dve.wait_ge(sems["gap_exp"], w.at("gap_exp", 1))
                    nc.vector.tensor_scalar(col[s][:, 2, :], col[s][:, 1, :], 1.0, None, ALU.add).then_inc(sems["dve_step"], 1)
                    dve.wait_ge(sems["dve_step"], w.step())
                    nc.vector.reciprocal(col[s][:, 3, :], col[s][:, 2, :]).then_inc(sems["dve_step"], 1)
                    dve.wait_ge(sems["dve_step"], w.step())
                    gate = tg[:, LAYERS + l:LAYERS + l + 1]
                    nc.vector.scalar_tensor_tensor(col[s][:, 5, :], col[s][:, 1, :], gate, col[s][:, 3, :],
                                                        ALU.mult, ALU.mult).then_inc(sems["dve_step"], 1)
                    dve.wait_ge(sems["dve_step"], w.step())
                    nc.vector.tensor_scalar(col[s][:, 4, :], col[s][:, 3, :], gate, None, ALU.mult).then_inc(sems["dve_step"], 1)
                    dve.wait_ge(sems["dve_step"], w.step())
                    for r in range(RT):
                        nc.vector.tensor_scalar(comb[s][:, r, 0:EXPERTS], iota[:, :], topf[s][:, r, 0:1],
                                                col[s][:, 4, r:r + 1], ALU.is_equal, ALU.mult)
                        ins = nc.vector.tensor_scalar(cmb2[s][:, r, :], iota[:, :], topf[s][:, r, 1:2],
                                                      col[s][:, 5, r:r + 1], ALU.is_equal, ALU.mult)
                    ins.then_inc(sems["dve_step"], 1)
                    dve.wait_ge(sems["dve_step"], w.step())
                    return nc.vector.tensor_tensor(comb[s][:, :, 0:EXPERTS], comb[s][:, :, 0:EXPERTS],
                                                   cmb2[s][:, :, :], ALU.add)

                def accumulate(s, k, scale):
                    dve.wait_ge(sems["a_full"], w.at("a_full", k))
                    for r in range(RT):
                        ins = nc.vector.scalar_tensor_tensor(xs[s][:, r, :], A[:, w.slot("a_full", k, 2), r * D:(r + 1) * D],
                                                             scale(r), xs[s][:, r, :], ALU.mult, ALU.add)
                    ins.then_inc(sems["a_read"], 1)
                    dve.wait_ge(sems["a_read"], w.at("a_read", k))

                for w.i, (step, s, l) in enumerate(SCHEDULE):
                    if step == "keys":
                        dve.wait_ge(sems["dv_full"], w.at("dv_full", 1))
                        split(s, l, k_parts, 1, "k")
                        dve.wait_ge(sems["dv_full"], w.at("dv_full", 2))
                        bv = over_tiles(brow[:, R_BV + l * D:R_BV + (l + 1) * D], D).rearrange("p t (h d) -> p t h d", d=HD)
                        nc.vector.tensor_tensor(v_aug[s][:, :, :, 0:HD],
                                                DV[:, 0:RT * D].rearrange("p (t h d) -> p t h d", t=RT, d=HD), bv,
                                                ALU.add).then_inc(sems["dv_read"], 1)
                        if l == SPARSE:
                            rows_norms(s, 3, over_tiles(brow[:, R_BK3:R_BK3 + D], D))
                            dve.wait_ge(sems["rn_ready"], w.at("rn_ready", 1))
                            nc.vector.tensor_tensor(work_rows[1][s][:, :, :].rearrange("p t (d h) -> p t d h", d=HD),
                                                    work_rows[0][s][:, :, :].rearrange("p t (d h) -> p t d h", d=HD),
                                                    by_head(rn[s][:, :]), ALU.mult).then_inc(sems["rows_ready"], 1)
                            dve.wait_ge(sems["dv_full"], w.at("dv_full", 4))
                            nc.vector.tensor_copy(kbar[s][:, :], DV[:, 0:D]).then_inc(sems["dv_read"], 1)
                    if step == "query" or step.startswith("ffn"):
                        if step == "query" and l == 0:
                            dve.wait_ge(sems[f"x_loaded{s}"], w.at_step(f"x_loaded{s}", 16, "load", s, 0))
                        norm(s)
                    if step == "query":
                        dve.wait_ge(sems["dv_full"], w.at("dv_full", 1))
                        split(s, l, q_parts, 0, "q")
                        if l == SPARSE:
                            choose(s)
                    if step == "maxima":
                        for k, (r, keys, h0, n) in enumerate(max_tiles(l), 1):
                            dve.wait_ge(sems["a_full"], w.at("a_full", k))
                            nc.vector.tensor_reduce(mx[s][:, r, h0:h0 + n],
                                                    A[:, w.slot("a_full", k, 2), :].rearrange("p (n k) -> p n k", n=n),
                                                    AX.X, ALU.max).then_inc(sems["a_read"], 1)
                        dve.wait_ge(sems["a_read"], w.at("a_read", len(max_tiles(l))))
                        nc.vector.tensor_scalar(m_parts[s][:, :, 0:HEADS], mx[s][:, :, :], -1.0, None, ALU.mult).then_inc(sems["dve_step"], 1)
                        dve.wait_ge(sems["dve_step"], w.step())
                        nc.vector.scalar_tensor_tensor(mres[s][:, :, :], mx[s][:, :, :], -1.0,
                                                            m_parts[s][:, :, 0:HEADS], ALU.mult, ALU.subtract).then_inc(sems["dve_step"], 1)
                        dve.wait_ge(sems["dve_step"], w.step())
                        nc.vector.tensor_copy(m_parts[s][:, :, 1 * HEADS:2 * HEADS], mres[s][:, :, :]).then_inc(sems["dve_step"], 1)
                        dve.wait_ge(sems["dve_step"], w.step())
                        nc.vector.tensor_tensor(m_parts[s][:, :, 2 * HEADS:3 * HEADS], mres[s][:, :, :], m_parts[s][:, :, 1 * HEADS:2 * HEADS],
                                                ALU.subtract).then_inc(sems["m_parts_done"], 1)
                    if step == "project":
                        for r in range(RT):
                            dve.wait_ge(sems["a_full"], w.at("a_full", r + 1))
                            bank = A[:, w.slot("a_full", r + 1, 2), :].rearrange("p (h v) -> p h v", v=VW)
                            nc.vector.reciprocal(rden[s][:, r, :], bank[:, :, HD]).then_inc(sems["dve_step"], 1)
                            dve.wait_ge(sems["dve_step"], w.step())
                            if l == SPARSE:
                                nc.vector.tensor_tensor(rden[s][:, r, :], rden[s][:, r, :], selm[s][:, r, :],
                                                             ALU.mult).then_inc(sems["dve_step"], 1)
                                dve.wait_ge(sems["dve_step"], w.step())
                            nc.vector.tensor_tensor(heads_out[s][:, r, :].rearrange("p (h d) -> p h d", d=HD),
                                                    bank[:, :, 0:HD],
                                                    rden[s][:, r, :].unsqueeze(2).broadcast_to([P, HEADS, HD]),
                                                    ALU.mult).then_inc(sems["a_read"], 1)
                        dve.wait_ge(sems["a_read"], w.at("a_read", RT))
                        dve.sem_inc(sems["heads_ready"], 1)
                        dve.wait_ge(sems["dv_full"], w.at("dv_full", 1))
                        dve.wait_ge(sems["xb_ready"], w.at_step("xb_ready", 1, "query", s, l))
                        nc.vector.scalar_tensor_tensor(xs[s][:, :, :].rearrange("p t d -> p (t d)"), DV[:, 0:RT * D],
                                                       tg[:, l:l + 1], xs[s][:, :, :].rearrange("p t d -> p (t d)"),
                                                       ALU.mult, ALU.add).then_inc(sems["dv_read"], 1)
                        dve.wait_ge(sems["dv_read"], w.at("dv_read", 1))
                    if step == "ffn0":
                        dve.wait_ge(sems["dv_full"], w.at("dv_full", 1))
                        for r in range(RT):
                            nc.vector.scalar_tensor_tensor(junk[:, 0:P], DV[:, r * P:(r + 1) * P], 1.0,
                                                                ident[:, :], ALU.mult, ALU.mult,
                                                                accum_out=col[s][:, 0, r:r + 1]).then_inc(sems["dve_step"], 1)
                            dve.wait_ge(sems["dve_step"], w.step())
                            nc.vector.tensor_scalar(junk[:, :], DV[:, 0:ROWS], col[s][:, 0, r:r + 1], None,
                                                         ALU.is_gt, ALU.add, accum_out=col[s][:, 1, r:r + 1]).then_inc(sems["dve_step"], 1)
                            dve.wait_ge(sems["dve_step"], w.step())
                            ins = nc.vector.scalar_tensor_tensor(junk[:, :], DV[:, 0:ROWS], col[s][:, 0, r:r + 1],
                                                                 before[:, r, :], ALU.is_equal, ALU.mult,
                                                                 accum_out=col[s][:, 2, r:r + 1])
                            if r == 0:
                                ins.then_inc(sems["dve_step"], 1)
                                dve.wait_ge(sems["dve_step"], w.step())
                        ins.then_inc(sems["dv_read"], 1)
                        dve.wait_ge(sems["dv_read"], w.at("dv_read", 1))
                        nc.vector.tensor_tensor(col[s][:, 3, :], col[s][:, 1, :], col[s][:, 2, :], ALU.add).then_inc(sems["dve_step"], 1)
                        dve.wait_ge(sems["dve_step"], w.step())
                        nc.vector.tensor_scalar(col[s][:, 4, :], col[s][:, 3, :], KEEP0 - 0.5, None, ALU.is_lt)
                        nc.vector.tensor_scalar(col[s][:, 5, :], col[s][:, 3, :], KEEP0 - 0.5, None, ALU.is_gt).then_inc(sems["dve_step"], 1)
                        dve.wait_ge(sems["dve_step"], w.step())
                        dve.wait_ge(sems["ac_read"], w.at("ac_read", 2))
                        for r in range(RT):
                            nc.vector.tensor_scalar(h[s][:, r, :], h[s][:, r, :], col[s][:, 5, r:r + 1], None,
                                                         ALU.mult).then_inc(sems["dve_step"], 1)
                            dve.wait_ge(sems["dve_step"], w.step())
                            nc.vector.scalar_tensor_tensor(h[s][:, r, :], ffo[s][:, r, :], col[s][:, 4, r:r + 1],
                                                                h[s][:, r, :], ALU.mult, ALU.add).then_inc(sems["dve_step"], 1)
                            dve.wait_ge(sems["dve_step"], w.step())
                        nc.vector.scalar_tensor_tensor(xs[s][:, :, :], h[s][:, :, :], tg[:, LAYERS:LAYERS + 1],
                                                       xs[s][:, :, :], ALU.mult, ALU.add).then_inc(sems["x_done"], 1)
                        dve.wait_ge(sems["x_done"], w.at("x_done", 1))
                    if step == "ffn1":
                        combine(s, 1).then_inc(sems["dve_step"], 1)
                        dve.wait_ge(sems["dve_step"], w.step())
                        for k, (kind, e) in enumerate(MOE1, 1):
                            if kind == "h":
                                i = w.slot("silu_ready", e + 1, NACT)
                                dve.wait_ge(sems["silu_ready"], w.at("silu_ready", e + 1))
                                nc.vector.tensor_tensor(acts[:, i, :], sil[:, i, :],
                                                        A[:, w.slot("a_full", k, 2), ROWS:2 * ROWS], ALU.mult)\
                                    .then_inc(sems["a_read"], 1)
                            elif e < EXPERTS:
                                accumulate(s, k, lambda r: comb[s][:, r, e:e + 1])
                            else:
                                accumulate(s, k, lambda r: tg[:, LAYERS + 1:LAYERS + 2])
                    if step == "ffn2":
                        combine(s, 2).then_inc(sems["comb_ready"], 1)
                        dve.wait_ge(sems["comb_ready"], w.at("comb_ready", 1))
                        dve.wait_ge(sems["a_full"], w.at("a_full", 1))
                        nc.vector.tensor_tensor(xs[s][:, :, :].rearrange("p t d -> p (t d)"),
                                                A[:, w.slot("a_full", 1, 2), 0:RT * D],
                                                xs[s][:, :, :].rearrange("p t d -> p (t d)"), ALU.add)\
                            .then_inc(sems["a_read"], 1)
                        dve.wait_ge(sems["a_read"], w.at("a_read", 1))
                        for e in range(EXPERTS + 1):
                            accumulate(s, e + 2, lambda r: comb[s][:, r, e:e + 1])
                    if step == "ffn3":
                        dve.wait_ge(sems[f"h_ready{s}"], w.at(f"h_ready{s}", 1))
                        fp6(sems["dve_step"], w.step, s, RT, h[s][:, :, :], h[s][:, :, :]).then_inc(sems["xd_ready"], 1)
                        dve.wait_ge(sems["dv_full"], w.at("dv_full", 1))
                        dve.wait_ge(sems["xb_ready"], w.at("xb_ready", 1))
                        nc.vector.scalar_tensor_tensor(xs[s][:, :, :].rearrange("p t d -> p (t d)"), DV[:, 0:RT * D],
                                                       tg[:, 2 * LAYERS - 1:2 * LAYERS],
                                                       xs[s][:, :, :].rearrange("p t d -> p (t d)"),
                                                       ALU.mult, ALU.add).then_inc(sems["dv_read"], 1)
                assert w.links == LINKS["dve_step"], w.links

    return nc


def _arrays(i):
    import numpy as np

    f = np.float32

    def turned(w, by_feature):
        t = np.asarray(w).T
        return t.reshape(D, HEADS, HD).transpose(0, 2, 1).reshape(D, D) if by_feature else t

    def vec(name):
        return np.asarray(i[name]) if name in i else np.zeros(D, f)

    def dh(v):
        return v.reshape(HEADS, HD).T.reshape(D)

    attn_w = np.stack([np.stack([turned(i[f"L{l}_xattn_Wq"], True), turned(i[f"L{l}_xattn_Wk"], True),
                                 turned(i[f"L{l}_xattn_Wv"], False), turned(i[f"L{l}_xattn_Wo"], False)], axis=1)
                       for l in range(LAYERS)], axis=1)
    bias_cols = np.stack([np.stack([dh(vec(f"L{l}_xattn_bq")), dh(vec(f"L{l}_xattn_bk"))], axis=1)
                          for l in range(LAYERS)], axis=1)
    rows = [vec(f"L{l}_xattn_bv") for l in range(LAYERS)] + [vec(f"L{l}_xattn_bo") for l in range(LAYERS)]
    rows += [dh(vec("L3_xattn_bq")), dh(vec("L3_xattn_bk")), vec("L3_ffn_bias"), vec("L2_ffn_gate_b")]
    gate, up = (np.asarray(i[f"L1_ffn_{n}_w"]).reshape(D, 2, P) for n in ("gate", "up"))
    b1 = np.concatenate([i["L2_ffn_b1"], np.asarray(i["L2_ffn_bs1"])[None]])
    k, q = np.arange(P)[:, None], np.arange(P)[None, :]
    row = np.arange(ROWS).reshape(RT, P).T[:, :, None]
    return {
        "x": i["x"], "ctxT": np.asarray(i["ctx_1024"]).transpose(0, 2, 1),
        "attn_w": attn_w, "bias_cols": bias_cols, "bias_rows": np.concatenate(rows)[None],
        "g_all": np.concatenate([i["g_xattn"], i["g_ffn"]])[None],
        "router0": np.asarray(i["L0_ffn_w_router"])[:, None], "block0": i["L0_ffn_w_block"],
        "router1": i["L1_ffn_w_router"], "fc1": i["L1_ffn_fc1_w"], "fc2": i["L1_ffn_fc2_w"],
        "gate_up": np.stack([gate, up], axis=2), "down": i["L1_ffn_down_w"],
        "router2": i["L2_ffn_gate_w"], "w1": i["L2_ffn_w1"], "ws1": i["L2_ffn_ws1"],
        "b1_cols": b1.reshape(EXPERTS + 1, HC, P).transpose(2, 0, 1), "w2": i["L2_ffn_w2"],
        "ws2": i["L2_ffn_ws2"], "b2_all": np.concatenate([i["L2_ffn_b2"], np.asarray(i["L2_ffn_bs2"])[None]]),
        "w3": i["L3_ffn_weight"],
        "ident_in": np.eye(P, dtype=f), "causal_qk": np.where(q > k, f(-1e30), f(0)).astype(f),
        "causal_kq": np.where(k > q, f(-1e30), f(0)).astype(f),
        "before_in": (np.arange(ROWS)[None, None] < row).astype(f),
        "iota_in": np.broadcast_to(np.arange(EXPERTS, dtype=f), (P, EXPERTS)),
    }


def kernel(**inputs):
    import numpy as _np
    import concourse.bacc as _bacc
    from concourse import mybir as _mybir
    from concourse.bass_utils import run_bass_kernel_spmd as _run

    nc = _bacc.Bacc("TRN2", target_bir_lowering=False, num_devices=1)
    arrays, args = {}, {}
    for name, a in _arrays(inputs).items():
        a = _np.ascontiguousarray(a)
        arrays[f"in_{name}"] = a
        args[name] = nc.dram_tensor(f"in_{name}", a.shape, _mybir.dt.from_np(a.dtype), kind="ExternalInput").ap()
    out = nc.dram_tensor("out_x", (BATCHES, ROWS, D), F32, kind="ExternalOutput").ap()
    flamingo(nc, out=out, **args)
    r = _run(nc, [arrays], core_ids=[0])
    return r.results[0]["out_x"]
```

```python
from contextlib import ExitStack

import concourse.bass as bass
from concourse import mybir

F32 = mybir.dt.float32
BF16 = mybir.dt.bfloat16
U32 = mybir.dt.uint32
ALU = mybir.AluOpType
ACT = mybir.ActivationFunctionType
AX = mybir.AxisListType

P = 128
BATCHES, ROWS, D = 8, 256, 128
HEADS, HD = 16, 8
LAYERS = 4
STREAMS = 2
PAIRS = BATCHES // STREAMS
RT = ROWS // P
BANK = 512
Q_TERMS = (0, 0, 0, 1, 1, 2)
K_TERMS = (0, 1, 2, 0, 1, 0)
TERMS = len(Q_TERMS)
SC_ROWS = 96
MAX_ROW = 96
SCT_ROWS = 99
VW = 32
CAUSAL, SPARSE = 2, 3
KEEP0 = ROWS * 3 // 4
TOPQ = ROWS // 5
ROUNDS = -(-TOPQ // 8)
SENT = 8 * ROUNDS - TOPQ
BIG = 3.0e38
EXPERTS = 8
HID = 512
HC = HID // P
SQRT_HD = float(HD) ** -0.5
SQRT_2_PI = 0.7978845608028654
CUBIC = 0.044715
FP6_MAX = 7.5
MAGIC = 1.5 * 2.0 ** 23

R_BV, R_BO, R_BQ3, R_BK3, R_BF3, R_GB = 0, 4 * D, 8 * D, 9 * D, 10 * D, 11 * D
R_W = 11 * D + EXPERTS


MAX_STEPS = 2 * (HEADS // 4)
ATT_STEPS = HEADS // 2 + 2
CHUNKS = {1: EXPERTS + 2, 2: EXPERTS + 1}


def stream_steps():
    def keys(l):
        return [("keys", l, 0)] + ([("key_mean", l, 0)] if l == SPARSE else [])

    def norm(l):
        return [("stats", l, 0), ("norm", l, 0)]

    out = [("load", 0, 0)] + keys(0)
    for l in range(LAYERS):
        out += norm(l) + [("turn", l, 0), ("query", l, 0)]
        scores = [("maxima", l, part) for part in range(MAX_STEPS)] + [("attend", l, part) for part in range(ATT_STEPS)]
        half = MAX_STEPS // 2
        extra = {("maxima", half): ("max_parts", 0), ("maxima", half + 1): ("max_turn", 0),
                 ("attend", 0): ("max_parts", 1), ("attend", 2): ("max_turn", 1)}
        if l == SPARSE:
            extra.update({("maxima", 1): ("query_rows", 0), ("maxima", half - 1): ("query_means", 0),
                          ("attend", 1): ("choose", 0), ("attend", 3): ("choose", 1), ("attend", ATT_STEPS - 1): ("chosen", 0)})
        for step, _, part in scores:
            if (step, part) in extra:
                out.append((extra[step, part][0], l, extra[step, part][1]))
            out.append((step, l, part))
        out += [("heads", l, 0), ("heads_turn", l, 0)]
        if l + 1 < LAYERS:
            out += keys(l + 1)
        out += [("project", l, 0)] + norm(l + LAYERS)
        if l == 0:
            out += [("turn", LAYERS, 0), ("route0", l, 0), ("gelu0", l, 0), ("blend0", l, 0)]
        if l in CHUNKS:
            out += [("turn", l + LAYERS, 0), ("logits", l, 0), ("hidden", l, 0), ("combine", l, 0), ("hidden", l, 1)]
            if l == 2:
                out += [("comb_turn", l, 0), ("out_bias", l, 0)]
            for n in range(CHUNKS[l]):
                out += [("output", l, n)] + [("hidden", l, n + 2)] * (n + 2 < CHUNKS[l])
        if l == 3:
            out += [("quantise", l, 0), ("quantise", l, 1), ("turn", l + LAYERS, 0), ("affine3", l, 0)]
    return out + [("store", 0, 0)]


TURNS_TAKEN = """
1011100101001111111111110101110100101001010010101101010110100001100010100101001111111111111101100011
0101111100101000100101000110011010101101110101100101001000110100101001001001001000011111011111110110
1101101100110110100111010101010100010100011000000001001010101000101011001001010111100110010001100000
10111001010110101101111110110111101110000000100000101000001000010000100010011000
"""


def schedule():
    left = [iter([(step, s, l, part) for step, l, part in stream_steps()]) for s in range(STREAMS)]
    return [next(left[int(s)]) for s in TURNS_TAKEN.split() for s in s]


SCHEDULE = schedule()


def max_tiles(l, part):
    g, r = divmod(part, RT)
    keys = P * (r + 1) if l == CAUSAL else ROWS
    n = BANK // keys
    return [(r, keys, h0, n) for h0 in range(4 * g, 4 * g + 4, n)]


def signals(step, s, l, part):
    return {
        "load": {f"x_loaded{s}": 16, f"ctx_loaded{s}": 16},
        "keys": {"dv_full": 2, "dv_read": 2, f"hi_ready{s}": 1, f"k_split{s}": 2, f"k_moved{s}": 16 * TERMS},
        "key_mean": {"dv_full": 2, "dv_read": 2, "rows_ready": 2, "rn_ready": 1},
        "stats": {"var_ready": 1, "rstd_ready": 1},
        "norm": {f"h_ready{s}": 1, "xb_ready": int(l < LAYERS or l == 2 * LAYERS - 1)},
        "turn": {"ac_full": 1, "ac_read": 1},
        "query": {"dv_full": 1, "dv_read": 1, f"hi_ready{s}": 1, f"q_split{s}": 2, f"q_moved{s}": 16 * TERMS},
        "query_rows": {"dv_full": 1, "dv_read": 1, "rows_ready": 2, "rn_ready": 1},
        "query_means": {"ac_full": 1, "ac_read": 1},
        "choose": {"sel_ready": part},
        "chosen": {"dv_full": 1, "dv_read": 1},
        "maxima": {"a_full": len(max_tiles(l, part % MAX_STEPS)), "a_read": len(max_tiles(l, part % MAX_STEPS))},
        "max_parts": {"m_parts_done": 1},
        "max_turn": {"ac_full": 1, "ac_read": 1, f"m_moved{s}": 16},
        "attend": {"b_full": 2 * (part < HEADS // 2), "b_read": 2 * (part < HEADS // 2),
                   f"pv_done{s}": int(part > 2 and part % 2 == 1), f"c_read{s}": int(part in (5, ATT_STEPS - 1))},
        "heads": {"a_full": RT, "a_read": RT},
        "heads_turn": {"ac_full": 1, "ac_read": 1},
        "project": {"dv_full": 1, "dv_read": 1},
        "route0": {"dv_full": 1, "dv_read": 1, "ac_full": 1, "ac_read": 1},
        "gelu0": {"cubic_ready": 1, "tanh_ready": 1},
        "blend0": {"x_done": 1},
        "logits": {"dv_full": 1, "dv_read": 1, "gap_ready": 1, "gap_exp": 1},
        "combine": {"comb_ready": 1},
        "comb_turn": {"ac_full": 1, "ac_read": 1},
        "out_bias": {"a_full": 1, "a_read": 1},
        "hidden": ({"a_full": 1, "a_read": 1, "tanh_ready": 1} if l == 1 else {"b_full": 2, "b_read": 2}),
        "output": ({} if (l, part) == (1, EXPERTS) else {"a_full": 1, "a_read": 1}),
        "quantise": {"xd_ready": part},
        "affine3": {"dv_full": 1, "dv_read": 1},
        "store": {f"stored{s}": 16},
    }[step]


LINKS = {"dve_step": 236}
CREDIT = {"a_read": 2, "b_read": 2, "dv_read": 1, "ac_read": 1, "stored0": 1, "stored1": 1}


class Ledger:

    def __init__(self):
        self.start, total = [], {}
        for item in SCHEDULE:
            self.start.append(dict(total))
            for name, n in signals(*item).items():
                total[name] = total.get(name, 0) + int(n)
        self.per_turn = {**{name: n for name, n in total.items() if n}, **LINKS}

    def index(self, i, name, k):
        return self.start[i].get(name, 0) + k

    def value(self, turn, i, name, k):
        return turn * self.per_turn[name] + (self.index(i, name, k) + CREDIT.get(name, 0))


LEDGER = Ledger()
SEMAPHORES = sorted(LEDGER.per_turn)
STEP = {item: i for i, item in enumerate(SCHEDULE)}


def flamingo(nc, x, ctxT, attn_w, bias_cols, bias_rows, g_all, router0, block0, router1, fc1, fc2,
             gate_up, down, router2, w1, ws1, b1_cols, w2, ws2, b2_all, w3, ident_in, causal_qk,
             causal_kq, before_in, iota_in, out):
    with ExitStack() as ctx:
        def sb(name, shape, dt=F32):
            return ctx.enter_context(nc.sbuf_tensor(name, shape, dt))

        def two(name, shape, dt=F32):
            return [sb(f"{name}{s}", shape, dt) for s in range(STREAMS)]

        def psum(name, shape):
            return ctx.enter_context(nc.psum_tensor(name, shape, F32))

        def sem(name):
            return ctx.enter_context(nc.semaphore(name))

        attn_sb = sb("attn_sb", [P, LAYERS, 4, D])
        bcol = sb("bcol", [P, LAYERS, 2])
        brow = sb("brow", [P, R_W])
        gates = sb("gates", [P, 2 * LAYERS])
        tg = sb("tg", [P, 2 * LAYERS])
        tgh = sb("tgh", [P, 2 * LAYERS])
        gbo = sb("gbo", [P, LAYERS + 1, D])
        r0_sb = sb("r0_sb", [P, 1])
        r0_bc = sb("r0_bc", [P, P])
        blk0 = sb("blk0", [P, D])
        r1_sb = sb("r1_sb", [P, EXPERTS])
        fc1_sb = sb("fc1_sb", [P, EXPERTS + 2, 2, P])
        fc2_sb = sb("fc2_sb", [P, EXPERTS + 2, D])
        r2_sb = sb("r2_sb", [P, EXPERTS])
        w1_sb = sb("w1_sb", [P, EXPERTS + 1, HC, P])
        w2_sb = sb("w2_sb", [P, EXPERTS + 1, HC, D])
        b1_sb = sb("b1_sb", [P, EXPERTS + 1, HC])
        b2_sb = sb("b2_sb", [EXPERTS + 1, D])
        w3_sb = sb("w3_sb", [P, D])
        w3T = sb("w3T", [P, D])
        ident = sb("ident", [P, P])
        identb = sb("identb", [P, P], BF16)
        cqk = sb("cqk", [P, P])
        ckq = sb("ckq", [P, P])
        cqk_b = sb("cqk_b", [P, P], BF16)
        ckq_b = sb("ckq_b", [P, P], BF16)
        before = sb("before", [P, RT, ROWS])
        iota = sb("iota", [P, EXPERTS])
        mhalf = sb("mhalf", [P, RT * HEADS])
        idle = sb("idle", [1, STREAMS, 3])
        mean_k = sb("mean_k", [P, P])

        xs = two("xs", [P, RT, D])
        cT = two("cT", [P, ROWS])
        stats = two("stats", [P, RT, 6])
        mv = two("mv", [P, RT, 2])
        veps = two("veps", [P, RT])
        rstd = two("rstd", [P, RT])
        h = two("h", [P, RT, D])
        hT = two("hT", [P, ROWS])
        q_parts = two("q_parts", [P, 3, ROWS], BF16)
        k_parts = two("k_parts", [P, 3, ROWS], BF16)
        resid = two("resid", [P, ROWS])
        q_st = two("q_st", [SCT_ROWS, HEADS, ROWS], BF16)
        k_st = two("k_st", [SCT_ROWS, HEADS, ROWS], BF16)
        v_aug = two("v_aug", [P, RT, HEADS, VW])
        mx = two("mx", [P, RT, HEADS])
        mres = two("mres", [P, RT, HEADS])
        m_parts = two("m_parts", [P, 2, RT, P], BF16)
        mT = two("mT", [3 * HEADS // 2, 2, ROWS], BF16)
        raw = two("raw", [P, 4, ROWS])
        rden = two("rden", [P, RT, HEADS])
        heads_out = two("heads_out", [P, RT, D])
        coT = two("coT", [P, ROWS])
        ss = two("ss", [P, RT * HEADS])
        rn = two("rn", [P, RT * HEADS])
        dot = two("dot", [P, RT * HEADS])
        kbar = two("kbar", [P, D])
        work = two("work", [HEADS, SENT + ROWS])
        top8q = two("top8q", [HEADS, 8])
        selT = two("selT", [HEADS, ROWS])
        selm = two("selm", [P, RT, HEADS])
        junk = sb("junk", [P, ROWS])
        col = two("col", [P, 8, RT])
        lg = two("lg", [P, RT, EXPERTS])
        top = two("top", [P, RT, 8])
        topi = two("topi", [P, RT, 8], U32)
        topf = two("topf", [P, RT, 2])
        comb = two("comb", [P, RT, EXPERTS + 1])
        cmb2 = two("cmb2", [P, RT, EXPERTS])
        combT = two("combT", [EXPERTS + 1, ROWS])
        work_rows = [two(f"work_rows{i}_", [P, RT, D]) for i in range(4)]
        ffo = work_rows[2]
        sc3 = two("sc3", [P, RT * 4])
        rsc3 = two("rsc3", [P, RT * 4])
        amax = two("amax", [P, RT * 4])
        NPR, NACT = 8, 4
        probs = two("probs", [P, NPR, RT * ROWS])
        acts = [p[:, 0:NACT // 2, :].rearrange("p n (a r) -> p (n a) r", a=2) for p in probs]
        tanhs = [p[:, NACT // 2:NACT, :].rearrange("p n (a r) -> p (n a) r", a=2) for p in probs]
        hid = [p[:, :, :].rearrange("p (n c) (a r) -> p n (c a) r", n=NACT, a=2) for p in probs]

        A = psum("A", [P, 2, BANK])
        B = psum("B", [P, 2, BANK])
        C = psum("C", [P, STREAMS, 2, ROWS])
        DV = psum("DV", [P, BANK])
        AC = psum("AC", [P, BANK])

        sems = {name: sem(name) for name in SEMAPHORES}
        attn_loaded, ffn_loaded, big_loaded = sem("attn_loaded"), sem("ffn_loaded"), sem("big_loaded")
        gates_done, w3_quantised, w3_turned = sem("gates_done"), sem("w3_quantised"), sem("w3_turned")
        w3_copied, setup_done, setup_step = sem("w3_copied"), sem("setup_done"), sem("setup_step")

        attention_loads = [
            (attn_sb[:, :, :, :], attn_w), (bcol[:, :, :], bias_cols), (ident[:, :], ident_in),
            (brow[:, :], bias_rows.broadcast_to([P, R_W])), (gates[:, :], g_all.broadcast_to([P, 2 * LAYERS])),
            (cqk[:, :], causal_qk), (ckq[:, :], causal_kq), (iota[:, :], iota_in),
            (before[:, :, :], before_in), (r0_sb[:, :], router0), (w3_sb[:, :], w3)]
        ffn_loads = [
            (blk0[:, :], block0), (r1_sb[:, :], router1),
            (fc1_sb[:, 0:EXPERTS, :, :].rearrange("d e a i -> d e (a i)"), fc1.rearrange("e d i -> d e i")),
            (fc1_sb[:, EXPERTS:EXPERTS + 2, :, :], gate_up),
            (fc2_sb[:, 0:EXPERTS, :], fc2.rearrange("e i d -> i e d")),
            (fc2_sb[:, EXPERTS:EXPERTS + 2, :], down.rearrange("(c i) d -> i c d", c=2))]
        big_loads = [
            (r2_sb[:, :], router2), (b1_sb[:, :, :], b1_cols), (b2_sb[:, :], b2_all),
            (w1_sb[:, 0:EXPERTS, :, :].rearrange("d e c i -> d e (c i)"), w1.rearrange("e d i -> d e i")),
            (w1_sb[:, EXPERTS, :, :].rearrange("d c i -> d (c i)"), ws1),
            (w2_sb[:, 0:EXPERTS, :, :].rearrange("i e c d -> i (e c) d"),
             w2.rearrange("e (c i) d -> i (e c) d", c=HC)),
            (w2_sb[:, EXPERTS, :, :], ws2.rearrange("(c i) d -> i c d", c=HC))]

        class Walk:

            def __init__(self, turn, own=None):
                self.turn, self.own, self.i, self.links = turn, own, 0, 0

            def at(self, name, k):
                return LEDGER.value(self.turn, self.i, name, k)

            def at_step(self, name, k, *item):
                return LEDGER.value(self.turn, STEP[item], name, k)

            def slot(self, name, k, slots):
                return (LEDGER.index(self.i, name, k) - 1) % slots

            def step(self):
                self.links += 1
                return self.turn * LINKS[self.own] + self.links

        block = ctx.enter_context(nc.Block())

        @block.sync
        def _(sp):
            for s in range(STREAMS):
                sp.sem_inc(sems[f"stored{s}"], CREDIT[f"stored{s}"])
            for dst, src in attention_loads:
                sp.dma_start(dst, src).then_inc(attn_loaded, 16)

            with sp.Fori(0, PAIRS) as turn:
                w = Walk(turn)
                for w.i, (step, s, l, part) in enumerate(SCHEDULE):
                    if step == "load":
                        sp.wait_ge(sems[f"stored{s}"], w.at(f"stored{s}", 0))
                        b = turn * STREAMS + s
                        sp.dma_start(cT[s][:, :], ctxT[b, :, :]).then_inc(sems[f"ctx_loaded{s}"], 16)
                        sp.dma_start(xs[s][:, :, :], x[b, :, :].rearrange("(t p) d -> p t d", p=P))\
                          .then_inc(sems[f"x_loaded{s}"], 16)
                    if step == "keys":
                        for n in range(3):
                            if n == 0:
                                sp.wait_ge(sems[f"hi_ready{s}"], w.at(f"hi_ready{s}", 1))
                            else:
                                sp.wait_ge(sems[f"k_split{s}"], w.at(f"k_split{s}", n))
                            for i in [i for i in range(TERMS) if K_TERMS[i] == n]:
                                sp.dma_start(k_st[s][i * HD:(i + 1) * HD, :, :], k_parts[s][:, n, :])\
                                  .then_inc(sems[f"k_moved{s}"], 16)
                    if step == "query":
                        for n in range(3):
                            if n == 0:
                                sp.wait_ge(sems[f"hi_ready{s}"], w.at(f"hi_ready{s}", 1))
                            else:
                                sp.wait_ge(sems[f"q_split{s}"], w.at(f"q_split{s}", n))
                            for i in [i for i in range(TERMS) if Q_TERMS[i] == n]:
                                sp.dma_start(q_st[s][i * HD:(i + 1) * HD, :, :], q_parts[s][:, n, :])\
                                  .then_inc(sems[f"q_moved{s}"], 16)
                    if step == "max_turn":
                        sp.wait_ge(sems["ac_read"], w.at("ac_read", 1))
                        h0 = part * HEADS // 2
                        sp.dma_start(q_st[s][MAX_ROW:MAX_ROW + 3, h0:h0 + HEADS // 2, :],
                                     mT[s][0:3 * HEADS // 2, part, :]).then_inc(sems[f"m_moved{s}"], 16)
                    if step == "store":
                        sp.wait_ge(sems["dv_read"], w.at_step("dv_read", 1, "affine3", s, 3, 0))
                        sp.dma_start(out[turn * STREAMS + s, :, :].rearrange("(t p) d -> p t d", p=P),
                                     xs[s][:, :, :]).then_inc(sems[f"stored{s}"], 16)
            for s in range(STREAMS):
                sp.wait_ge(sems[f"stored{s}"], 16 * PAIRS + CREDIT[f"stored{s}"])

        @block.gpsimd
        def _(pool):
            for dst, src in ffn_loads:
                pool.dma_start(dst, src).then_inc(ffn_loaded, 16)
            for dst, src in big_loads:
                pool.dma_start(dst, src).then_inc(big_loaded, 16)
            pool.wait_ge(setup_done, 1)

            with pool.Fori(0, PAIRS) as turn:
                w = Walk(turn)
                for w.i, (step, s, l, part) in enumerate(SCHEDULE):
                    if step == "stats":
                        pool.wait_ge(sems["var_ready"], w.at("var_ready", 1))
                        nc.gpsimd.tensor_tensor(rstd[s][:, :], veps[s][:, :], mhalf[:, 0:RT], ALU.pow)\
                            .then_inc(sems["rstd_ready"], 1)
                    if step == "norm" and (l < LAYERS or l == 2 * LAYERS - 1):
                        pool.wait_ge(sems[f"h_ready{s}"], w.at(f"h_ready{s}", 1))
                        nc.gpsimd.tensor_tensor(xs[s][:, :, :], xs[s][:, :, :],
                                                gbo[:, min(l, LAYERS), :].unsqueeze(1).broadcast_to([P, RT, D]), ALU.add)\
                            .then_inc(sems["xb_ready"], 1)
                    if step in ("key_mean", "query_rows"):
                        pool.wait_ge(sems["rows_ready"], w.at("rows_ready", 1))
                        nc.gpsimd.tensor_tensor(rn[s][:, :], ss[s][:, :], mhalf[:, :], ALU.pow)\
                            .then_inc(sems["rn_ready"], 1)

        @block.scalar
        def _(act):
            for name in ("b_read", "ac_read"):
                act.sem_inc(sems[name], CREDIT[name])
            act.wait_ge(attn_loaded, 16 * len(attention_loads))
            nc.scalar.activation(tg[:, :], gates[:, :], ACT.Tanh).then_inc(gates_done, 1)
            act.wait_ge(w3_turned, 1)
            nc.scalar.activation(w3T[:, :], AC[:, 0:D], ACT.Copy).then_inc(w3_copied, 1)
            act.wait_ge(setup_done, 1)

            with act.Fori(0, PAIRS) as turn:
                w = Walk(turn)

                def copy_ac(k, dst, src, func=ACT.Copy):
                    act.wait_ge(sems["ac_full"], w.at("ac_full", k))
                    nc.scalar.activation(dst, src, func).then_inc(sems["ac_read"], 1)

                for w.i, (step, s, l, part) in enumerate(SCHEDULE):
                    if step == "turn":
                        copy_ac(1, hT[s][:, :], AC[:, 0:ROWS])
                    if step in ("keys", "query"):
                        parts, b = (k_parts, 1) if step == "keys" else (q_parts, 0)
                        act.wait_ge(sems["dv_full"], w.at("dv_full", 1))
                        nc.scalar.activation(parts[s][:, 0, :], DV[:, 0:ROWS], ACT.Identity,
                                             bias=bcol[:, l, b:b + 1]).then_inc(sems[f"hi_ready{s}"], 1)
                    if step == "query_means":
                        copy_ac(1, work[s][:, SENT:SENT + ROWS], AC[0:HEADS, 0:ROWS])
                    if step == "max_turn":
                        copy_ac(1, mT[s][:, part, :], AC[:, :].bitcast(BF16)[0:3 * HEADS // 2, 0:ROWS])
                    if step == "attend":
                        n = P + ROWS if l == CAUSAL else RT * ROWS
                        if part in (4, 6):
                            act.wait_ge(sems[f"pv_done{s}"], w.at_step(f"pv_done{s}", 1, "attend", s, l, part - 1))
                        for k in range(1, 3 if part < HEADS // 2 else 1):
                            act.wait_ge(sems["b_full"], w.at("b_full", k))
                            nc.scalar.activation(probs[s][:, (2 * part + k - 1) % NPR, 0:n],
                                                 B[:, w.slot("b_full", k, 2), 0:n],
                                                 ACT.Exp, scale=SQRT_HD).then_inc(sems["b_read"], 1)
                        if part in (5, ATT_STEPS - 1):
                            g0 = 0 if part == 5 else 2
                            act.wait_ge(sems[f"pv_done{s}"], w.at(f"pv_done{s}", 1))
                            nc.scalar.activation(raw[s][:, g0:g0 + 2, :], C[:, s, :, :], ACT.Copy)\
                                .then_inc(sems[f"c_read{s}"], 1)
                    if step == "heads_turn":
                        copy_ac(1, coT[s][:, :], AC[:, 0:ROWS])
                    if step == "route0":
                        copy_ac(1, ffo[s][:, :, :].rearrange("p t d -> p (t d)"), AC[:, 0:RT * D])
                    if step == "gelu0":
                        act.wait_ge(sems["cubic_ready"], w.at("cubic_ready", 1))
                        nc.scalar.activation(work_rows[1][s][:, :, :], work_rows[0][s][:, :, :], ACT.Tanh,
                                             scale=SQRT_2_PI).then_inc(sems["tanh_ready"], 1)
                    if step == "logits":
                        act.wait_ge(sems["gap_ready"], w.at("gap_ready", 1))
                        nc.scalar.activation(col[s][:, 1, :], col[s][:, 0, :], ACT.Exp).then_inc(sems["gap_exp"], 1)
                    if step == "hidden" and l == 1:
                        act.wait_ge(sems["a_full"], w.at("a_full", 1))
                        nc.scalar.activation(tanhs[s][:, part % NACT, :], A[:, w.slot("a_full", 1, 2), 0:ROWS], ACT.Tanh,
                                             scale=0.5).then_inc(sems["tanh_ready"], 1)
                    if step == "comb_turn":
                        copy_ac(1, combT[s][:, :], AC[0:EXPERTS + 1, 0:ROWS])
                    if step == "hidden" and l == 2:
                        for half in range(2):
                            act.wait_ge(sems["b_full"], w.at("b_full", half + 1))
                            for j in range(2):
                                c = 2 * half + j
                                ins = nc.scalar.activation(
                                    hid[s][:, part % NACT, c, :],
                                    B[:, w.slot("b_full", half + 1, 2), j * ROWS:(j + 1) * ROWS],
                                    ACT.Gelu, bias=b1_sb[:, part, c:c + 1])
                            ins.then_inc(sems["b_read"], 1)

        @block.tensor
        def _(pe):
            pe.wait_ge(w3_quantised, 1)
            nc.tensor.transpose(AC[:, 0:D], work_rows[0][0][:, 0, :], ident[:, :]).then_inc(w3_turned, 1)
            pe.wait_ge(w3_copied, 1)
            pe.wait_ge(setup_done, 1)

            with pe.Fori(0, PAIRS) as turn:
                w = Walk(turn)

                def turn_rows(k, src):
                    pe.wait_ge(sems["ac_read"], w.at("ac_read", k - 1))
                    for r in range(RT):
                        ins = nc.tensor.transpose(AC[:, r * P:(r + 1) * P], src[:, r, :], ident[:, :])
                    ins.then_inc(sems["ac_full"], 1)

                def rows_product(dst, xT, rhs):
                    n = rhs.shape[-1]
                    for r in range(RT):
                        ins = nc.tensor.matmul(dst[:, r * n:(r + 1) * n], xT[:, r * P:(r + 1) * P], rhs,
                                               start=True, stop=True)
                    return ins

                def scores(s, l, k, r, keys, h0, n):
                    pe.wait_ge(sems["a_read"], w.at("a_read", k - 2))
                    bank = A[:, w.slot("a_full", k, 2), :]
                    for i in range(n):
                        o = bank[:, i * keys:(i + 1) * keys]
                        ins = nc.tensor.matmul(o, q_st[s][0:SC_ROWS, h0 + i, r * P:(r + 1) * P],
                                               k_st[s][0:SC_ROWS, h0 + i, 0:keys], start=True, stop=l != CAUSAL)
                        if l == CAUSAL:
                            ins = nc.tensor.matmul(o[:, keys - P:keys], identb[:, :], cqk_b[:, :], start=False, stop=True)
                    ins.then_inc(sems["a_full"], 1)

                def scores_turned(s, l, hh, k):
                    pe.wait_ge(sems["b_read"], w.at("b_read", k - 2))
                    bank = B[:, w.slot("b_full", k, 2), :]
                    for t in range(RT):
                        q0 = P * t if l == CAUSAL else 0
                        o = bank[:, t * ROWS:t * ROWS + ROWS - q0]
                        ins = nc.tensor.matmul(o, k_st[s][0:SCT_ROWS, hh, t * P:(t + 1) * P],
                                               q_st[s][0:SCT_ROWS, hh, q0:ROWS], start=True, stop=l != CAUSAL)
                        if l == CAUSAL:
                            ins = nc.tensor.matmul(o[:, 0:P], identb[:, :], ckq_b[:, :], start=False, stop=True)
                    ins.then_inc(sems["b_full"], 1)

                def weigh(s, l, g, t):
                    if t == 0:
                        pe.wait_ge(sems["b_read"], w.at_step("b_read", 2, "attend", s, l, 2 * g + 1))
                        if g == 2:
                            pe.wait_ge(sems[f"c_read{s}"], w.at_step(f"c_read{s}", 1, "attend", s, l, 5))
                    q0 = P * t if l == CAUSAL else 0
                    for j in range(4):
                        hh = 4 * g + j
                        ins = nc.tensor.matmul(C[VW * j:VW * (j + 1), s, g % 2, q0:ROWS], v_aug[s][:, t, hh, :],
                                               probs[s][:, hh % NPR, t * ROWS:t * ROWS + ROWS - q0],
                                               start=t == 0, stop=t == RT - 1, tile_position=(0, VW * j))
                    if t == RT - 1:
                        ins.then_inc(sems[f"pv_done{s}"], 1)

                for w.i, (step, s, l, part) in enumerate(SCHEDULE):
                    if step == "keys":
                        if l == 0:
                            pe.wait_ge(sems[f"ctx_loaded{s}"], w.at_step(f"ctx_loaded{s}", 16, "load", s, 0, 0))
                        pe.wait_ge(sems["dv_read"], w.at("dv_read", 0))
                        nc.tensor.matmul(DV[:, 0:ROWS], attn_sb[:, l, 1, :], cT[s][:, :], start=True, stop=True)\
                            .then_inc(sems["dv_full"], 1)
                        pe.wait_ge(sems["dv_read"], w.at("dv_read", 1))
                        rows_product(DV, cT[s], attn_sb[:, l, 2, :]).then_inc(sems["dv_full"], 1)
                    if step == "key_mean":
                        pe.wait_ge(sems["dv_read"], w.at("dv_read", 0))
                        rows_product(DV, cT[s], attn_sb[:, l, 1, :]).then_inc(sems["dv_full"], 1)
                        pe.wait_ge(sems["rows_ready"], w.at("rows_ready", 2))
                        pe.wait_ge(sems["dv_read"], w.at("dv_read", 1))
                        for t in range(RT):
                            ins = nc.tensor.matmul(DV[:, 0:D], mean_k[:, :], work_rows[1][s][:, t, :],
                                                   start=t == 0, stop=t == RT - 1)
                        ins.then_inc(sems["dv_full"], 1)
                    if step == "turn":
                        if l < 2 * LAYERS - 1:
                            pe.wait_ge(sems[f"h_ready{s}"], w.at_step(f"h_ready{s}", 1, "norm", s, l, 0))
                        else:
                            pe.wait_ge(sems["xd_ready"], w.at_step("xd_ready", 1, "quantise", s, 3, 1))
                        turn_rows(1, h[s])
                    if step == "query":
                        pe.wait_ge(sems["ac_read"], w.at_step("ac_read", 1, "turn", s, l, 0))
                        pe.wait_ge(sems["dv_read"], w.at("dv_read", 0))
                        nc.tensor.matmul(DV[:, 0:ROWS], attn_sb[:, l, 0, :], hT[s][:, :], start=True, stop=True)\
                            .then_inc(sems["dv_full"], 1)
                    if step == "query_rows":
                        pe.wait_ge(sems["dv_read"], w.at("dv_read", 0))
                        rows_product(DV, hT[s], attn_sb[:, l, 0, :]).then_inc(sems["dv_full"], 1)
                    if step == "query_means":
                        pe.wait_ge(sems["rows_ready"], w.at_step("rows_ready", 2, "query_rows", s, l, 0))
                        pe.wait_ge(sems["ac_read"], w.at("ac_read", 0))
                        for r in range(RT):
                            ins = nc.tensor.transpose(AC[0:HEADS, r * P:(r + 1) * P],
                                                      rn[s][:, r * HEADS:(r + 1) * HEADS], ident[:, :])
                        ins.then_inc(sems["ac_full"], 1)
                    if step == "chosen":
                        pe.wait_ge(sems["sel_ready"], w.at_step("sel_ready", 1, "choose", s, l, 1))
                        pe.wait_ge(sems["dv_read"], w.at("dv_read", 0))
                        for r in range(RT):
                            ins = nc.tensor.matmul(DV[:, r * HEADS:(r + 1) * HEADS], selT[s][:, r * P:(r + 1) * P],
                                                   ident[0:HEADS, 0:HEADS], start=True, stop=True)
                        ins.then_inc(sems["dv_full"], 1)
                    if step == "maxima":
                        if part == 0:
                            pe.wait_ge(sems[f"q_moved{s}"], w.at_step(f"q_moved{s}", 16 * TERMS, "query", s, l, 0))
                            pe.wait_ge(sems[f"k_moved{s}"], w.at_step(f"k_moved{s}", 16 * TERMS, "keys", s, l, 0))
                        for k, tile in enumerate(max_tiles(l, part), 1):
                            scores(s, l, k, *tile)
                    if step == "max_turn":
                        pe.wait_ge(sems["m_parts_done"], w.at_step("m_parts_done", 1, "max_parts", s, l, part))
                        pe.wait_ge(sems["ac_read"], w.at("ac_read", 0))
                        for r in range(RT):
                            ins = nc.tensor.transpose(AC[:, :].bitcast(BF16)[:, r * P:(r + 1) * P],
                                                      m_parts[s][:, part, r, :], identb[:, :])
                        ins.then_inc(sems["ac_full"], 1)
                    if step == "attend":
                        if part == 0:
                            pe.wait_ge(sems["dv_read"], w.at_step("dv_read", 2, "keys", s, l, 0))
                        if part in (0, 4):
                            pe.wait_ge(sems[f"m_moved{s}"], w.at_step(f"m_moved{s}", 16, "max_turn", s, l, part // 4))
                        if part < HEADS // 2:
                            scores_turned(s, l, 2 * part, 1)
                            scores_turned(s, l, 2 * part + 1, 2)
                        if part > 1:
                            weigh(s, l, (part - 2) // 2, part % 2)
                    if step == "heads":
                        pe.wait_ge(sems[f"c_read{s}"], w.at_step(f"c_read{s}", 1, "attend", s, l, ATT_STEPS - 1))
                        for r in range(RT):
                            pe.wait_ge(sems["a_read"], w.at("a_read", r + 1 - 2))
                            for g in range(4):
                                ins = nc.tensor.transpose(A[:, w.slot("a_full", r + 1, 2), g * P:(g + 1) * P],
                                                          raw[s][:, g, r * P:(r + 1) * P], ident[:, :])
                            ins.then_inc(sems["a_full"], 1)
                    if step == "heads_turn":
                        pe.wait_ge(sems["a_read"], w.at_step("a_read", RT, "heads", s, l, 0))
                        turn_rows(1, heads_out[s])
                    if step == "project":
                        pe.wait_ge(sems["ac_read"], w.at_step("ac_read", 1, "heads_turn", s, l, 0))
                        pe.wait_ge(sems["dv_read"], w.at("dv_read", 0))
                        rows_product(DV, coT[s], attn_sb[:, l, 3, :]).then_inc(sems["dv_full"], 1)
                    if step == "route0":
                        pe.wait_ge(ffn_loaded, 16 * len(ffn_loads))
                        pe.wait_ge(sems["ac_read"], w.at_step("ac_read", 1, "turn", s, LAYERS, 0))
                        pe.wait_ge(sems["dv_read"], w.at("dv_read", 0))
                        nc.tensor.matmul(DV[:, 0:ROWS], r0_bc[:, :], hT[s][:, :], start=True, stop=True)\
                            .then_inc(sems["dv_full"], 1)
                        pe.wait_ge(sems["ac_read"], w.at("ac_read", 0))
                        rows_product(AC, hT[s], blk0[:, :]).then_inc(sems["ac_full"], 1)
                    if step == "logits":
                        if l == 2:
                            pe.wait_ge(big_loaded, 16 * len(big_loads))
                        pe.wait_ge(sems["ac_read"], w.at_step("ac_read", 1, "turn", s, l + LAYERS, 0))
                        pe.wait_ge(sems["dv_read"], w.at("dv_read", 0))
                        rows_product(DV, hT[s], (r1_sb if l == 1 else r2_sb)[:, :]).then_inc(sems["dv_full"], 1)
                    if step == "hidden" and l == 1:
                        pe.wait_ge(sems["a_read"], w.at("a_read", 1 - 2))
                        for a in range(2):
                            ins = nc.tensor.matmul(A[:, w.slot("a_full", 1, 2), a * ROWS:(a + 1) * ROWS],
                                                   fc1_sb[:, part, a, :], hT[s][:, :], start=True, stop=True)
                        ins.then_inc(sems["a_full"], 1)
                    if step == "output" and l == 1 and part != EXPERTS:
                        chunks = [part] if part < EXPERTS else [part - 1, part]
                        pe.wait_ge(sems["a_read"], w.at_step("a_read", 1, "hidden", s, 1, part))
                        pe.wait_ge(sems["a_read"], w.at("a_read", 1 - 2))
                        for r in range(RT):
                            for c in chunks:
                                ins = nc.tensor.matmul(A[:, w.slot("a_full", 1, 2), r * D:(r + 1) * D],
                                                       acts[s][:, c % NACT, r * P:(r + 1) * P], fc2_sb[:, c, :],
                                                       start=c == chunks[0], stop=c == chunks[-1])
                        ins.then_inc(sems["a_full"], 1)
                    if step == "comb_turn":
                        pe.wait_ge(sems["comb_ready"], w.at_step("comb_ready", 1, "combine", s, 2, 0))
                        pe.wait_ge(sems["ac_read"], w.at("ac_read", 0))
                        for r in range(RT):
                            ins = nc.tensor.transpose(AC[0:EXPERTS + 1, r * P:(r + 1) * P], comb[s][:, r, :], ident[:, :])
                        ins.then_inc(sems["ac_full"], 1)
                    if step == "out_bias":
                        pe.wait_ge(sems["ac_read"], w.at_step("ac_read", 1, "comb_turn", s, 2, 0))
                        pe.wait_ge(sems["a_read"], w.at("a_read", 1 - 2))
                        rows_product(A[:, w.slot("a_full", 1, 2), :], combT[s], b2_sb[:, :]).then_inc(sems["a_full"], 1)
                    if step == "hidden" and l == 2:
                        for half in range(2):
                            pe.wait_ge(sems["b_read"], w.at("b_read", half + 1 - 2))
                            for j in range(2):
                                ins = nc.tensor.matmul(B[:, w.slot("b_full", half + 1, 2), j * ROWS:(j + 1) * ROWS],
                                                       w1_sb[:, part, 2 * half + j, :], hT[s][:, :], start=True, stop=True)
                            ins.then_inc(sems["b_full"], 1)
                    if step == "output" and l == 2:
                        pe.wait_ge(sems["b_read"], w.at_step("b_read", 2, "hidden", s, 2, part))
                        pe.wait_ge(sems["a_read"], w.at("a_read", 1 - 2))
                        for r in range(RT):
                            for c in range(HC):
                                ins = nc.tensor.matmul(A[:, w.slot("a_full", 1, 2), r * D:(r + 1) * D],
                                                       hid[s][:, part % NACT, c, r * P:(r + 1) * P],
                                                       w2_sb[:, part, c, :], start=c == 0, stop=c == HC - 1)
                        ins.then_inc(sems["a_full"], 1)
                    if step == "affine3":
                        pe.wait_ge(sems["ac_read"], w.at_step("ac_read", 1, "turn", s, 2 * LAYERS - 1, 0))
                        pe.wait_ge(sems["dv_read"], w.at("dv_read", 0))
                        rows_product(DV, hT[s], w3T[:, :]).then_inc(sems["dv_full"], 1)

        @block.vector
        def _(dve):
            for name in ("a_read", "dv_read"):
                dve.sem_inc(sems[name], CREDIT[name])
            nc.vector.memset(mhalf[:, :], -0.5)
            nc.vector.memset(mean_k[:, :], 1.0 / ROWS)
            for s in range(STREAMS):
                nc.vector.memset(q_st[s][:, :, :].bitcast(F32), 0.0)
                nc.vector.memset(k_st[s][0:MAX_ROW, :, :].bitcast(F32), 0.0)
                nc.vector.memset(m_parts[s][:, :, :, :], 0.0)
                nc.vector.memset(k_st[s][MAX_ROW:SCT_ROWS, :, :], 1.0)
                nc.vector.memset(v_aug[s][:, :, :, HD:VW], 1.0)
                nc.vector.memset(work[s][:, 0:SENT], BIG)
            setup_count = iter(range(1, 100))

            def next_setup():
                return next(setup_count)

            def blocks(ap):
                return ap.rearrange("p t (b i) -> p (t b) i", b=4)

            def per_block(ap, rows):
                return ap.unsqueeze(2).broadcast_to([P, 4 * rows, D // 4])

            def fp6_scales(done, after, s, rows, src):
                y, a, m2, inv = (wr[s][:, 0:rows, :] for wr in work_rows)
                amx, scale, rscale = (t[s][:, 0:4 * rows] for t in (amax, sc3, rsc3))

                nc.vector.tensor_reduce(amx, blocks(src), AX.X, ALU.max, apply_absolute_value=True).then_inc(done, 1)
                dve.wait_ge(done, after())
                nc.vector.tensor_scalar(scale, amx, 1.0 / FP6_MAX, 1e-30, ALU.mult, ALU.max).then_inc(done, 1)
                dve.wait_ge(done, after())
                nc.vector.reciprocal(rscale, scale).then_inc(done, 1)
                dve.wait_ge(done, after())
                nc.vector.tensor_tensor(blocks(y), blocks(src), per_block(rscale, rows), ALU.mult).then_inc(done, 1)
                dve.wait_ge(done, after())
                nc.vector.tensor_tensor(a, y, y, ALU.mult).then_inc(done, 1)
                dve.wait_ge(done, after())

            def fp6_values(done, after, s, rows, dst):
                y, a, m2, inv = (wr[s][:, 0:rows, :] for wr in work_rows)
                nc.vector.tensor_scalar(m2, a, 4.0, -4.0, ALU.is_ge, ALU.mult).then_inc(done, 1)
                dve.wait_ge(done, after())
                nc.vector.tensor_scalar(inv, a, 16.0, -2.0, ALU.is_ge, ALU.mult).then_inc(done, 1)
                dve.wait_ge(done, after())
                nc.vector.scalar_tensor_tensor(inv, m2, 8.0, inv, ALU.add, ALU.add).then_inc(done, 1)
                dve.wait_ge(done, after())
                nc.vector.tensor_tensor(y, y, inv, ALU.mult).then_inc(done, 1)
                dve.wait_ge(done, after())
                nc.vector.tensor_scalar(a, y, MAGIC, MAGIC, ALU.add, ALU.subtract).then_inc(done, 1)
                dve.wait_ge(done, after())
                nc.vector.tensor_tensor(y, a, y, ALU.subtract).then_inc(done, 1)
                dve.wait_ge(done, after())
                nc.vector.scalar_tensor_tensor(a, y, 0.5, a, ALU.is_ge, ALU.subtract).then_inc(done, 1)
                dve.wait_ge(done, after())
                nc.vector.reciprocal(m2, inv).then_inc(done, 1)
                dve.wait_ge(done, after())
                nc.vector.scalar_tensor_tensor(y, a, -1.0, m2, ALU.mult, ALU.mult).then_inc(done, 1)
                dve.wait_ge(done, after())
                return nc.vector.tensor_tensor(blocks(dst), blocks(y), per_block(sc3[s][:, 0:4 * rows], rows), ALU.mult)

            dve.wait_ge(attn_loaded, 16 * len(attention_loads))
            nc.vector.tensor_copy(identb[:, :], ident[:, :])
            nc.vector.tensor_copy(cqk_b[:, :], cqk[:, :])
            nc.vector.tensor_copy(ckq_b[:, :], ckq[:, :])
            nc.vector.tensor_copy(r0_bc[:, :], r0_sb[:, :].broadcast_to([P, P])).then_inc(setup_step, 1)
            dve.wait_ge(setup_step, next_setup())
            dve.wait_ge(gates_done, 1)
            nc.vector.tensor_scalar(tgh[:, :], tg[:, :], 0.5, None, ALU.mult)
            for l in range(LAYERS):
                nc.vector.tensor_scalar(gbo[:, l, :], brow[:, R_BO + l * D:R_BO + (l + 1) * D], tg[:, l:l + 1], None,
                                        ALU.mult)
            for s in range(STREAMS):
                nc.vector.tensor_copy(comb[s][:, :, EXPERTS],
                                      tg[:, LAYERS + 2:LAYERS + 3].broadcast_to([P, RT]))
            nc.vector.tensor_scalar(gbo[:, LAYERS, :], brow[:, R_BF3:R_BF3 + D],
                                               tg[:, 2 * LAYERS - 1:2 * LAYERS], None, ALU.mult).then_inc(setup_step, 1)
            dve.wait_ge(setup_step, next_setup())
            fp6_scales(setup_step, next_setup, 0, 1, w3_sb[:, :].unsqueeze(1))
            fp6_values(setup_step, next_setup, 0, 1, work_rows[0][0][:, 0:1, :]).then_inc(w3_quantised, 1)
            dve.wait_ge(w3_copied, 1)
            nc.vector.memset(junk[:, :], 0.0).then_inc(setup_done, 1)

            with dve.Fori(0, PAIRS) as turn:
                w = Walk(turn, "dve_step")

                STATS, LOGITS, CHOICE = range(3)

                def pause(s, kind):
                    nc.vector.memset(idle[:, s, kind:kind + 1], 0.0)

                def split(s, l, parts, b, name):
                    dve.wait_ge(sems[f"hi_ready{s}"], w.at(f"hi_ready{s}", 1))
                    nc.vector.scalar_tensor_tensor(resid[s][:, :], DV[:, 0:ROWS], bcol[:, l, b:b + 1],
                                                   parts[s][:, 0, :], ALU.add, ALU.subtract)\
                        .then_inc(sems["dv_read"], 1)
                    dve.wait_ge(sems["dv_read"], w.at("dv_read", 1))
                    nc.vector.tensor_copy(parts[s][:, 1, :], resid[s][:, :]).then_inc(sems[f"{name}_split{s}"], 1)
                    dve.wait_ge(sems[f"{name}_split{s}"], w.at(f"{name}_split{s}", 1))
                    nc.vector.tensor_tensor(parts[s][:, 2, :], resid[s][:, :], parts[s][:, 1, :], ALU.subtract)\
                        .then_inc(sems[f"{name}_split{s}"], 1)

                def rows_norms(s, k, bias):
                    dve.wait_ge(sems["dv_full"], w.at("dv_full", k))
                    nc.vector.tensor_tensor(work_rows[0][s][:, :, :],
                                            DV[:, 0:RT * D].rearrange("p (h t d) -> p t h d", t=RT, h=1).rearrange("p t h d -> p t (h d)"),
                                            bias, ALU.add).then_inc(sems["dv_read"], 1)
                    dve.wait_ge(sems["dv_read"], w.at("dv_read", k))
                    nc.vector.tensor_tensor(work_rows[1][s][:, :, :], work_rows[0][s][:, :, :],
                                                 work_rows[0][s][:, :, :], ALU.mult).then_inc(sems["dve_step"], 1)
                    dve.wait_ge(sems["dve_step"], w.step())
                    head_sums(ss[s], work_rows[1][s]).then_inc(sems["rows_ready"], 1)

                def head_sums(dst, src):
                    return nc.vector.tensor_reduce(dst[:, :].rearrange("p (t h) -> p t h", t=RT),
                                                   src[:, :, :].rearrange("p t (d h) -> p t h d", d=HD), AX.X, ALU.add)

                def by_head(ap):
                    return ap.rearrange("p (t h) -> p t h", t=RT).unsqueeze(2).broadcast_to([P, RT, HD, HEADS])

                def over_tiles(ap, n):
                    return ap.unsqueeze(1).broadcast_to([P, RT, n])

                def combine_logits(s, l):
                    dve.wait_ge(sems["dv_full"], w.at("dv_full", 1))
                    logits = DV[:, 0:RT * EXPERTS].rearrange("p (t e) -> p t e", t=RT)
                    if l == 2:
                        ins = nc.vector.tensor_tensor(lg[s][:, :, :], logits,
                                                      over_tiles(brow[:, R_GB:R_GB + EXPERTS], EXPERTS), ALU.add)
                    else:
                        ins = nc.vector.tensor_copy(lg[s][:, :, :], logits)
                    ins.then_inc(sems["dv_read"], 1)
                    dve.wait_ge(sems["dv_read"], w.at("dv_read", 1))
                    pause(s, LOGITS)
                    nc.vector.max(top[s][:, 0, :], lg[s][:, 0, :])
                    nc.vector.max(top[s][:, 1, :], lg[s][:, 1, :]).then_inc(sems["dve_step"], 1)
                    dve.wait_ge(sems["dve_step"], w.step())
                    nc.vector.tensor_tensor(col[s][:, 0, :], top[s][:, :, 1], top[s][:, :, 0], ALU.subtract)\
                        .then_inc(sems["gap_ready"], 1)
                    nc.vector.max_index(topi[s][:, 0, :], top[s][:, 0, :], lg[s][:, 0, :])
                    nc.vector.max_index(topi[s][:, 1, :], top[s][:, 1, :], lg[s][:, 1, :]).then_inc(sems["dve_step"], 1)
                    dve.wait_ge(sems["dve_step"], w.step())
                    nc.vector.tensor_copy(topf[s][:, :, :], topi[s][:, :, 0:2]).then_inc(sems["dve_step"], 1)
                    dve.wait_ge(sems["dve_step"], w.step())

                def combine(s, l):
                    gate = (tgh if l == 1 else tg)[:, LAYERS + l:LAYERS + l + 1]
                    dve.wait_ge(sems["gap_exp"], w.at_step("gap_exp", 1, "logits", s, l, 0))
                    nc.vector.tensor_scalar(col[s][:, 2, :], col[s][:, 1, :], 1.0, None, ALU.add)\
                        .then_inc(sems["dve_step"], 1)
                    dve.wait_ge(sems["dve_step"], w.step())
                    nc.vector.reciprocal(col[s][:, 3, :], col[s][:, 2, :]).then_inc(sems["dve_step"], 1)
                    dve.wait_ge(sems["dve_step"], w.step())
                    nc.vector.scalar_tensor_tensor(col[s][:, 5, :], col[s][:, 1, :], gate, col[s][:, 3, :],
                                                   ALU.mult, ALU.mult)
                    nc.vector.tensor_scalar(col[s][:, 4, :], col[s][:, 3, :], gate, None, ALU.mult)\
                        .then_inc(sems["dve_step"], 1)
                    dve.wait_ge(sems["dve_step"], w.step())
                    for r in range(RT):
                        nc.vector.tensor_scalar(comb[s][:, r, 0:EXPERTS], iota[:, :], topf[s][:, r, 0:1],
                                                col[s][:, 4, r:r + 1], ALU.is_equal, ALU.mult)
                        ins = nc.vector.tensor_scalar(cmb2[s][:, r, :], iota[:, :], topf[s][:, r, 1:2],
                                                      col[s][:, 5, r:r + 1], ALU.is_equal, ALU.mult)
                    ins.then_inc(sems["dve_step"], 1)
                    dve.wait_ge(sems["dve_step"], w.step())
                    nc.vector.tensor_tensor(comb[s][:, :, 0:EXPERTS], comb[s][:, :, 0:EXPERTS], cmb2[s][:, :, :],
                                            ALU.add).then_inc(sems["comb_ready"], 1)
                    dve.wait_ge(sems["comb_ready"], w.at("comb_ready", 1))

                def accumulate(s, k, scale):
                    dve.wait_ge(sems["a_full"], w.at("a_full", k))
                    for r in range(RT):
                        ins = nc.vector.scalar_tensor_tensor(xs[s][:, r, :], A[:, w.slot("a_full", k, 2), r * D:(r + 1) * D],
                                                             scale(r), xs[s][:, r, :], ALU.mult, ALU.add)
                    ins.then_inc(sems["a_read"], 1)
                    dve.wait_ge(sems["a_read"], w.at("a_read", k))

                for w.i, (step, s, l, part) in enumerate(SCHEDULE):
                    if step == "keys":
                        dve.wait_ge(sems["dv_full"], w.at("dv_full", 1))
                        split(s, l, k_parts, 1, "k")
                        dve.wait_ge(sems["dv_full"], w.at("dv_full", 2))
                        bv = over_tiles(brow[:, R_BV + l * D:R_BV + (l + 1) * D], D).rearrange("p t (h d) -> p t h d", d=HD)
                        nc.vector.tensor_tensor(v_aug[s][:, :, :, 0:HD],
                                                DV[:, 0:RT * D].rearrange("p (t h d) -> p t h d", t=RT, d=HD), bv,
                                                ALU.add).then_inc(sems["dv_read"], 1)
                    if step == "key_mean":
                        rows_norms(s, 1, over_tiles(brow[:, R_BK3:R_BK3 + D], D))
                        dve.wait_ge(sems["rn_ready"], w.at("rn_ready", 1))
                        nc.vector.tensor_tensor(work_rows[1][s][:, :, :].rearrange("p t (d h) -> p t d h", d=HD),
                                                work_rows[0][s][:, :, :].rearrange("p t (d h) -> p t d h", d=HD),
                                                by_head(rn[s][:, :]), ALU.mult).then_inc(sems["rows_ready"], 1)
                        dve.wait_ge(sems["dv_full"], w.at("dv_full", 2))
                        nc.vector.tensor_copy(kbar[s][:, :], DV[:, 0:D]).then_inc(sems["dv_read"], 1)
                    if step == "stats":
                        if l == 0:
                            dve.wait_ge(sems[f"x_loaded{s}"], w.at_step(f"x_loaded{s}", 16, "load", s, 0, 0))
                        for r in range(RT):
                            ins = nc.vector.bn_stats(stats[s][:, r, :], xs[s][:, r, :])
                        ins.then_inc(sems["dve_step"], 1)
                        dve.wait_ge(sems["dve_step"], w.step())
                        pause(s, STATS)
                        nc.vector.bn_aggr(mv[s][:, 0, :], stats[s][:, 0, :])
                        nc.vector.bn_aggr(mv[s][:, 1, :], stats[s][:, 1, :]).then_inc(sems["dve_step"], 1)
                        dve.wait_ge(sems["dve_step"], w.step())
                        nc.vector.tensor_scalar(veps[s][:, :], mv[s][:, :, 1], 1e-5, None, ALU.add)\
                            .then_inc(sems["var_ready"], 1)
                    if step == "norm":
                        dve.wait_ge(sems["rstd_ready"], w.at_step("rstd_ready", 1, "stats", s, l, 0))
                        for r in range(RT):
                            ins = nc.vector.tensor_scalar(h[s][:, r, :], xs[s][:, r, :], mv[s][:, r, 0:1],
                                                          rstd[s][:, r:r + 1], ALU.subtract, ALU.mult)
                        ins.then_inc(sems[f"h_ready{s}"], 1)
                    if step == "query":
                        dve.wait_ge(sems["dv_full"], w.at("dv_full", 1))
                        split(s, l, q_parts, 0, "q")
                    if step == "query_rows":
                        rows_norms(s, 1, over_tiles(brow[:, R_BQ3:R_BQ3 + D], D))
                        dve.wait_ge(sems["rows_ready"], w.at("rows_ready", 1))
                        nc.vector.tensor_tensor(work_rows[1][s][:, :, :], work_rows[0][s][:, :, :],
                                                over_tiles(kbar[s][:, :], D), ALU.mult).then_inc(sems["dve_step"], 1)
                        dve.wait_ge(sems["dve_step"], w.step())
                        head_sums(dot[s], work_rows[1][s]).then_inc(sems["dve_step"], 1)
                        dve.wait_ge(sems["dve_step"], w.step())
                        dve.wait_ge(sems["rn_ready"], w.at("rn_ready", 1))
                        nc.vector.tensor_tensor(rn[s][:, :], rn[s][:, :], dot[s][:, :], ALU.mult)\
                            .then_inc(sems["rows_ready"], 1)
                    if step == "choose":
                        dve.wait_ge(sems["ac_read"], w.at_step("ac_read", 1, "query_means", s, l, 0))
                        for _ in range(4 * part, 4 if part == 0 else ROUNDS):
                            pause(s, CHOICE)
                            nc.vector.max(top8q[s][:, :], work[s][:, :]).then_inc(sems["dve_step"], 1)
                            dve.wait_ge(sems["dve_step"], w.step())
                            pause(s, CHOICE)
                            nc.vector.match_replace(work[s][:, :], top8q[s][:, :], work[s][:, :], -BIG)\
                                .then_inc(sems["dve_step"], 1)
                            dve.wait_ge(sems["dve_step"], w.step())
                        if part == 1:
                            nc.vector.tensor_scalar(selT[s][:, :], work[s][:, SENT:SENT + ROWS], -0.5 * BIG, None,
                                                    ALU.is_le).then_inc(sems["sel_ready"], 1)
                            dve.wait_ge(sems["sel_ready"], w.at("sel_ready", 1))
                            nc.vector.memset(work[s][:, 0:SENT], BIG).then_inc(sems["dve_step"], 1)
                            dve.wait_ge(sems["dve_step"], w.step())
                    if step == "chosen":
                        dve.wait_ge(sems["dv_full"], w.at("dv_full", 1))
                        nc.vector.tensor_copy(selm[s][:, :, :].rearrange("p t h -> p (t h)"), DV[:, 0:RT * HEADS])\
                            .then_inc(sems["dv_read"], 1)
                    if step == "maxima":
                        for k, (r, keys, h0, n) in enumerate(max_tiles(l, part), 1):
                            dve.wait_ge(sems["a_full"], w.at("a_full", k))
                            nc.vector.tensor_reduce(mx[s][:, r, h0:h0 + n],
                                                    A[:, w.slot("a_full", k, 2), :].rearrange("p (n k) -> p n k", n=n),
                                                    AX.X, ALU.max).then_inc(sems["a_read"], 1)
                    if step == "max_parts":
                        last = (part + 1) * MAX_STEPS // 2 - 1
                        dve.wait_ge(sems["a_read"], w.at_step("a_read", len(max_tiles(l, last)), "maxima", s, l, last))
                        half = slice(part * HEADS // 2, (part + 1) * HEADS // 2)
                        first, second, third = (m_parts[s][:, part, :, i * HEADS // 2:(i + 1) * HEADS // 2] for i in range(3))
                        nc.vector.tensor_scalar(first, mx[s][:, :, half], -1.0, None, ALU.mult)\
                            .then_inc(sems["dve_step"], 1)
                        dve.wait_ge(sems["dve_step"], w.step())
                        nc.vector.scalar_tensor_tensor(mres[s][:, :, half], mx[s][:, :, half], -1.0, first,
                                                       ALU.mult, ALU.subtract).then_inc(sems["dve_step"], 1)
                        dve.wait_ge(sems["dve_step"], w.step())
                        nc.vector.tensor_copy(second, mres[s][:, :, half]).then_inc(sems["dve_step"], 1)
                        dve.wait_ge(sems["dve_step"], w.step())
                        nc.vector.tensor_tensor(third, mres[s][:, :, half], second, ALU.subtract)\
                            .then_inc(sems["m_parts_done"], 1)
                    if step == "heads":
                        for r in range(RT):
                            dve.wait_ge(sems["a_full"], w.at("a_full", r + 1))
                            bank = A[:, w.slot("a_full", r + 1, 2), :].rearrange("p (h v) -> p h v", v=VW)
                            nc.vector.reciprocal(rden[s][:, r, :], bank[:, :, HD]).then_inc(sems["dve_step"], 1)
                            dve.wait_ge(sems["dve_step"], w.step())
                            if l == SPARSE:
                                if r == 0:
                                    dve.wait_ge(sems["dv_read"], w.at_step("dv_read", 1, "chosen", s, l, 0))
                                nc.vector.tensor_tensor(rden[s][:, r, :], rden[s][:, r, :], selm[s][:, r, :], ALU.mult)\
                                    .then_inc(sems["dve_step"], 1)
                                dve.wait_ge(sems["dve_step"], w.step())
                            nc.vector.tensor_tensor(heads_out[s][:, r, :].rearrange("p (h d) -> p h d", d=HD),
                                                    bank[:, :, 0:HD],
                                                    rden[s][:, r, :].unsqueeze(2).broadcast_to([P, HEADS, HD]),
                                                    ALU.mult).then_inc(sems["a_read"], 1)
                    if step in ("project", "affine3"):
                        dve.wait_ge(sems["dv_full"], w.at("dv_full", 1))
                        n = l if step == "project" else 2 * LAYERS - 1
                        dve.wait_ge(sems["xb_ready"], w.at_step("xb_ready", 1, "norm", s, n, 0))
                        nc.vector.scalar_tensor_tensor(xs[s][:, :, :].rearrange("p t d -> p (t d)"), DV[:, 0:RT * D],
                                                       tg[:, n:n + 1], xs[s][:, :, :].rearrange("p t d -> p (t d)"),
                                                       ALU.mult, ALU.add).then_inc(sems["dv_read"], 1)
                        dve.wait_ge(sems["dv_read"], w.at("dv_read", 1))
                    if step == "route0":
                        dve.wait_ge(sems["dv_full"], w.at("dv_full", 1))
                        for r in range(RT):
                            nc.vector.scalar_tensor_tensor(junk[:, 0:P], DV[:, r * P:(r + 1) * P], 1.0, ident[:, :],
                                                           ALU.mult, ALU.mult, accum_out=col[s][:, 0, r:r + 1])\
                                .then_inc(sems["dve_step"], 1)
                            dve.wait_ge(sems["dve_step"], w.step())
                            nc.vector.tensor_scalar(junk[:, :], DV[:, 0:ROWS], col[s][:, 0, r:r + 1], None,
                                                    ALU.is_gt, ALU.add, accum_out=col[s][:, 1, r:r + 1])\
                                .then_inc(sems["dve_step"], 1)
                            dve.wait_ge(sems["dve_step"], w.step())
                            ins = nc.vector.scalar_tensor_tensor(junk[:, :], DV[:, 0:ROWS], col[s][:, 0, r:r + 1],
                                                                 before[:, r, :], ALU.is_equal, ALU.mult,
                                                                 accum_out=col[s][:, 2, r:r + 1])
                            if r == 0:
                                ins.then_inc(sems["dve_step"], 1)
                                dve.wait_ge(sems["dve_step"], w.step())
                        ins.then_inc(sems["dv_read"], 1)
                        dve.wait_ge(sems["dv_read"], w.at("dv_read", 1))
                        nc.vector.tensor_tensor(col[s][:, 3, :], col[s][:, 1, :], col[s][:, 2, :], ALU.add)\
                            .then_inc(sems["dve_step"], 1)
                        dve.wait_ge(sems["dve_step"], w.step())
                        nc.vector.tensor_scalar(col[s][:, 4, :], col[s][:, 3, :], KEEP0 - 0.5, 0.5, ALU.is_lt, ALU.mult)
                        nc.vector.tensor_scalar(col[s][:, 5, :], col[s][:, 3, :], KEEP0 - 0.5, None, ALU.is_gt)\
                            .then_inc(sems["dve_step"], 1)
                        dve.wait_ge(sems["dve_step"], w.step())
                    if step == "gelu0":
                        z, u = ffo[s][:, :, :], work_rows[0][s][:, :, :]
                        dve.wait_ge(sems["ac_read"], w.at_step("ac_read", 1, "route0", s, l, 0))
                        nc.vector.tensor_tensor(u, z, z, ALU.mult).then_inc(sems["dve_step"], 1)
                        dve.wait_ge(sems["dve_step"], w.step())
                        nc.vector.tensor_scalar(u, u, CUBIC, 1.0, ALU.mult, ALU.add).then_inc(sems["dve_step"], 1)
                        dve.wait_ge(sems["dve_step"], w.step())
                        nc.vector.tensor_tensor(u, u, z, ALU.mult).then_inc(sems["cubic_ready"], 1)
                    if step == "blend0":
                        z, t = ffo[s][:, :, :], work_rows[1][s][:, :, :]
                        dve.wait_ge(sems["tanh_ready"], w.at_step("tanh_ready", 1, "gelu0", s, l, 0))
                        nc.vector.scalar_tensor_tensor(z, t, 1.0, z, ALU.add, ALU.mult)
                        for r in range(RT):
                            ins = nc.vector.tensor_scalar(h[s][:, r, :], h[s][:, r, :], col[s][:, 5, r:r + 1], None, ALU.mult)
                        ins.then_inc(sems["dve_step"], 1)
                        dve.wait_ge(sems["dve_step"], w.step())
                        for r in range(RT):
                            ins = nc.vector.scalar_tensor_tensor(h[s][:, r, :], ffo[s][:, r, :], col[s][:, 4, r:r + 1],
                                                                 h[s][:, r, :], ALU.mult, ALU.add)
                        ins.then_inc(sems["dve_step"], 1)
                        dve.wait_ge(sems["dve_step"], w.step())
                        nc.vector.scalar_tensor_tensor(xs[s][:, :, :], h[s][:, :, :], tg[:, LAYERS:LAYERS + 1],
                                                       xs[s][:, :, :], ALU.mult, ALU.add).then_inc(sems["x_done"], 1)
                        dve.wait_ge(sems["x_done"], w.at("x_done", 1))
                    if step == "logits":
                        combine_logits(s, l)
                    if step == "combine":
                        combine(s, l)
                    if step == "hidden" and l == 1:
                        i, bank = part % NACT, A[:, w.slot("a_full", 1, 2), :]
                        dve.wait_ge(sems["tanh_ready"], w.at("tanh_ready", 1))
                        nc.vector.scalar_tensor_tensor(tanhs[s][:, i, :], tanhs[s][:, i, :], 1.0, bank[:, 0:ROWS],
                                                       ALU.add, ALU.mult).then_inc(sems["dve_step"], 1)
                        dve.wait_ge(sems["dve_step"], w.step())
                        nc.vector.tensor_tensor(acts[s][:, i, :], tanhs[s][:, i, :], bank[:, ROWS:2 * ROWS], ALU.mult)\
                            .then_inc(sems["a_read"], 1)
                    if step == "output" and l == 1 and part < EXPERTS:
                        accumulate(s, 1, lambda r: comb[s][:, r, part:part + 1])
                    if step == "output" and l == 1 and part > EXPERTS:
                        accumulate(s, 1, lambda r: tgh[:, LAYERS + 1:LAYERS + 2])
                    if step == "out_bias":
                        dve.wait_ge(sems["a_full"], w.at("a_full", 1))
                        nc.vector.tensor_tensor(xs[s][:, :, :].rearrange("p t d -> p (t d)"),
                                                A[:, w.slot("a_full", 1, 2), 0:RT * D],
                                                xs[s][:, :, :].rearrange("p t d -> p (t d)"), ALU.add)\
                            .then_inc(sems["a_read"], 1)
                        dve.wait_ge(sems["a_read"], w.at("a_read", 1))
                    if step == "output" and l == 2:
                        accumulate(s, 1, lambda r: comb[s][:, r, part:part + 1])
                    if step == "quantise":
                        if part == 0:
                            dve.wait_ge(sems[f"h_ready{s}"], w.at_step(f"h_ready{s}", 1, "norm", s, 2 * LAYERS - 1, 0))
                            fp6_scales(sems["dve_step"], w.step, s, RT, h[s][:, :, :])
                        else:
                            fp6_values(sems["dve_step"], w.step, s, RT, h[s][:, :, :]).then_inc(sems["xd_ready"], 1)
                assert w.links == LINKS["dve_step"], w.links

    return nc


def _arrays(i):
    import numpy as np

    f = np.float32

    def turned(w, by_feature):
        t = np.asarray(w).T
        return t.reshape(D, HEADS, HD).transpose(0, 2, 1).reshape(D, D) if by_feature else t

    def vec(name):
        return np.asarray(i[name]) if name in i else np.zeros(D, f)

    def dh(v):
        return v.reshape(HEADS, HD).T.reshape(D)

    attn_w = np.stack([np.stack([turned(i[f"L{l}_xattn_Wq"], True), turned(i[f"L{l}_xattn_Wk"], True),
                                 turned(i[f"L{l}_xattn_Wv"], False), turned(i[f"L{l}_xattn_Wo"], False)], axis=1)
                       for l in range(LAYERS)], axis=1)
    bias_cols = np.stack([np.stack([dh(vec(f"L{l}_xattn_bq")), dh(vec(f"L{l}_xattn_bk"))], axis=1)
                          for l in range(LAYERS)], axis=1)
    rows = [vec(f"L{l}_xattn_bv") for l in range(LAYERS)] + [vec(f"L{l}_xattn_bo") for l in range(LAYERS)]
    rows += [dh(vec("L3_xattn_bq")), dh(vec("L3_xattn_bk")), vec("L3_ffn_bias"), vec("L2_ffn_gate_b")]
    gate, up = (np.asarray(i[f"L1_ffn_{n}_w"]).reshape(D, 2, P) for n in ("gate", "up"))
    b1 = np.concatenate([i["L2_ffn_b1"], np.asarray(i["L2_ffn_bs1"])[None]])
    k, q = np.arange(P)[:, None], np.arange(P)[None, :]
    row = np.arange(ROWS).reshape(RT, P).T[:, :, None]
    return {
        "x": i["x"], "ctxT": np.asarray(i["ctx_1024"]).transpose(0, 2, 1),
        "attn_w": attn_w, "bias_cols": bias_cols, "bias_rows": np.concatenate(rows)[None],
        "g_all": np.concatenate([i["g_xattn"], i["g_ffn"]])[None],
        "router0": np.asarray(i["L0_ffn_w_router"])[:, None], "block0": i["L0_ffn_w_block"],
        "router1": i["L1_ffn_w_router"], "fc1": i["L1_ffn_fc1_w"], "fc2": i["L1_ffn_fc2_w"],
        "gate_up": np.stack([gate, up], axis=2), "down": i["L1_ffn_down_w"],
        "router2": i["L2_ffn_gate_w"], "w1": i["L2_ffn_w1"], "ws1": i["L2_ffn_ws1"],
        "b1_cols": b1.reshape(EXPERTS + 1, HC, P).transpose(2, 0, 1), "w2": i["L2_ffn_w2"],
        "ws2": i["L2_ffn_ws2"], "b2_all": np.concatenate([i["L2_ffn_b2"], np.asarray(i["L2_ffn_bs2"])[None]]),
        "w3": i["L3_ffn_weight"],
        "ident_in": np.eye(P, dtype=f), "causal_qk": np.where(q > k, f(-1e30), f(0)).astype(f),
        "causal_kq": np.where(k > q, f(-1e30), f(0)).astype(f),
        "before_in": (np.arange(ROWS)[None, None] < row).astype(f),
        "iota_in": np.broadcast_to(np.arange(EXPERTS, dtype=f), (P, EXPERTS)),
    }


def kernel(**inputs):
    import numpy as _np
    import concourse.bacc as _bacc
    from concourse import mybir as _mybir
    from concourse.bass_utils import run_bass_kernel_spmd as _run

    nc = _bacc.Bacc("TRN2", target_bir_lowering=False, num_devices=1)
    arrays, args = {}, {}
    for name, a in _arrays(inputs).items():
        a = _np.ascontiguousarray(a)
        arrays[f"in_{name}"] = a
        args[name] = nc.dram_tensor(f"in_{name}", a.shape, _mybir.dt.from_np(a.dtype), kind="ExternalInput").ap()
    out = nc.dram_tensor("out_x", (BATCHES, ROWS, D), F32, kind="ExternalOutput").ap()
    flamingo(nc, out=out, **args)
    r = _run(nc, [arrays], core_ids=[0])
    return r.results[0]["out_x"]
```

```python
from contextlib import ExitStack

import concourse.bass as bass
from concourse import mybir

F32 = mybir.dt.float32
BF16 = mybir.dt.bfloat16
U32 = mybir.dt.uint32
ALU = mybir.AluOpType
ACT = mybir.ActivationFunctionType
AX = mybir.AxisListType

P = 128
BATCHES, ROWS, D = 8, 256, 128
HEADS, HD = 16, 8
LAYERS = 4
STREAMS = 2
PAIRS = BATCHES // STREAMS
RT = ROWS // P
BANK = 512
Q_TERMS = (0, 0, 0, 1, 1, 2)
K_TERMS = (0, 1, 2, 0, 1, 0)
TERMS = len(Q_TERMS)
SC_ROWS = 96
MAX_ROW = 96
SCT_ROWS = 99
RING = 3
VW = 32
CAUSAL, SPARSE = 2, 3
KEEP0 = ROWS * 3 // 4
TOPQ = ROWS // 5
ROUNDS = -(-TOPQ // 8)
SENT = 8 * ROUNDS - TOPQ
BIG = 3.0e38
EXPERTS = 8
HID = 512
HC = HID // P
SQRT_HD = float(HD) ** -0.5
SQRT_2_PI = 0.7978845608028654
CUBIC = 0.044715
FP6_MAX = 7.5
TWO_ONES = 0x3F803F80
MAGIC = 1.5 * 2.0 ** 23

R_BV, R_BO, R_BQ3, R_BK3, R_BF3, R_GB = 0, 4 * D, 8 * D, 9 * D, 10 * D, 11 * D
R_W = 11 * D + EXPERTS


MAX_STEPS = 2 * (HEADS // 4)
ATT_STEPS = HEADS // 2 + 2
CHUNKS = {1: EXPERTS + 2, 2: EXPERTS + 1}


def stream_steps():
    def norm(l):
        return [("stats", l, 0), ("norm", l, 0)]

    out = [("keys", 0, 0)]
    for l in range(LAYERS):
        out += norm(l) + [("turn", l, 0), ("query", l, 0)] + [("load_x", 0, 0)] * (l == 0)
        scores = [("maxima", l, part) for part in range(MAX_STEPS)] + [("attend", l, part) for part in range(ATT_STEPS)]
        half = MAX_STEPS // 2
        extra = {("maxima", half): ("max_parts", 0), ("maxima", half + 1): ("max_turn", 0),
                 ("attend", 0): ("max_parts", 1), ("attend", 2): ("max_turn", 1)}
        if l == SPARSE:
            extra.update({("maxima", 1): ("query_rows", 0), ("maxima", half - 1): ("query_means", 0),
                          ("attend", 1): ("choose", 0), ("attend", 3): ("choose", 1), ("attend", ATT_STEPS - 1): ("chosen", 0)})
        for step, _, part in scores:
            if (step, part) in extra:
                out.append((extra[step, part][0], l, extra[step, part][1]))
            out.append((step, l, part))
        out += [("heads", l, 0), ("heads_turn", l, 0)]
        out += [("project", l, 0)] + [("key_rows", SPARSE, 0)] * (l + 1 == SPARSE) + norm(l + LAYERS)
        if l + 1 == SPARSE:
            out += [("key_unit", SPARSE, 0), ("keys", SPARSE, 0), ("key_mean", SPARSE, 0), ("load_ctx", 0, 0)]
        elif l + 1 < LAYERS:
            out += [("keys", l + 1, 0)]
        if l == 0:
            out += [("turn", LAYERS, 0), ("route0", l, 0), ("gelu0", l, 0), ("blend0", l, 0)]
        if l in CHUNKS:
            out += [("turn", l + LAYERS, 0), ("logits", l, 0), ("hidden", l, 0), ("combine", l, 0), ("hidden", l, 1)]
            for n in range(CHUNKS[l]):
                out += [("output", l, n)] + [("comb_turn", l, 0)] * (l == 2 and n == 0) + [("out_bias", l, 0)] * (l == 2 and n == 1)
                out += [("hidden", l, n + 2)] * (n + 2 < CHUNKS[l])
        if l == 3:
            out += [("quantise", l, 0), ("quantise", l, 1), ("turn", l + LAYERS, 0), ("affine3", l, 0)]
    return out + [("store", 0, 0)]


TURNS_TAKEN = """
0010100111001000000000001001010101011010100101101011100001011101100110011011111101010100100000100010
0101100110101001011010001011010010001010000100001010011100100111011111011101110101111111001110010010
0100000000110101101011001010110011110000111110001001001011010000001110011010100000001011011011111010
11111010010010100110101010000000110000101110111110111111011111011010101110111101000111
"""


def schedule():
    left = [iter([(step, s, l, part) for step, l, part in stream_steps()]) for s in range(STREAMS)]
    return [next(left[int(s)]) for s in TURNS_TAKEN.split() for s in s]


SCHEDULE = schedule()


def max_tiles(l, part):
    g, r = divmod(part, RT)
    keys = P * (r + 1) if l == CAUSAL else ROWS
    n = BANK // keys
    return [(r, keys, h0, n) for h0 in range(4 * g, 4 * g + 4, n)]


def signals(step, s, l, part):
    return {
        "load_x": {f"x_loaded{s}": 16},
        "load_ctx": {f"ctx_loaded{s}": 16},
        "keys": {"a_full": 2, "a_read": 2, f"hi_ready{s}": 1, f"k_split{s}": 2, f"k_moved{s}": 16 * TERMS},
        "key_rows": {"a_full": 1, "a_read": 1, "rows_ready": 1, "rn_ready": 1},
        "key_unit": {"rows_ready": 1},
        "key_mean": {"a_full": 1, "a_read": 1},
        "stats": {"var_ready": 1, "rstd_ready": 1},
        "norm": {f"h_ready{s}": 1, "xb_ready": int(l < LAYERS or l == 2 * LAYERS - 1)},
        "turn": {"b_full": 1, "b_read": 1},
        "query": {"a_full": 1, "a_read": 1, f"hi_ready{s}": 1, f"q_split{s}": 2, f"q_moved{s}": 16 * TERMS},
        "query_rows": {"a_full": 1, "a_read": 1, "rows_ready": 2, "rn_ready": 1},
        "query_means": {"b_full": 1, "b_read": 1},
        "choose": {"sel_ready": part},
        "chosen": {"a_full": 1, "a_read": 1},
        "maxima": {"a_full": len(max_tiles(l, part % MAX_STEPS)), "a_read": len(max_tiles(l, part % MAX_STEPS))},
        "max_parts": {"m_parts_done": 1},
        "max_turn": {"b_full": 1, "b_read": 1, f"m_moved{s}": 16},
        "attend": {"b_full": 2 * (part < HEADS // 2), "b_read": 2 * (part < HEADS // 2),
                   f"pv_done{s}": int(part > 2 and part % 2 == 1), f"c_read{s}": int(part in (5, ATT_STEPS - 1))},
        "heads": {"a_full": RT, "a_read": RT},
        "heads_turn": {"b_full": 1, "b_read": 1},
        "project": {"a_full": 1, "a_read": 1},
        "route0": {"a_full": 1, "a_read": 1, "b_full": 1, "b_read": 1},
        "gelu0": {"cubic_ready": 1, "tanh_ready": 1},
        "blend0": {"x_done": 1},
        "logits": {"a_full": 1, "a_read": 1, "gap_ready": 1, "gap_exp": 1},
        "combine": {"comb_ready": 1},
        "comb_turn": {"b_full": 1, "b_read": 1},
        "out_bias": {"a_full": RT, "a_read": RT},
        "hidden": ({"a_full": 1, "a_read": 1, "tanh_ready": 1} if l == 1 else {"b_full": 2, "b_read": 2}),
        "output": ({} if (l, part) == (1, EXPERTS) else {"a_full": 1, "a_read": 1}),
        "quantise": {"xd_ready": part},
        "affine3": {"a_full": RT, "a_read": RT},
        "store": {f"stored{s}": 16},
    }[step]


LINKS = {"dve_step": 232}
CREDIT = {"a_read": RING, "b_read": RING, "stored0": 1, "stored1": 1}


class Ledger:

    def __init__(self):
        self.start, total = [], {}
        for item in SCHEDULE:
            self.start.append(dict(total))
            for name, n in signals(*item).items():
                total[name] = total.get(name, 0) + int(n)
        self.per_turn = {**{name: n for name, n in total.items() if n}, **LINKS}

    def index(self, i, name, k):
        return self.start[i].get(name, 0) + k

    def value(self, turn, i, name, k):
        return turn * self.per_turn[name] + (self.index(i, name, k) + CREDIT.get(name, 0))


LEDGER = Ledger()
assert LEDGER.per_turn["a_full"] % RING == 0 and LEDGER.per_turn["b_full"] % RING == 0
SEMAPHORES = sorted(LEDGER.per_turn)
STEP = {item: i for i, item in enumerate(SCHEDULE)}


def flamingo(nc, x, ctxT, attn_w, bias_cols, bias_rows, g_all, router0, block0, router1, fc1, fc2,
             gate_up, down, router2, w1, ws1, b1_cols, w2, ws2, b2_all, w3, ident_in, causal_qk,
             causal_kq, before_in, iota_in, out):
    with ExitStack() as ctx:
        def sb(name, shape, dt=F32):
            return ctx.enter_context(nc.sbuf_tensor(name, shape, dt))

        def two(name, shape, dt=F32):
            return [sb(f"{name}{s}", shape, dt) for s in range(STREAMS)]

        def psum(name, shape):
            return ctx.enter_context(nc.psum_tensor(name, shape, F32))

        def sem(name):
            return ctx.enter_context(nc.semaphore(name))

        attn_sb = sb("attn_sb", [P, LAYERS, 4, D])
        bcol = sb("bcol", [P, LAYERS, 2])
        brow = sb("brow", [P, R_W])
        gates = sb("gates", [P, 2 * LAYERS])
        tg = sb("tg", [P, 2 * LAYERS])
        tgh = sb("tgh", [P, 2 * LAYERS])
        gbo = sb("gbo", [P, LAYERS + 1, D])
        r0_sb = sb("r0_sb", [P, 1])
        r0_bc = sb("r0_bc", [P, P])
        blk0 = sb("blk0", [P, D])
        r1_sb = sb("r1_sb", [P, EXPERTS])
        fc1_sb = sb("fc1_sb", [P, EXPERTS + 2, 2, P])
        fc2_sb = sb("fc2_sb", [P, EXPERTS + 2, D])
        r2_sb = sb("r2_sb", [P, EXPERTS])
        w1_sb = sb("w1_sb", [P, EXPERTS + 1, HC, P])
        w2_sb = sb("w2_sb", [P, EXPERTS + 1, HC, D])
        b1_sb = sb("b1_sb", [P, EXPERTS + 1, HC])
        b2_sb = sb("b2_sb", [EXPERTS + 1, D])
        w3_sb = sb("w3_sb", [P, D])
        w3T = sb("w3T", [P, D])
        ident = sb("ident", [P, P])
        identb = sb("identb", [P, P], BF16)
        cqk = sb("cqk", [P, P])
        ckq = sb("ckq", [P, P])
        cqk_b = sb("cqk_b", [P, P], BF16)
        ckq_b = sb("ckq_b", [P, P], BF16)
        before = sb("before", [P, RT, ROWS])
        iota = sb("iota", [P, EXPERTS])
        mhalf = sb("mhalf", [P, RT * HEADS])
        idle = sb("idle", [1, STREAMS, 3])
        mean_k = sb("mean_k", [P, P])

        x_in = two("x_in", [P, RT, D])
        xs = two("xs", [P, RT, D])
        cT = two("cT", [P, ROWS])
        stats = two("stats", [P, RT, 6])
        mv = two("mv", [P, RT, 2])
        veps = two("veps", [P, RT])
        rstd = two("rstd", [P, RT])
        h = two("h", [P, RT, D])
        hT = two("hT", [P, ROWS])
        q_parts = two("q_parts", [P, 3, ROWS], BF16)
        k_parts = two("k_parts", [P, 3, ROWS], BF16)
        resid = two("resid", [P, ROWS])
        q_st = two("q_st", [SCT_ROWS, HEADS, ROWS], BF16)
        k_st = two("k_st", [SCT_ROWS, HEADS, ROWS], BF16)
        v_aug = two("v_aug", [P, RT, HEADS, VW])
        mx = two("mx", [P, RT, HEADS])
        mres = two("mres", [P, RT, HEADS])
        m_parts = two("m_parts", [P, 2, RT, P], BF16)
        mT = two("mT", [3 * HEADS // 2, 2, ROWS], BF16)
        raw = two("raw", [P, 4, ROWS])
        rden = two("rden", [P, RT, HEADS])
        heads_out = two("heads_out", [P, RT, D])
        coT = two("coT", [P, ROWS])
        ss = two("ss", [P, RT * HEADS])
        rn = two("rn", [P, RT * HEADS])
        dot = two("dot", [P, RT * HEADS])
        kbar = two("kbar", [P, D])
        work = two("work", [HEADS, SENT + ROWS])
        top8q = two("top8q", [HEADS, 8])
        selT = two("selT", [HEADS, ROWS])
        selm = two("selm", [P, RT, HEADS])
        junk = sb("junk", [P, ROWS])
        col = two("col", [P, 8, RT])
        lg = two("lg", [P, RT, EXPERTS])
        top = two("top", [P, RT, 8])
        topi = two("topi", [P, RT, 8], U32)
        topf = two("topf", [P, RT, 2])
        comb = two("comb", [P, RT, EXPERTS + 1])
        cmb2 = two("cmb2", [P, RT, EXPERTS])
        combT = two("combT", [EXPERTS + 1, ROWS])
        work_rows = [two(f"work_rows{i}_", [P, RT, D]) for i in range(4)]
        ffo = work_rows[2]
        sc3 = two("sc3", [P, RT * 4])
        rsc3 = two("rsc3", [P, RT * 4])
        amax = two("amax", [P, RT * 4])
        NPR, NACT = 8, 4
        probs = two("probs", [P, NPR, RT * ROWS])
        acts = [p[:, 0:NACT // 2, :].rearrange("p n (a r) -> p (n a) r", a=2) for p in probs]
        tanhs = [p[:, NACT // 2:NACT, :].rearrange("p n (a r) -> p (n a) r", a=2) for p in probs]
        hid = [p[:, :, :].rearrange("p (n c) (a r) -> p n (c a) r", n=NACT, a=2) for p in probs]

        A = psum("A", [P, RING, BANK])
        B = psum("B", [P, RING, BANK])
        C = psum("C", [P, STREAMS, 2, ROWS])

        sems = {name: sem(name) for name in SEMAPHORES}
        w3_loaded, cleared, attn_loaded, ffn_loaded, big_loaded = sem("w3_loaded"), sem("cleared"), sem("attn_loaded"), sem("ffn_loaded"), sem("big_loaded")
        gates_done, w3_quantised, w3_turned = sem("gates_done"), sem("w3_quantised"), sem("w3_turned")
        w3_copied, setup_done, setup_step = sem("w3_copied"), sem("setup_done"), sem("setup_step")

        attention_loads = [
            (attn_sb[:, :, :, :], attn_w), (bcol[:, :, :], bias_cols), (ident[:, :], ident_in),
            (brow[:, :], bias_rows.broadcast_to([P, R_W])), (gates[:, :], g_all.broadcast_to([P, 2 * LAYERS])),
            (cqk[:, :], causal_qk), (ckq[:, :], causal_kq), (iota[:, :], iota_in),
            (before[:, :, :], before_in), (r0_sb[:, :], router0)]
        ffn_loads = [
            (blk0[:, :], block0), (r1_sb[:, :], router1),
            (fc1_sb[:, 0:EXPERTS, :, :].rearrange("d e a i -> d e (a i)"), fc1.rearrange("e d i -> d e i")),
            (fc1_sb[:, EXPERTS:EXPERTS + 2, :, :], gate_up),
            (fc2_sb[:, 0:EXPERTS, :], fc2.rearrange("e i d -> i e d")),
            (fc2_sb[:, EXPERTS:EXPERTS + 2, :], down.rearrange("(c i) d -> i c d", c=2))]
        big_loads = [
            (r2_sb[:, :], router2), (b1_sb[:, :, :], b1_cols), (b2_sb[:, :], b2_all),
            (w1_sb[:, 0:EXPERTS, :, :].rearrange("d e c i -> d e (c i)"), w1.rearrange("e d i -> d e i")),
            (w1_sb[:, EXPERTS, :, :].rearrange("d c i -> d (c i)"), ws1),
            (w2_sb[:, 0:EXPERTS, :, :].rearrange("i e c d -> i (e c) d"),
             w2.rearrange("e (c i) d -> i (e c) d", c=HC)),
            (w2_sb[:, EXPERTS, :, :], ws2.rearrange("(c i) d -> i c d", c=HC))]

        class Walk:

            def __init__(self, turn, own=None):
                self.turn, self.own, self.i, self.links = turn, own, 0, 0

            def at(self, name, k):
                return LEDGER.value(self.turn, self.i, name, k)

            def at_step(self, name, k, *item):
                return LEDGER.value(self.turn, STEP[item], name, k)

            def slot(self, name, k, slots):
                return (LEDGER.index(self.i, name, k) - 1) % slots

            def step(self):
                self.links += 1
                return self.turn * LINKS[self.own] + self.links

        def a_bank(w, k):
            return A[:, w.slot("a_full", k, RING), :]

        def b_bank(w, k):
            return B[:, w.slot("b_full", k, RING), :]

        def clear(engine, s):
            engine.memset(q_st[s][:, :, :].bitcast(F32), 0.0)
            engine.memset(k_st[s][0:MAX_ROW, :, :].bitcast(F32), 0.0)
            engine.memset(m_parts[s][:, :, :, :], 0.0)
            engine.memset(v_aug[s][:, :, :, HD:VW], 1.0)
            return engine.memset(work[s][:, 0:SENT], BIG)

        block = ctx.enter_context(nc.Block())

        @block.sync
        def _(sp):
            for s in range(STREAMS):
                sp.sem_inc(sems[f"stored{s}"], CREDIT[f"stored{s}"])
            sp.dma_start(w3_sb[:, :], w3).then_inc(w3_loaded, 16)
            for dst, src in attention_loads:
                sp.dma_start(dst, src).then_inc(attn_loaded, 16)

            def load_x(b, s):
                sp.dma_start(x_in[s][:, :, :], x[b, :, :].rearrange("(t p) d -> p t d", p=P))\
                  .then_inc(sems[f"x_loaded{s}"], 16)

            def load_ctx(b, s):
                sp.dma_start(cT[s][:, :], ctxT[b, :, :]).then_inc(sems[f"ctx_loaded{s}"], 16)

            for s in range(STREAMS):
                load_ctx(s, s)
                load_x(s, s)

            def moves(turn, more):
                w = Walk(turn)
                for w.i, (step, s, l, part) in enumerate(SCHEDULE):
                    if step == "load_x" and more:
                        sp.wait_ge(sems["xb_ready"], w.at_step("xb_ready", 1, "norm", s, 0, 0))
                        load_x((turn + 1) * STREAMS + s, s)
                    if step == "load_ctx" and more:
                        sp.wait_ge(sems["a_full"], w.at_step("a_full", 2, "keys", s, LAYERS - 1, 0))
                        load_ctx((turn + 1) * STREAMS + s, s)
                    if step == "keys":
                        for n in range(3):
                            if n == 0:
                                sp.wait_ge(sems[f"hi_ready{s}"], w.at(f"hi_ready{s}", 1))
                            else:
                                sp.wait_ge(sems[f"k_split{s}"], w.at(f"k_split{s}", n))
                            for i in [i for i in range(TERMS) if K_TERMS[i] == n]:
                                sp.dma_start(k_st[s][i * HD:(i + 1) * HD, :, :], k_parts[s][:, n, :])\
                                  .then_inc(sems[f"k_moved{s}"], 16)
                    if step == "query":
                        for n in range(3):
                            if n == 0:
                                sp.wait_ge(sems[f"hi_ready{s}"], w.at(f"hi_ready{s}", 1))
                            else:
                                sp.wait_ge(sems[f"q_split{s}"], w.at(f"q_split{s}", n))
                            for i in [i for i in range(TERMS) if Q_TERMS[i] == n]:
                                sp.dma_start(q_st[s][i * HD:(i + 1) * HD, :, :], q_parts[s][:, n, :])\
                                  .then_inc(sems[f"q_moved{s}"], 16)
                    if step == "max_turn":
                        sp.wait_ge(sems["b_read"], w.at("b_read", 1))
                        h0 = part * HEADS // 2
                        sp.dma_start(q_st[s][MAX_ROW:MAX_ROW + 3, h0:h0 + HEADS // 2, :],
                                     mT[s][0:3 * HEADS // 2, part, :]).then_inc(sems[f"m_moved{s}"], 16)
                    if step == "store":
                        sp.wait_ge(sems["a_read"], w.at_step("a_read", RT, "affine3", s, 3, 0))
                        sp.dma_start(out[turn * STREAMS + s, :, :].rearrange("(t p) d -> p t d", p=P),
                                     xs[s][:, :, :]).then_inc(sems[f"stored{s}"], 16)

            with sp.Fori(0, PAIRS - 1) as turn:
                moves(turn, True)
            moves(PAIRS - 1, False)
            for s in range(STREAMS):
                sp.wait_ge(sems[f"stored{s}"], 16 * PAIRS + CREDIT[f"stored{s}"])

        @block.gpsimd
        def _(pool):
            for s in range(STREAMS):
                ones = nc.gpsimd.memset(k_st[s][MAX_ROW:SCT_ROWS, :, :].bitcast(U32), TWO_ONES)
            ones.then_inc(cleared, 1)
            pool.wait_ge(cleared, 1)
            clear(nc.gpsimd, 1).then_inc(cleared, 1)
            for dst, src in ffn_loads:
                pool.dma_start(dst, src).then_inc(ffn_loaded, 16)
            for dst, src in big_loads:
                pool.dma_start(dst, src).then_inc(big_loaded, 16)
            pool.wait_ge(setup_done, 1)

            with pool.Fori(0, PAIRS) as turn:
                w = Walk(turn)
                for w.i, (step, s, l, part) in enumerate(SCHEDULE):
                    if step == "stats":
                        pool.wait_ge(sems["var_ready"], w.at("var_ready", 1))
                        nc.gpsimd.tensor_tensor(rstd[s][:, :], veps[s][:, :], mhalf[:, 0:RT], ALU.pow)\
                            .then_inc(sems["rstd_ready"], 1)
                    if step == "norm" and (l < LAYERS or l == 2 * LAYERS - 1):
                        pool.wait_ge(sems[f"h_ready{s}"], w.at(f"h_ready{s}", 1))
                        if l == 0:
                            pool.wait_ge(sems[f"stored{s}"], w.at(f"stored{s}", 0))
                        nc.gpsimd.tensor_tensor(xs[s][:, :, :], (x_in if l == 0 else xs)[s][:, :, :],
                                                gbo[:, min(l, LAYERS), :].unsqueeze(1).broadcast_to([P, RT, D]), ALU.add)\
                            .then_inc(sems["xb_ready"], 1)
                    if step in ("key_rows", "query_rows"):
                        pool.wait_ge(sems["rows_ready"], w.at("rows_ready", 1))
                        nc.gpsimd.tensor_tensor(rn[s][:, :], ss[s][:, :], mhalf[:, :], ALU.pow)\
                            .then_inc(sems["rn_ready"], 1)

        @block.scalar
        def _(act):
            act.sem_inc(sems["b_read"], CREDIT["b_read"])
            act.wait_ge(attn_loaded, 16 * len(attention_loads))
            nc.scalar.activation(tg[:, :], gates[:, :], ACT.Tanh).then_inc(gates_done, 1)
            act.wait_ge(w3_turned, 1)
            nc.scalar.activation(w3T[:, :], B[:, 0, 0:D], ACT.Copy).then_inc(w3_copied, 1)
            act.wait_ge(setup_done, 1)

            with act.Fori(0, PAIRS) as turn:
                w = Walk(turn)

                def copy_ac(k, dst, src, func=ACT.Copy):
                    act.wait_ge(sems["b_full"], w.at("b_full", k))
                    nc.scalar.activation(dst, src, func).then_inc(sems["b_read"], 1)

                for w.i, (step, s, l, part) in enumerate(SCHEDULE):
                    if step == "turn":
                        copy_ac(1, hT[s][:, :], b_bank(w, 1)[:, 0:ROWS])
                    if step in ("keys", "query"):
                        parts, b = (k_parts, 1) if step == "keys" else (q_parts, 0)
                        act.wait_ge(sems["a_full"], w.at("a_full", 1))
                        nc.scalar.activation(parts[s][:, 0, :], a_bank(w, 1)[:, 0:ROWS], ACT.Identity,
                                             bias=bcol[:, l, b:b + 1]).then_inc(sems[f"hi_ready{s}"], 1)
                    if step == "query_means":
                        copy_ac(1, work[s][:, SENT:SENT + ROWS], b_bank(w, 1)[0:HEADS, 0:ROWS])
                    if step == "max_turn":
                        copy_ac(1, mT[s][:, part, :], b_bank(w, 1)[:, :].bitcast(BF16)[0:3 * HEADS // 2, 0:ROWS])
                    if step == "attend":
                        n = P + ROWS if l == CAUSAL else RT * ROWS
                        if part in (4, 6):
                            act.wait_ge(sems[f"pv_done{s}"], w.at_step(f"pv_done{s}", 1, "attend", s, l, part - 1))
                        for k in range(1, 3 if part < HEADS // 2 else 1):
                            act.wait_ge(sems["b_full"], w.at("b_full", k))
                            nc.scalar.activation(probs[s][:, (2 * part + k - 1) % NPR, 0:n],
                                                 b_bank(w, k)[:, 0:n],
                                                 ACT.Exp, scale=SQRT_HD).then_inc(sems["b_read"], 1)
                        if part in (5, ATT_STEPS - 1):
                            g0 = 0 if part == 5 else 2
                            act.wait_ge(sems[f"pv_done{s}"], w.at(f"pv_done{s}", 1))
                            nc.scalar.activation(raw[s][:, g0:g0 + 2, :], C[:, s, :, :], ACT.Copy)\
                                .then_inc(sems[f"c_read{s}"], 1)
                    if step == "heads_turn":
                        copy_ac(1, coT[s][:, :], b_bank(w, 1)[:, 0:ROWS])
                    if step == "route0":
                        act.wait_ge(sems["b_full"], w.at("b_full", 1))
                        z = b_bank(w, 1)[:, 0:RT * D]
                        nc.scalar.activation(ffo[s][:, :, :].rearrange("p t d -> p (t d)"), z, ACT.Copy)
                        nc.scalar.activation(work_rows[0][s][:, :, :].rearrange("p t d -> p (t d)"), z, ACT.Square)\
                            .then_inc(sems["b_read"], 1)
                    if step == "gelu0":
                        act.wait_ge(sems["cubic_ready"], w.at("cubic_ready", 1))
                        nc.scalar.activation(work_rows[1][s][:, :, :], work_rows[0][s][:, :, :], ACT.Tanh,
                                             scale=SQRT_2_PI).then_inc(sems["tanh_ready"], 1)
                    if step == "logits":
                        act.wait_ge(sems["gap_ready"], w.at("gap_ready", 1))
                        nc.scalar.activation(col[s][:, 1, :], col[s][:, 0, :], ACT.Exp).then_inc(sems["gap_exp"], 1)
                    if step == "hidden" and l == 1:
                        act.wait_ge(sems["a_full"], w.at("a_full", 1))
                        nc.scalar.activation(tanhs[s][:, part % NACT, :], a_bank(w, 1)[:, 0:ROWS], ACT.Tanh,
                                             scale=0.5).then_inc(sems["tanh_ready"], 1)
                    if step == "comb_turn":
                        copy_ac(1, combT[s][:, :], b_bank(w, 1)[0:EXPERTS + 1, 0:ROWS])
                    if step == "hidden" and l == 2:
                        for half in range(2):
                            act.wait_ge(sems["b_full"], w.at("b_full", half + 1))
                            for j in range(2):
                                c = 2 * half + j
                                ins = nc.scalar.activation(
                                    hid[s][:, part % NACT, c, :],
                                    b_bank(w, half + 1)[:, j * ROWS:(j + 1) * ROWS],
                                    ACT.Gelu, bias=b1_sb[:, part, c:c + 1])
                            ins.then_inc(sems["b_read"], 1)

        @block.tensor
        def _(pe):
            pe.wait_ge(w3_quantised, 1)
            pe.wait_ge(attn_loaded, 16 * len(attention_loads))
            nc.tensor.transpose(B[:, 0, 0:D], work_rows[0][0][:, 0, :], ident[:, :]).then_inc(w3_turned, 1)
            pe.wait_ge(w3_copied, 1)
            pe.wait_ge(setup_done, 1)

            with pe.Fori(0, PAIRS) as turn:
                w = Walk(turn)

                def turn_rows(k, src):
                    pe.wait_ge(sems["b_read"], w.at("b_read", k - RING))
                    for r in range(RT):
                        ins = nc.tensor.transpose(b_bank(w, 1)[:, r * P:(r + 1) * P], src[:, r, :], ident[:, :])
                    ins.then_inc(sems["b_full"], 1)

                def rows_product(dst, xT, rhs):
                    n = rhs.shape[-1]
                    for r in range(RT):
                        ins = nc.tensor.matmul(dst[:, r * n:(r + 1) * n], xT[:, r * P:(r + 1) * P], rhs,
                                               start=True, stop=True)
                    return ins

                def scores(s, l, k, r, keys, h0, n):
                    pe.wait_ge(sems["a_read"], w.at("a_read", k - RING))
                    bank = a_bank(w, k)
                    for i in range(n):
                        o = bank[:, i * keys:(i + 1) * keys]
                        ins = nc.tensor.matmul(o, q_st[s][0:SC_ROWS, h0 + i, r * P:(r + 1) * P],
                                               k_st[s][0:SC_ROWS, h0 + i, 0:keys], start=True, stop=l != CAUSAL)
                        if l == CAUSAL:
                            ins = nc.tensor.matmul(o[:, keys - P:keys], identb[:, :], cqk_b[:, :], start=False, stop=True)
                    ins.then_inc(sems["a_full"], 1)

                def scores_turned(s, l, hh, k):
                    pe.wait_ge(sems["b_read"], w.at("b_read", k - RING))
                    bank = b_bank(w, k)
                    for t in range(RT):
                        q0 = P * t if l == CAUSAL else 0
                        o = bank[:, t * ROWS:t * ROWS + ROWS - q0]
                        ins = nc.tensor.matmul(o, k_st[s][0:SCT_ROWS, hh, t * P:(t + 1) * P],
                                               q_st[s][0:SCT_ROWS, hh, q0:ROWS], start=True, stop=l != CAUSAL)
                        if l == CAUSAL:
                            ins = nc.tensor.matmul(o[:, 0:P], identb[:, :], ckq_b[:, :], start=False, stop=True)
                    ins.then_inc(sems["b_full"], 1)

                def weigh(s, l, g, t):
                    if t == 0:
                        pe.wait_ge(sems["b_read"], w.at_step("b_read", 2, "attend", s, l, 2 * g + 1))
                        if g == 2:
                            pe.wait_ge(sems[f"c_read{s}"], w.at_step(f"c_read{s}", 1, "attend", s, l, 5))
                    q0 = P * t if l == CAUSAL else 0
                    for j in range(4):
                        hh = 4 * g + j
                        ins = nc.tensor.matmul(C[VW * j:VW * (j + 1), s, g % 2, q0:ROWS], v_aug[s][:, t, hh, :],
                                               probs[s][:, hh % NPR, t * ROWS:t * ROWS + ROWS - q0],
                                               start=t == 0, stop=t == RT - 1, tile_position=(0, VW * j))
                    if t == RT - 1:
                        ins.then_inc(sems[f"pv_done{s}"], 1)

                for w.i, (step, s, l, part) in enumerate(SCHEDULE):
                    if step == "keys":
                        if l == 0:
                            pe.wait_ge(sems[f"ctx_loaded{s}"], w.at_step(f"ctx_loaded{s}", 16, "load_ctx", s, 0, 0))
                        pe.wait_ge(sems["a_read"], w.at("a_read", 1 - RING))
                        nc.tensor.matmul(a_bank(w, 1)[:, 0:ROWS], attn_sb[:, l, 1, :], cT[s][:, :], start=True, stop=True)\
                            .then_inc(sems["a_full"], 1)
                        pe.wait_ge(sems["a_read"], w.at("a_read", 2 - RING))
                        rows_product(a_bank(w, 2), cT[s], attn_sb[:, l, 2, :]).then_inc(sems["a_full"], 1)
                    if step == "key_rows":
                        pe.wait_ge(sems["a_read"], w.at("a_read", 1 - RING))
                        rows_product(a_bank(w, 1), cT[s], attn_sb[:, l, 1, :]).then_inc(sems["a_full"], 1)
                    if step == "key_mean":
                        pe.wait_ge(sems["rows_ready"], w.at_step("rows_ready", 1, "key_unit", s, l, 0))
                        pe.wait_ge(sems["a_read"], w.at("a_read", 1 - RING))
                        for t in range(RT):
                            ins = nc.tensor.matmul(a_bank(w, 1)[:, 0:D], mean_k[:, :], work_rows[1][s][:, t, :],
                                                   start=t == 0, stop=t == RT - 1)
                        ins.then_inc(sems["a_full"], 1)
                    if step == "turn":
                        if l < 2 * LAYERS - 1:
                            pe.wait_ge(sems[f"h_ready{s}"], w.at_step(f"h_ready{s}", 1, "norm", s, l, 0))
                        else:
                            pe.wait_ge(sems["xd_ready"], w.at_step("xd_ready", 1, "quantise", s, 3, 1))
                        turn_rows(1, h[s])
                    if step == "query":
                        pe.wait_ge(sems["b_read"], w.at_step("b_read", 1, "turn", s, l, 0))
                        pe.wait_ge(sems["a_read"], w.at("a_read", 1 - RING))
                        nc.tensor.matmul(a_bank(w, 1)[:, 0:ROWS], attn_sb[:, l, 0, :], hT[s][:, :], start=True, stop=True)\
                            .then_inc(sems["a_full"], 1)
                    if step == "query_rows":
                        pe.wait_ge(sems["a_read"], w.at("a_read", 1 - RING))
                        rows_product(a_bank(w, 1), hT[s], attn_sb[:, l, 0, :]).then_inc(sems["a_full"], 1)
                    if step == "query_means":
                        pe.wait_ge(sems["rows_ready"], w.at_step("rows_ready", 2, "query_rows", s, l, 0))
                        pe.wait_ge(sems["b_read"], w.at("b_read", 1 - RING))
                        for r in range(RT):
                            ins = nc.tensor.transpose(b_bank(w, 1)[0:HEADS, r * P:(r + 1) * P],
                                                      rn[s][:, r * HEADS:(r + 1) * HEADS], ident[:, :])
                        ins.then_inc(sems["b_full"], 1)
                    if step == "chosen":
                        pe.wait_ge(sems["sel_ready"], w.at_step("sel_ready", 1, "choose", s, l, 1))
                        pe.wait_ge(sems["a_read"], w.at("a_read", 1 - RING))
                        for r in range(RT):
                            ins = nc.tensor.matmul(a_bank(w, 1)[:, r * HEADS:(r + 1) * HEADS], selT[s][:, r * P:(r + 1) * P],
                                                   ident[0:HEADS, 0:HEADS], start=True, stop=True)
                        ins.then_inc(sems["a_full"], 1)
                    if step == "maxima":
                        if part == 0:
                            pe.wait_ge(sems[f"q_moved{s}"], w.at_step(f"q_moved{s}", 16 * TERMS, "query", s, l, 0))
                            pe.wait_ge(sems[f"k_moved{s}"], w.at_step(f"k_moved{s}", 16 * TERMS, "keys", s, l, 0))
                        for k, tile in enumerate(max_tiles(l, part), 1):
                            scores(s, l, k, *tile)
                    if step == "max_turn":
                        pe.wait_ge(sems["m_parts_done"], w.at_step("m_parts_done", 1, "max_parts", s, l, part))
                        pe.wait_ge(sems["b_read"], w.at("b_read", 1 - RING))
                        for r in range(RT):
                            ins = nc.tensor.transpose(b_bank(w, 1)[:, :].bitcast(BF16)[:, r * P:(r + 1) * P],
                                                      m_parts[s][:, part, r, :], identb[:, :])
                        ins.then_inc(sems["b_full"], 1)
                    if step == "attend":
                        if part == 0:
                            pe.wait_ge(sems["a_read"], w.at_step("a_read", 2, "keys", s, l, 0))
                        if part in (0, 4):
                            pe.wait_ge(sems[f"m_moved{s}"], w.at_step(f"m_moved{s}", 16, "max_turn", s, l, part // 4))
                        if part < HEADS // 2:
                            scores_turned(s, l, 2 * part, 1)
                            scores_turned(s, l, 2 * part + 1, 2)
                        if part > 1:
                            weigh(s, l, (part - 2) // 2, part % 2)
                    if step == "heads":
                        pe.wait_ge(sems[f"c_read{s}"], w.at_step(f"c_read{s}", 1, "attend", s, l, ATT_STEPS - 1))
                        for r in range(RT):
                            pe.wait_ge(sems["a_read"], w.at("a_read", r + 1 - RING))
                            for g in range(4):
                                ins = nc.tensor.transpose(a_bank(w, r + 1)[:, g * P:(g + 1) * P],
                                                          raw[s][:, g, r * P:(r + 1) * P], ident[:, :])
                            ins.then_inc(sems["a_full"], 1)
                    if step == "heads_turn":
                        pe.wait_ge(sems["a_read"], w.at_step("a_read", RT, "heads", s, l, 0))
                        turn_rows(1, heads_out[s])
                    if step == "project":
                        pe.wait_ge(sems["b_read"], w.at_step("b_read", 1, "heads_turn", s, l, 0))
                        pe.wait_ge(sems["a_read"], w.at("a_read", 1 - RING))
                        rows_product(a_bank(w, 1), coT[s], attn_sb[:, l, 3, :]).then_inc(sems["a_full"], 1)
                    if step == "route0":
                        pe.wait_ge(ffn_loaded, 16 * len(ffn_loads))
                        pe.wait_ge(sems["b_read"], w.at_step("b_read", 1, "turn", s, LAYERS, 0))
                        pe.wait_ge(sems["a_read"], w.at("a_read", 1 - RING))
                        nc.tensor.matmul(a_bank(w, 1)[:, 0:ROWS], r0_bc[:, :], hT[s][:, :], start=True, stop=True)\
                            .then_inc(sems["a_full"], 1)
                        pe.wait_ge(sems["b_read"], w.at("b_read", 1 - RING))
                        rows_product(b_bank(w, 1), hT[s], blk0[:, :]).then_inc(sems["b_full"], 1)
                    if step == "logits":
                        if l == 2:
                            pe.wait_ge(big_loaded, 16 * len(big_loads))
                        pe.wait_ge(sems["b_read"], w.at_step("b_read", 1, "turn", s, l + LAYERS, 0))
                        pe.wait_ge(sems["a_read"], w.at("a_read", 1 - RING))
                        rows_product(a_bank(w, 1), hT[s], (r1_sb if l == 1 else r2_sb)[:, :]).then_inc(sems["a_full"], 1)
                    if step == "hidden" and l == 1:
                        pe.wait_ge(sems["a_read"], w.at("a_read", 1 - RING))
                        for a in range(2):
                            ins = nc.tensor.matmul(a_bank(w, 1)[:, a * ROWS:(a + 1) * ROWS],
                                                   fc1_sb[:, part, a, :], hT[s][:, :], start=True, stop=True)
                        ins.then_inc(sems["a_full"], 1)
                    if step == "output" and l == 1 and part != EXPERTS:
                        chunks = [part] if part < EXPERTS else [part - 1, part]
                        pe.wait_ge(sems["a_read"], w.at_step("a_read", 1, "hidden", s, 1, part))
                        pe.wait_ge(sems["a_read"], w.at("a_read", 1 - RING))
                        for r in range(RT):
                            for c in chunks:
                                ins = nc.tensor.matmul(a_bank(w, 1)[:, r * D:(r + 1) * D],
                                                       acts[s][:, c % NACT, r * P:(r + 1) * P], fc2_sb[:, c, :],
                                                       start=c == chunks[0], stop=c == chunks[-1])
                        ins.then_inc(sems["a_full"], 1)
                    if step == "comb_turn":
                        pe.wait_ge(sems["comb_ready"], w.at_step("comb_ready", 1, "combine", s, 2, 0))
                        pe.wait_ge(sems["b_read"], w.at("b_read", 1 - RING))
                        for r in range(RT):
                            ins = nc.tensor.transpose(b_bank(w, 1)[0:EXPERTS + 1, r * P:(r + 1) * P], comb[s][:, r, :], ident[:, :])
                        ins.then_inc(sems["b_full"], 1)
                    if step == "out_bias":
                        pe.wait_ge(sems["b_read"], w.at_step("b_read", 1, "comb_turn", s, 2, 0))
                        for r in range(RT):
                            pe.wait_ge(sems["a_read"], w.at("a_read", r + 1 - RING))
                            nc.tensor.matmul(a_bank(w, r + 1)[:, 0:D], combT[s][:, r * P:(r + 1) * P], b2_sb[:, :],
                                             start=True, stop=True).then_inc(sems["a_full"], 1)
                    if step == "hidden" and l == 2:
                        for half in range(2):
                            pe.wait_ge(sems["b_read"], w.at("b_read", half + 1 - RING))
                            for j in range(2):
                                ins = nc.tensor.matmul(b_bank(w, half + 1)[:, j * ROWS:(j + 1) * ROWS],
                                                       w1_sb[:, part, 2 * half + j, :], hT[s][:, :], start=True, stop=True)
                            ins.then_inc(sems["b_full"], 1)
                    if step == "output" and l == 2:
                        pe.wait_ge(sems["b_read"], w.at_step("b_read", 2, "hidden", s, 2, part))
                        pe.wait_ge(sems["a_read"], w.at("a_read", 1 - RING))
                        for r in range(RT):
                            for c in range(HC):
                                ins = nc.tensor.matmul(a_bank(w, 1)[:, r * D:(r + 1) * D],
                                                       hid[s][:, part % NACT, c, r * P:(r + 1) * P],
                                                       w2_sb[:, part, c, :], start=c == 0, stop=c == HC - 1)
                        ins.then_inc(sems["a_full"], 1)
                    if step == "affine3":
                        pe.wait_ge(sems["b_read"], w.at_step("b_read", 1, "turn", s, 2 * LAYERS - 1, 0))
                        for r in range(RT):
                            pe.wait_ge(sems["a_read"], w.at("a_read", r + 1 - RING))
                            nc.tensor.matmul(a_bank(w, r + 1)[:, 0:D], hT[s][:, r * P:(r + 1) * P], w3T[:, :],
                                             start=True, stop=True).then_inc(sems["a_full"], 1)

        @block.vector
        def _(dve):
            dve.sem_inc(sems["a_read"], CREDIT["a_read"])
            nc.vector.memset(mhalf[:, :], -0.5)
            nc.vector.memset(mean_k[:, :], 1.0 / ROWS)
            clear(nc.vector, 0)
            setup_count = iter(range(1, 100))

            def next_setup():
                return next(setup_count)

            def blocks(ap):
                return ap.rearrange("p t (b i) -> p (t b) i", b=4)

            def per_block(ap, rows):
                return ap.unsqueeze(2).broadcast_to([P, 4 * rows, D // 4])

            def fp6_scales(done, after, s, rows, src):
                y, a, m2, inv = (wr[s][:, 0:rows, :] for wr in work_rows)
                amx, scale, rscale = (t[s][:, 0:4 * rows] for t in (amax, sc3, rsc3))

                nc.vector.tensor_reduce(amx, blocks(src), AX.X, ALU.max, apply_absolute_value=True).then_inc(done, 1)
                dve.wait_ge(done, after())
                nc.vector.tensor_scalar(scale, amx, 1.0 / FP6_MAX, 1e-30, ALU.mult, ALU.max).then_inc(done, 1)
                dve.wait_ge(done, after())
                nc.vector.reciprocal(rscale, scale).then_inc(done, 1)
                dve.wait_ge(done, after())
                nc.vector.tensor_tensor(blocks(y), blocks(src), per_block(rscale, rows), ALU.mult).then_inc(done, 1)
                dve.wait_ge(done, after())
                nc.vector.tensor_tensor(a, y, y, ALU.mult).then_inc(done, 1)
                dve.wait_ge(done, after())

            def fp6_values(done, after, s, rows, dst):
                y, a, m2, inv = (wr[s][:, 0:rows, :] for wr in work_rows)
                nc.vector.tensor_scalar(m2, a, 4.0, -4.0, ALU.is_ge, ALU.mult)
                nc.vector.tensor_scalar(inv, a, 16.0, -2.0, ALU.is_ge, ALU.mult).then_inc(done, 1)
                dve.wait_ge(done, after())
                nc.vector.scalar_tensor_tensor(inv, m2, 8.0, inv, ALU.add, ALU.add).then_inc(done, 1)
                dve.wait_ge(done, after())
                nc.vector.tensor_scalar(m2, m2, -1.0 / 32, 0.125, ALU.mult, ALU.add)
                nc.vector.tensor_tensor(y, y, inv, ALU.mult).then_inc(done, 1)
                dve.wait_ge(done, after())
                nc.vector.tensor_scalar(inv, a, 16.0, 0.25, ALU.is_ge, ALU.mult).then_inc(done, 1)
                dve.wait_ge(done, after())
                nc.vector.tensor_scalar(a, y, MAGIC, MAGIC, ALU.add, ALU.subtract)
                nc.vector.tensor_tensor(m2, m2, inv, ALU.add).then_inc(done, 1)
                dve.wait_ge(done, after())
                nc.vector.tensor_tensor(y, a, y, ALU.subtract).then_inc(done, 1)
                dve.wait_ge(done, after())
                nc.vector.scalar_tensor_tensor(a, y, 0.5, a, ALU.is_ge, ALU.subtract).then_inc(done, 1)
                dve.wait_ge(done, after())
                nc.vector.scalar_tensor_tensor(y, a, -1.0, m2, ALU.mult, ALU.mult).then_inc(done, 1)
                dve.wait_ge(done, after())
                return nc.vector.tensor_tensor(blocks(dst), blocks(y), per_block(sc3[s][:, 0:4 * rows], rows), ALU.mult)

            dve.wait_ge(w3_loaded, 16)
            fp6_scales(setup_step, next_setup, 0, 1, w3_sb[:, :].unsqueeze(1))
            fp6_values(setup_step, next_setup, 0, 1, work_rows[0][0][:, 0:1, :]).then_inc(w3_quantised, 1)
            dve.wait_ge(attn_loaded, 16 * len(attention_loads))
            nc.vector.tensor_copy(identb[:, :], ident[:, :])
            nc.vector.tensor_copy(cqk_b[:, :], cqk[:, :])
            nc.vector.tensor_copy(ckq_b[:, :], ckq[:, :])
            nc.vector.tensor_copy(r0_bc[:, :], r0_sb[:, :].broadcast_to([P, P])).then_inc(setup_step, 1)
            dve.wait_ge(setup_step, next_setup())
            dve.wait_ge(gates_done, 1)
            nc.vector.tensor_scalar(tgh[:, :], tg[:, :], 0.5, None, ALU.mult)
            for l in range(LAYERS):
                nc.vector.tensor_scalar(gbo[:, l, :], brow[:, R_BO + l * D:R_BO + (l + 1) * D], tg[:, l:l + 1], None,
                                        ALU.mult)
            for s in range(STREAMS):
                nc.vector.tensor_copy(comb[s][:, :, EXPERTS],
                                      tg[:, LAYERS + 2:LAYERS + 3].broadcast_to([P, RT]))
            nc.vector.tensor_scalar(gbo[:, LAYERS, :], brow[:, R_BF3:R_BF3 + D],
                                               tg[:, 2 * LAYERS - 1:2 * LAYERS], None, ALU.mult).then_inc(setup_step, 1)
            dve.wait_ge(setup_step, next_setup())
            dve.wait_ge(w3_copied, 1)
            dve.wait_ge(cleared, 2)
            nc.vector.memset(junk[:, :], 0.0).then_inc(setup_done, 1)

            with dve.Fori(0, PAIRS) as turn:
                w = Walk(turn, "dve_step")

                STATS, LOGITS, CHOICE = range(3)

                def pause(s, kind):
                    nc.vector.memset(idle[:, s, kind:kind + 1], 0.0)

                def split(s, l, parts, b, name):
                    dve.wait_ge(sems[f"hi_ready{s}"], w.at(f"hi_ready{s}", 1))
                    nc.vector.scalar_tensor_tensor(resid[s][:, :], a_bank(w, 1)[:, 0:ROWS], bcol[:, l, b:b + 1],
                                                   parts[s][:, 0, :], ALU.add, ALU.subtract)\
                        .then_inc(sems["a_read"], 1)
                    dve.wait_ge(sems["a_read"], w.at("a_read", 1))
                    nc.vector.tensor_copy(parts[s][:, 1, :], resid[s][:, :]).then_inc(sems[f"{name}_split{s}"], 1)
                    dve.wait_ge(sems[f"{name}_split{s}"], w.at(f"{name}_split{s}", 1))
                    nc.vector.tensor_tensor(parts[s][:, 2, :], resid[s][:, :], parts[s][:, 1, :], ALU.subtract)\
                        .then_inc(sems[f"{name}_split{s}"], 1)

                def rows_norms(s, k, bias):
                    dve.wait_ge(sems["a_full"], w.at("a_full", k))
                    nc.vector.tensor_tensor(work_rows[0][s][:, :, :],
                                            a_bank(w, 1)[:, 0:RT * D].rearrange("p (t d) -> p t d", t=RT),
                                            bias, ALU.add).then_inc(sems["a_read"], 1)
                    dve.wait_ge(sems["a_read"], w.at("a_read", k))
                    nc.vector.tensor_tensor(work_rows[1][s][:, :, :], work_rows[0][s][:, :, :],
                                                 work_rows[0][s][:, :, :], ALU.mult).then_inc(sems["dve_step"], 1)
                    dve.wait_ge(sems["dve_step"], w.step())
                    head_sums(ss[s], work_rows[1][s]).then_inc(sems["rows_ready"], 1)

                def head_sums(dst, src):
                    return nc.vector.tensor_reduce(dst[:, :].rearrange("p (t h) -> p t h", t=RT),
                                                   src[:, :, :].rearrange("p t (d h) -> p t h d", d=HD), AX.X, ALU.add)

                def by_head(ap):
                    return ap.rearrange("p (t h) -> p t h", t=RT).unsqueeze(2).broadcast_to([P, RT, HD, HEADS])

                def over_tiles(ap, n):
                    return ap.unsqueeze(1).broadcast_to([P, RT, n])

                def combine_logits(s, l):
                    dve.wait_ge(sems["a_full"], w.at("a_full", 1))
                    logits = a_bank(w, 1)[:, 0:RT * EXPERTS].rearrange("p (t e) -> p t e", t=RT)
                    if l == 2:
                        ins = nc.vector.tensor_tensor(lg[s][:, :, :], logits,
                                                      over_tiles(brow[:, R_GB:R_GB + EXPERTS], EXPERTS), ALU.add)
                    else:
                        ins = nc.vector.tensor_copy(lg[s][:, :, :], logits)
                    ins.then_inc(sems["a_read"], 1)
                    dve.wait_ge(sems["a_read"], w.at("a_read", 1))
                    pause(s, LOGITS)
                    nc.vector.max(top[s][:, 0, :], lg[s][:, 0, :])
                    nc.vector.max(top[s][:, 1, :], lg[s][:, 1, :]).then_inc(sems["dve_step"], 1)
                    dve.wait_ge(sems["dve_step"], w.step())
                    nc.vector.tensor_tensor(col[s][:, 0, :], top[s][:, :, 1], top[s][:, :, 0], ALU.subtract)\
                        .then_inc(sems["gap_ready"], 1)
                    nc.vector.max_index(topi[s][:, 0, :], top[s][:, 0, :], lg[s][:, 0, :])
                    nc.vector.max_index(topi[s][:, 1, :], top[s][:, 1, :], lg[s][:, 1, :]).then_inc(sems["dve_step"], 1)
                    dve.wait_ge(sems["dve_step"], w.step())
                    nc.vector.tensor_copy(topf[s][:, :, :], topi[s][:, :, 0:2]).then_inc(sems["dve_step"], 1)
                    dve.wait_ge(sems["dve_step"], w.step())

                def combine(s, l):
                    gate = (tgh if l == 1 else tg)[:, LAYERS + l:LAYERS + l + 1]
                    dve.wait_ge(sems["gap_exp"], w.at_step("gap_exp", 1, "logits", s, l, 0))
                    nc.vector.tensor_scalar(col[s][:, 2, :], col[s][:, 1, :], 1.0, None, ALU.add)\
                        .then_inc(sems["dve_step"], 1)
                    dve.wait_ge(sems["dve_step"], w.step())
                    nc.vector.reciprocal(col[s][:, 3, :], col[s][:, 2, :]).then_inc(sems["dve_step"], 1)
                    dve.wait_ge(sems["dve_step"], w.step())
                    nc.vector.scalar_tensor_tensor(col[s][:, 5, :], col[s][:, 1, :], gate, col[s][:, 3, :],
                                                   ALU.mult, ALU.mult)
                    nc.vector.tensor_scalar(col[s][:, 4, :], col[s][:, 3, :], gate, None, ALU.mult)\
                        .then_inc(sems["dve_step"], 1)
                    dve.wait_ge(sems["dve_step"], w.step())
                    for r in range(RT):
                        nc.vector.tensor_scalar(comb[s][:, r, 0:EXPERTS], iota[:, :], topf[s][:, r, 0:1],
                                                col[s][:, 4, r:r + 1], ALU.is_equal, ALU.mult)
                        ins = nc.vector.tensor_scalar(cmb2[s][:, r, :], iota[:, :], topf[s][:, r, 1:2],
                                                      col[s][:, 5, r:r + 1], ALU.is_equal, ALU.mult)
                    ins.then_inc(sems["dve_step"], 1)
                    dve.wait_ge(sems["dve_step"], w.step())
                    nc.vector.tensor_tensor(comb[s][:, :, 0:EXPERTS], comb[s][:, :, 0:EXPERTS], cmb2[s][:, :, :],
                                            ALU.add).then_inc(sems["comb_ready"], 1)
                    dve.wait_ge(sems["comb_ready"], w.at("comb_ready", 1))

                def accumulate(s, k, scale):
                    dve.wait_ge(sems["a_full"], w.at("a_full", k))
                    for r in range(RT):
                        ins = nc.vector.scalar_tensor_tensor(xs[s][:, r, :], a_bank(w, k)[:, r * D:(r + 1) * D],
                                                             scale(r), xs[s][:, r, :], ALU.mult, ALU.add)
                    ins.then_inc(sems["a_read"], 1)
                    dve.wait_ge(sems["a_read"], w.at("a_read", k))

                for w.i, (step, s, l, part) in enumerate(SCHEDULE):
                    if step == "keys":
                        dve.wait_ge(sems["a_full"], w.at("a_full", 1))
                        split(s, l, k_parts, 1, "k")
                        dve.wait_ge(sems["a_full"], w.at("a_full", 2))
                        bv = over_tiles(brow[:, R_BV + l * D:R_BV + (l + 1) * D], D).rearrange("p t (h d) -> p t h d", d=HD)
                        nc.vector.tensor_tensor(v_aug[s][:, :, :, 0:HD],
                                                a_bank(w, 2)[:, 0:RT * D].rearrange("p (t h d) -> p t h d", t=RT, d=HD), bv,
                                                ALU.add).then_inc(sems["a_read"], 1)
                    if step == "key_rows":
                        rows_norms(s, 1, over_tiles(brow[:, R_BK3:R_BK3 + D], D))
                    if step == "key_unit":
                        dve.wait_ge(sems["rn_ready"], w.at_step("rn_ready", 1, "key_rows", s, l, 0))
                        nc.vector.tensor_tensor(work_rows[1][s][:, :, :].rearrange("p t (d h) -> p t d h", d=HD),
                                                work_rows[0][s][:, :, :].rearrange("p t (d h) -> p t d h", d=HD),
                                                by_head(rn[s][:, :]), ALU.mult).then_inc(sems["rows_ready"], 1)
                    if step == "key_mean":
                        dve.wait_ge(sems["a_full"], w.at("a_full", 1))
                        nc.vector.tensor_copy(kbar[s][:, :], a_bank(w, 1)[:, 0:D]).then_inc(sems["a_read"], 1)
                    if step == "stats":
                        if l == 0:
                            dve.wait_ge(sems[f"x_loaded{s}"], w.at_step(f"x_loaded{s}", 16, "load_x", s, 0, 0))
                        for r in range(RT):
                            ins = nc.vector.bn_stats(stats[s][:, r, :], (x_in if l == 0 else xs)[s][:, r, :])
                        ins.then_inc(sems["dve_step"], 1)
                        dve.wait_ge(sems["dve_step"], w.step())
                        pause(s, STATS)
                        nc.vector.bn_aggr(mv[s][:, 0, :], stats[s][:, 0, :])
                        nc.vector.bn_aggr(mv[s][:, 1, :], stats[s][:, 1, :]).then_inc(sems["dve_step"], 1)
                        dve.wait_ge(sems["dve_step"], w.step())
                        nc.vector.tensor_scalar(veps[s][:, :], mv[s][:, :, 1], 1e-5, None, ALU.add)\
                            .then_inc(sems["var_ready"], 1)
                    if step == "norm":
                        dve.wait_ge(sems["rstd_ready"], w.at_step("rstd_ready", 1, "stats", s, l, 0))
                        for r in range(RT):
                            ins = nc.vector.tensor_scalar(h[s][:, r, :], (x_in if l == 0 else xs)[s][:, r, :], mv[s][:, r, 0:1],
                                                          rstd[s][:, r:r + 1], ALU.subtract, ALU.mult)
                        ins.then_inc(sems[f"h_ready{s}"], 1)
                    if step == "query":
                        dve.wait_ge(sems["a_full"], w.at("a_full", 1))
                        split(s, l, q_parts, 0, "q")
                    if step == "query_rows":
                        rows_norms(s, 1, over_tiles(brow[:, R_BQ3:R_BQ3 + D], D))
                        dve.wait_ge(sems["rows_ready"], w.at("rows_ready", 1))
                        nc.vector.tensor_tensor(work_rows[1][s][:, :, :], work_rows[0][s][:, :, :],
                                                over_tiles(kbar[s][:, :], D), ALU.mult).then_inc(sems["dve_step"], 1)
                        dve.wait_ge(sems["dve_step"], w.step())
                        head_sums(dot[s], work_rows[1][s]).then_inc(sems["dve_step"], 1)
                        dve.wait_ge(sems["dve_step"], w.step())
                        dve.wait_ge(sems["rn_ready"], w.at("rn_ready", 1))
                        nc.vector.tensor_tensor(rn[s][:, :], rn[s][:, :], dot[s][:, :], ALU.mult)\
                            .then_inc(sems["rows_ready"], 1)
                    if step == "choose":
                        dve.wait_ge(sems["b_read"], w.at_step("b_read", 1, "query_means", s, l, 0))
                        for _ in range(4 * part, 4 if part == 0 else ROUNDS):
                            pause(s, CHOICE)
                            nc.vector.max(top8q[s][:, :], work[s][:, :]).then_inc(sems["dve_step"], 1)
                            dve.wait_ge(sems["dve_step"], w.step())
                            pause(s, CHOICE)
                            nc.vector.match_replace(work[s][:, :], top8q[s][:, :], work[s][:, :], -BIG)\
                                .then_inc(sems["dve_step"], 1)
                            dve.wait_ge(sems["dve_step"], w.step())
                        if part == 1:
                            nc.vector.tensor_scalar(selT[s][:, :], work[s][:, SENT:SENT + ROWS], -0.5 * BIG, None,
                                                    ALU.is_le).then_inc(sems["sel_ready"], 1)
                            dve.wait_ge(sems["sel_ready"], w.at("sel_ready", 1))
                            nc.vector.memset(work[s][:, 0:SENT], BIG).then_inc(sems["dve_step"], 1)
                            dve.wait_ge(sems["dve_step"], w.step())
                    if step == "chosen":
                        dve.wait_ge(sems["a_full"], w.at("a_full", 1))
                        nc.vector.tensor_copy(selm[s][:, :, :].rearrange("p t h -> p (t h)"), a_bank(w, 1)[:, 0:RT * HEADS])\
                            .then_inc(sems["a_read"], 1)
                    if step == "maxima":
                        for k, (r, keys, h0, n) in enumerate(max_tiles(l, part), 1):
                            dve.wait_ge(sems["a_full"], w.at("a_full", k))
                            nc.vector.tensor_reduce(mx[s][:, r, h0:h0 + n],
                                                    a_bank(w, k).rearrange("p (n k) -> p n k", n=n),
                                                    AX.X, ALU.max).then_inc(sems["a_read"], 1)
                    if step == "max_parts":
                        last = (part + 1) * MAX_STEPS // 2 - 1
                        dve.wait_ge(sems["a_read"], w.at_step("a_read", len(max_tiles(l, last)), "maxima", s, l, last))
                        half = slice(part * HEADS // 2, (part + 1) * HEADS // 2)
                        first, second, third = (m_parts[s][:, part, :, i * HEADS // 2:(i + 1) * HEADS // 2] for i in range(3))
                        nc.vector.tensor_scalar(first, mx[s][:, :, half], -1.0, None, ALU.mult)\
                            .then_inc(sems["dve_step"], 1)
                        dve.wait_ge(sems["dve_step"], w.step())
                        nc.vector.scalar_tensor_tensor(mres[s][:, :, half], mx[s][:, :, half], -1.0, first,
                                                       ALU.mult, ALU.subtract).then_inc(sems["dve_step"], 1)
                        dve.wait_ge(sems["dve_step"], w.step())
                        nc.vector.tensor_copy(second, mres[s][:, :, half]).then_inc(sems["dve_step"], 1)
                        dve.wait_ge(sems["dve_step"], w.step())
                        nc.vector.tensor_tensor(third, mres[s][:, :, half], second, ALU.subtract)\
                            .then_inc(sems["m_parts_done"], 1)
                    if step == "heads":
                        for r in range(RT):
                            dve.wait_ge(sems["a_full"], w.at("a_full", r + 1))
                            bank = a_bank(w, r + 1).rearrange("p (h v) -> p h v", v=VW)
                            nc.vector.reciprocal(rden[s][:, r, :], bank[:, :, HD]).then_inc(sems["dve_step"], 1)
                            dve.wait_ge(sems["dve_step"], w.step())
                            if l == SPARSE:
                                if r == 0:
                                    dve.wait_ge(sems["a_read"], w.at_step("a_read", 1, "chosen", s, l, 0))
                                nc.vector.tensor_tensor(rden[s][:, r, :], rden[s][:, r, :], selm[s][:, r, :], ALU.mult)\
                                    .then_inc(sems["dve_step"], 1)
                                dve.wait_ge(sems["dve_step"], w.step())
                            nc.vector.tensor_tensor(heads_out[s][:, r, :].rearrange("p (h d) -> p h d", d=HD),
                                                    bank[:, :, 0:HD],
                                                    rden[s][:, r, :].unsqueeze(2).broadcast_to([P, HEADS, HD]),
                                                    ALU.mult).then_inc(sems["a_read"], 1)
                    if step == "project":
                        dve.wait_ge(sems["a_full"], w.at("a_full", 1))
                        dve.wait_ge(sems["xb_ready"], w.at_step("xb_ready", 1, "norm", s, l, 0))
                        nc.vector.scalar_tensor_tensor(xs[s][:, :, :].rearrange("p t d -> p (t d)"),
                                                       a_bank(w, 1)[:, 0:RT * D], tg[:, l:l + 1],
                                                       xs[s][:, :, :].rearrange("p t d -> p (t d)"),
                                                       ALU.mult, ALU.add).then_inc(sems["a_read"], 1)
                        dve.wait_ge(sems["a_read"], w.at("a_read", 1))
                    if step == "affine3":
                        n = 2 * LAYERS - 1
                        dve.wait_ge(sems["xb_ready"], w.at_step("xb_ready", 1, "norm", s, n, 0))
                        for r in range(RT):
                            dve.wait_ge(sems["a_full"], w.at("a_full", r + 1))
                            nc.vector.scalar_tensor_tensor(xs[s][:, r, :], a_bank(w, r + 1)[:, 0:D], tg[:, n:n + 1],
                                                           xs[s][:, r, :], ALU.mult, ALU.add).then_inc(sems["a_read"], 1)
                    if step == "route0":
                        dve.wait_ge(sems["a_full"], w.at("a_full", 1))
                        for r in range(RT):
                            nc.vector.scalar_tensor_tensor(junk[:, 0:P], a_bank(w, 1)[:, r * P:(r + 1) * P], 1.0, ident[:, :],
                                                           ALU.mult, ALU.mult, accum_out=col[s][:, 0, r:r + 1])\
                                .then_inc(sems["dve_step"], 1)
                            dve.wait_ge(sems["dve_step"], w.step())
                            nc.vector.tensor_scalar(junk[:, :], a_bank(w, 1)[:, 0:ROWS], col[s][:, 0, r:r + 1], None,
                                                    ALU.is_gt, ALU.add, accum_out=col[s][:, 1, r:r + 1])\
                                .then_inc(sems["dve_step"], 1)
                            dve.wait_ge(sems["dve_step"], w.step())
                            ins = nc.vector.scalar_tensor_tensor(junk[:, :], a_bank(w, 1)[:, 0:ROWS], col[s][:, 0, r:r + 1],
                                                                 before[:, r, :], ALU.is_equal, ALU.mult,
                                                                 accum_out=col[s][:, 2, r:r + 1])
                            if r == 0:
                                ins.then_inc(sems["dve_step"], 1)
                                dve.wait_ge(sems["dve_step"], w.step())
                        ins.then_inc(sems["a_read"], 1)
                        dve.wait_ge(sems["a_read"], w.at("a_read", 1))
                        nc.vector.tensor_tensor(col[s][:, 3, :], col[s][:, 1, :], col[s][:, 2, :], ALU.add)\
                            .then_inc(sems["dve_step"], 1)
                        dve.wait_ge(sems["dve_step"], w.step())
                        nc.vector.tensor_scalar(col[s][:, 4, :], col[s][:, 3, :], KEEP0 - 0.5, 0.5, ALU.is_lt, ALU.mult)
                        nc.vector.tensor_scalar(col[s][:, 5, :], col[s][:, 3, :], KEEP0 - 0.5, None, ALU.is_gt)\
                            .then_inc(sems["dve_step"], 1)
                        dve.wait_ge(sems["dve_step"], w.step())
                    if step == "gelu0":
                        z, u = ffo[s][:, :, :], work_rows[0][s][:, :, :]
                        dve.wait_ge(sems["b_read"], w.at_step("b_read", 1, "route0", s, l, 0))
                        nc.vector.tensor_scalar(u, u, CUBIC, 1.0, ALU.mult, ALU.add).then_inc(sems["dve_step"], 1)
                        dve.wait_ge(sems["dve_step"], w.step())
                        nc.vector.tensor_tensor(u, u, z, ALU.mult).then_inc(sems["cubic_ready"], 1)
                        for r in range(RT):
                            nc.vector.tensor_scalar(h[s][:, r, :], h[s][:, r, :], col[s][:, 5, r:r + 1], None, ALU.mult)
                    if step == "blend0":
                        z, t = ffo[s][:, :, :], work_rows[1][s][:, :, :]
                        dve.wait_ge(sems["tanh_ready"], w.at_step("tanh_ready", 1, "gelu0", s, l, 0))
                        nc.vector.scalar_tensor_tensor(z, t, 1.0, z, ALU.add, ALU.mult).then_inc(sems["dve_step"], 1)
                        dve.wait_ge(sems["dve_step"], w.step())
                        for r in range(RT):
                            ins = nc.vector.scalar_tensor_tensor(h[s][:, r, :], ffo[s][:, r, :], col[s][:, 4, r:r + 1],
                                                                 h[s][:, r, :], ALU.mult, ALU.add)
                        ins.then_inc(sems["dve_step"], 1)
                        dve.wait_ge(sems["dve_step"], w.step())
                        nc.vector.scalar_tensor_tensor(xs[s][:, :, :], h[s][:, :, :], tg[:, LAYERS:LAYERS + 1],
                                                       xs[s][:, :, :], ALU.mult, ALU.add).then_inc(sems["x_done"], 1)
                        dve.wait_ge(sems["x_done"], w.at("x_done", 1))
                    if step == "logits":
                        combine_logits(s, l)
                    if step == "combine":
                        combine(s, l)
                    if step == "hidden" and l == 1:
                        i, bank = part % NACT, a_bank(w, 1)
                        dve.wait_ge(sems["tanh_ready"], w.at("tanh_ready", 1))
                        nc.vector.scalar_tensor_tensor(tanhs[s][:, i, :], tanhs[s][:, i, :], 1.0, bank[:, 0:ROWS],
                                                       ALU.add, ALU.mult).then_inc(sems["dve_step"], 1)
                        dve.wait_ge(sems["dve_step"], w.step())
                        nc.vector.tensor_tensor(acts[s][:, i, :], tanhs[s][:, i, :], bank[:, ROWS:2 * ROWS], ALU.mult)\
                            .then_inc(sems["a_read"], 1)
                    if step == "output" and l == 1 and part < EXPERTS:
                        accumulate(s, 1, lambda r: comb[s][:, r, part:part + 1])
                    if step == "output" and l == 1 and part > EXPERTS:
                        accumulate(s, 1, lambda r: tgh[:, LAYERS + 1:LAYERS + 2])
                    if step == "out_bias":
                        for r in range(RT):
                            dve.wait_ge(sems["a_full"], w.at("a_full", r + 1))
                            nc.vector.tensor_tensor(xs[s][:, r, :], a_bank(w, r + 1)[:, 0:D], xs[s][:, r, :], ALU.add)\
                                .then_inc(sems["a_read"], 1)
                        dve.wait_ge(sems["a_read"], w.at("a_read", RT))
                    if step == "output" and l == 2:
                        accumulate(s, 1, lambda r: comb[s][:, r, part:part + 1])
                    if step == "quantise":
                        if part == 0:
                            dve.wait_ge(sems[f"h_ready{s}"], w.at_step(f"h_ready{s}", 1, "norm", s, 2 * LAYERS - 1, 0))
                            fp6_scales(sems["dve_step"], w.step, s, RT, h[s][:, :, :])
                        else:
                            fp6_values(sems["dve_step"], w.step, s, RT, h[s][:, :, :]).then_inc(sems["xd_ready"], 1)
                assert w.links == LINKS["dve_step"], w.links

    return nc


def _arrays(i):
    import numpy as np

    f = np.float32

    def turned(w, by_feature):
        t = np.asarray(w).T
        return t.reshape(D, HEADS, HD).transpose(0, 2, 1).reshape(D, D) if by_feature else t

    def vec(name):
        return np.asarray(i[name]) if name in i else np.zeros(D, f)

    def dh(v):
        return v.reshape(HEADS, HD).T.reshape(D)

    attn_w = np.stack([np.stack([turned(i[f"L{l}_xattn_Wq"], True), turned(i[f"L{l}_xattn_Wk"], True),
                                 turned(i[f"L{l}_xattn_Wv"], False), turned(i[f"L{l}_xattn_Wo"], False)], axis=1)
                       for l in range(LAYERS)], axis=1)
    bias_cols = np.stack([np.stack([dh(vec(f"L{l}_xattn_bq")), dh(vec(f"L{l}_xattn_bk"))], axis=1)
                          for l in range(LAYERS)], axis=1)
    rows = [vec(f"L{l}_xattn_bv") for l in range(LAYERS)] + [vec(f"L{l}_xattn_bo") for l in range(LAYERS)]
    rows += [dh(vec("L3_xattn_bq")), dh(vec("L3_xattn_bk")), vec("L3_ffn_bias"), vec("L2_ffn_gate_b")]
    gate, up = (np.asarray(i[f"L1_ffn_{n}_w"]).reshape(D, 2, P) for n in ("gate", "up"))
    b1 = np.concatenate([i["L2_ffn_b1"], np.asarray(i["L2_ffn_bs1"])[None]])
    k, q = np.arange(P)[:, None], np.arange(P)[None, :]
    row = np.arange(ROWS).reshape(RT, P).T[:, :, None]
    return {
        "x": i["x"], "ctxT": np.asarray(i["ctx_1024"]).transpose(0, 2, 1),
        "attn_w": attn_w, "bias_cols": bias_cols, "bias_rows": np.concatenate(rows)[None],
        "g_all": np.concatenate([i["g_xattn"], i["g_ffn"]])[None],
        "router0": np.asarray(i["L0_ffn_w_router"])[:, None], "block0": i["L0_ffn_w_block"],
        "router1": i["L1_ffn_w_router"], "fc1": i["L1_ffn_fc1_w"], "fc2": i["L1_ffn_fc2_w"],
        "gate_up": np.stack([gate, up], axis=2), "down": i["L1_ffn_down_w"],
        "router2": i["L2_ffn_gate_w"], "w1": i["L2_ffn_w1"], "ws1": i["L2_ffn_ws1"],
        "b1_cols": b1.reshape(EXPERTS + 1, HC, P).transpose(2, 0, 1), "w2": i["L2_ffn_w2"],
        "ws2": i["L2_ffn_ws2"], "b2_all": np.concatenate([i["L2_ffn_b2"], np.asarray(i["L2_ffn_bs2"])[None]]),
        "w3": i["L3_ffn_weight"],
        "ident_in": np.eye(P, dtype=f), "causal_qk": np.where(q > k, f(-1e30), f(0)).astype(f),
        "causal_kq": np.where(k > q, f(-1e30), f(0)).astype(f),
        "before_in": (np.arange(ROWS)[None, None] < row).astype(f),
        "iota_in": np.broadcast_to(np.arange(EXPERTS, dtype=f), (P, EXPERTS)),
    }


def kernel(**inputs):
    import numpy as _np
    import concourse.bacc as _bacc
    from concourse import mybir as _mybir
    from concourse.bass_utils import run_bass_kernel_spmd as _run

    nc = _bacc.Bacc("TRN2", target_bir_lowering=False, num_devices=1)
    arrays, args = {}, {}
    for name, a in _arrays(inputs).items():
        a = _np.ascontiguousarray(a)
        arrays[f"in_{name}"] = a
        args[name] = nc.dram_tensor(f"in_{name}", a.shape, _mybir.dt.from_np(a.dtype), kind="ExternalInput").ap()
    out = nc.dram_tensor("out_x", (BATCHES, ROWS, D), F32, kind="ExternalOutput").ap()
    flamingo(nc, out=out, **args)
    r = _run(nc, [arrays], core_ids=[0])
    return r.results[0]["out_x"]
```
